# Optimizing a Trainium2 kernel written in Bass

```python
import numpy as np
import jax
import jax.numpy as jnp

def _softmax(x, axis=-1):
    return jax.nn.softmax(x, axis=axis)

def _gelu(x):
    return jax.nn.gelu(x, approximate=True)

def _silu(x):
    return jax.nn.silu(x)

def _sigmoid(x):
    return jax.nn.sigmoid(x)

def _layernorm(x, axis=-1, eps=1e-05):
    m = jnp.mean(x, axis=axis, keepdims=True)
    v = jnp.var(x, axis=axis, keepdims=True)
    return (x - m) / jnp.sqrt(v + eps)

def _scatter_add(tgt, idx, src, axis=0):
    return tgt.at[idx].add(src)

def _segment_sum(src, seg, n):
    return jax.ops.segment_sum(src, seg, n)
kernel_name = 'mk_gnn_resnorm_d2_gnn_r64_7ac0f7'

def setup_inputs(seed: int=0):
    np.random.seed(seed)
    _w = jnp.asarray

    def _rec_inputs():
        import jax
        import jax.numpy as jnp
        _gk = jax.random.key(seed)
        x = -0.000202 + 1 * jax.random.normal(jax.random.fold_in(_gk, 1), (100000, 64), jnp.float32)
        src = jax.random.randint(jax.random.fold_in(_gk, 2), (50000,), 0, 100000, jnp.int32)
        dst = jax.random.randint(jax.random.fold_in(_gk, 3), (50000,), 0, 100000, jnp.int32)
        _o = jnp.argsort(dst, stable=True)
        src = src[_o]
        dst = dst[_o]
        edge_attr_64 = -8.16379e-05 + 0.999858 * jax.random.normal(jax.random.fold_in(_gk, 13), (50000, 64), jnp.float32)
        edge_weight = jax.random.uniform(jax.random.fold_in(_gk, 15), (50000,), jnp.float32, 0.0, 0.999999)
        return (x, src, dst, edge_attr_64, edge_weight)
    x, src, dst, edge_attr_64, edge_weight = _rec_inputs()

    def _L0_gnn_setup():
        import jax, jax.numpy as jnp
        import numpy as np
        N_NODES = 100000
        N_EDGES = 25000
        H, D = (4, 16)
        DE = 16
        DIN_N = 64
        DIN_E = 64
        key = jax.random.key(seed)
        ks = jax.random.split(key, 9)
        return {'inputs_node': jax.random.normal(ks[0], (N_NODES, DIN_N), dtype=jnp.float32), 'inputs_edge': jax.random.normal(ks[1], (N_EDGES, DIN_E), dtype=jnp.float32), 'src': jax.random.randint(ks[2], (N_EDGES,), 0, N_NODES, dtype=jnp.int32), 'dst': jax.random.randint(ks[3], (N_EDGES,), 0, N_NODES, dtype=jnp.int32), 'W_node': jax.random.normal(ks[4], (DIN_N, H * D), dtype=jnp.float32) * (1.0 / np.sqrt(DIN_N)), 'W_edge': jax.random.normal(ks[5], (DIN_E, H * DE), dtype=jnp.float32) * (1.0 / np.sqrt(DIN_E)), 'attn_query': jax.random.normal(ks[6], (H, D), dtype=jnp.float32) * (1.0 / np.sqrt(D)), 'attn_key': jax.random.normal(ks[7], (H, D), dtype=jnp.float32) * (1.0 / np.sqrt(D)), 'attn_edge': jax.random.normal(ks[8], (H, DE), dtype=jnp.float32) * (1.0 / np.sqrt(DE)), 'bias': jnp.zeros((H * D,), dtype=jnp.float32)}
    _L0_gnn_all = _L0_gnn_setup()
    _L0_gnn_in = {k: v for k, v in _L0_gnn_all.items() if k in ('W_node', 'W_edge', 'attn_query', 'attn_key', 'attn_edge', 'bias')}
    del _L0_gnn_all

    def _L1_gnn_setup():
        import jax, jax.numpy as jnp
        import numpy as np
        N_NODES = 100000
        N_EDGES = 25000
        D_IN = 64
        D_HID = 64

        def _add_self_loops(row, col, ew, n):
            loop = jnp.arange(n, dtype=row.dtype)
            row = jnp.concatenate([row, loop])
            col = jnp.concatenate([col, loop])
            ew = jnp.concatenate([ew, jnp.ones((n,), dtype=ew.dtype)])
            return (row, col, ew)

        def _gcn_conv(x, W, b, row, col, ew, n):
            xw = x @ W
            deg = jax.ops.segment_sum(ew, col, num_segments=n)
            dis = jnp.where(deg > 0, jax.lax.rsqrt(deg), 0.0)
            norm = dis[row] * ew * dis[col]
            msg = xw[row] * norm[:, None]
            out = jax.ops.segment_sum(msg, col, num_segments=n)
            return out + b
        key = jax.random.key(seed)
        ks = jax.random.split(key, 8)
        x = jax.random.normal(ks[0], (N_NODES, D_IN), dtype=jnp.float32)
        edge_index = jax.random.randint(ks[1], (2, N_EDGES), 0, N_NODES, dtype=jnp.int64)
        edge_weight = jax.random.uniform(ks[2], (N_EDGES,), dtype=jnp.float32)
        batch = jnp.zeros((N_NODES,), dtype=jnp.int64)
        s_in = 1.0 / np.sqrt(D_IN)
        s_h = 1.0 / np.sqrt(D_HID)
        W0 = jax.random.normal(ks[3], (D_IN, D_HID), dtype=jnp.float32) * s_in
        b0 = jnp.zeros((D_HID,), dtype=jnp.float32)
        W1 = jax.random.normal(ks[4], (D_HID, D_HID), dtype=jnp.float32) * s_h
        b1 = jnp.zeros((D_HID,), dtype=jnp.float32)
        W2 = jax.random.normal(ks[5], (D_HID, D_HID), dtype=jnp.float32) * s_h
        b2 = jnp.zeros((D_HID,), dtype=jnp.float32)
        return {'x': x, 'edge_index': edge_index, 'edge_weight': edge_weight, 'batch': batch, 'W0': W0, 'b0': b0, 'W1': W1, 'b1': b1, 'W2': W2, 'b2': b2}
    _L1_gnn_all = _L1_gnn_setup()
    _L1_gnn_in = {k: v for k, v in _L1_gnn_all.items() if k in ('W0', 'b0', 'W1', 'b1', 'W2', 'b2')}
    del _L1_gnn_all
    return {'x': x, 'src': src, 'dst': dst, 'edge_attr_64': edge_attr_64, 'edge_weight': edge_weight, 'L0_gnn_W_node': _L0_gnn_in['W_node'], 'L0_gnn_W_edge': _L0_gnn_in['W_edge'], 'L0_gnn_attn_query': _L0_gnn_in['attn_query'], 'L0_gnn_attn_key': _L0_gnn_in['attn_key'], 'L0_gnn_attn_edge': _L0_gnn_in['attn_edge'], 'L0_gnn_bias': _L0_gnn_in['bias'], 'L1_gnn_W0': _L1_gnn_in['W0'], 'L1_gnn_b0': _L1_gnn_in['b0'], 'L1_gnn_W1': _L1_gnn_in['W1'], 'L1_gnn_b1': _L1_gnn_in['b1'], 'L1_gnn_W2': _L1_gnn_in['W2'], 'L1_gnn_b2': _L1_gnn_in['b2']}

def reference(x, src, dst, edge_attr_64, edge_weight, L0_gnn_W_node, L0_gnn_W_edge, L0_gnn_attn_query, L0_gnn_attn_key, L0_gnn_attn_edge, L0_gnn_bias, L1_gnn_W0, L1_gnn_b0, L1_gnn_W1, L1_gnn_b1, L1_gnn_W2, L1_gnn_b2):
    import jax
    import jax.numpy as jnp

    def _L0_gnn_ref(inputs_node, inputs_edge, src, dst, W_node, W_edge, attn_query, attn_key, attn_edge, bias):
        import jax, jax.numpy as jnp
        import numpy as np
        N_NODES = 100000
        N_EDGES = 25000
        H, D = (4, 16)
        DE = 16
        DIN_N = 64
        DIN_E = 64
        n = inputs_node.shape[0]
        hn = (inputs_node @ W_node).reshape(n, H, D)
        he = (inputs_edge @ W_edge).reshape(-1, H, DE)
        w_q = jnp.einsum('nhd,hd->nh', hn, attn_query)
        w_k = jnp.einsum('nhd,hd->nh', hn, attn_key)
        w_e = jnp.einsum('ehd,hd->eh', he, attn_edge)
        logits = jax.nn.leaky_relu(w_k[src] + w_q[dst] + w_e, negative_slope=0.01)
        seg_max = jax.ops.segment_max(logits, dst, num_segments=n)
        seg_max = jnp.where(jnp.isfinite(seg_max), seg_max, 0.0)
        ex = jnp.exp(logits - seg_max[dst])
        denom = jax.ops.segment_sum(ex, dst, num_segments=n)
        attn = ex / denom[dst]
        msg = hn[src] * attn[:, :, None]
        out = jax.ops.segment_sum(msg, dst, num_segments=n)
        out = out.reshape(n, H * D) + bias
        out = out + inputs_node
        return out

    def _L1_gnn_ref(x, edge_index, edge_weight, batch, W0, b0, W1, b1, W2, b2):
        import jax, jax.numpy as jnp
        import numpy as np
        N_NODES = 100000
        N_EDGES = 25000
        D_IN = 64
        D_HID = 64

        def _add_self_loops(row, col, ew, n):
            loop = jnp.arange(n, dtype=row.dtype)
            row = jnp.concatenate([row, loop])
            col = jnp.concatenate([col, loop])
            ew = jnp.concatenate([ew, jnp.ones((n,), dtype=ew.dtype)])
            return (row, col, ew)

        def _gcn_conv(x, W, b, row, col, ew, n):
            xw = x @ W
            deg = jax.ops.segment_sum(ew, col, num_segments=n)
            dis = jnp.where(deg > 0, jax.lax.rsqrt(deg), 0.0)
            norm = dis[row] * ew * dis[col]
            msg = xw[row] * norm[:, None]
            out = jax.ops.segment_sum(msg, col, num_segments=n)
            return out + b
        n = x.shape[0]
        row, col, ew = _add_self_loops(edge_index[0], edge_index[1], edge_weight, n)
        h = x.astype(jnp.float32)
        h = _gcn_conv(h, W0, b0, row, col, ew, n)
        for W, b in ((W1, b1), (W2, b2)):
            h = jax.nn.relu(h)
            h = _gcn_conv(h, W, b, row, col, ew, n)
        return jax.nn.relu(h)
    edge_index = jnp.stack([src, dst])
    batch0 = jnp.zeros((100000,), jnp.int32)
    x = _layernorm(x + _L0_gnn_ref(x, edge_attr_64, src, dst, L0_gnn_W_node, L0_gnn_W_edge, L0_gnn_attn_query, L0_gnn_attn_key, L0_gnn_attn_edge, L0_gnn_bias), axis=-1)
    x = _layernorm(x + _L1_gnn_ref(x, edge_index, edge_weight, batch0, L1_gnn_W0, L1_gnn_b0, L1_gnn_W1, L1_gnn_b1, L1_gnn_W2, L1_gnn_b2), axis=-1)
    return x

_drawn_inputs = setup_inputs


def setup_inputs(seed=0):
    import zlib

    import numpy as np

    out = dict(_drawn_inputs(seed))
    spreads = {'L0_gnn_bias': (0.0, 0.1),
     'L1_gnn_b0': (0.0, 0.273),
     'L1_gnn_b1': (0.0, 0.1),
     'L1_gnn_b2': (0.0, 0.1)}
    factors = {'L0_gnn_attn_query': 3.032}
    for name, (base, spread) in spreads.items():
        noise = np.random.default_rng([zlib.crc32(name.encode()), seed]).standard_normal(out[name].shape)
        drawn = base * np.exp(spread * noise) if base else spread * noise
        out[name] = jnp.asarray(drawn.astype(out[name].dtype))
    for name, factor in factors.items():
        out[name] = (out[name] * factor).astype(out[name].dtype)
    return out
```

```python
from contextlib import ExitStack

import concourse.bass as bass
from concourse import mybir

F32 = mybir.dt.float32
I32 = mybir.dt.int32
ALU = mybir.AluOpType
ACT = mybir.ActivationFunctionType
AX = mybir.AxisListType

P = 128
N, E, D, H = 100000, 50000, 64, 4
HD = D // H
T = 392
PA, TA = 112, 392
PB, TB = 16, 381
assert PA * TA + PB * TB == E and PA + PB == P
C = 14
CH = T // C
R4 = 4
NB4 = CH // R4
SW = D + H
SLOT0 = N
ROWS = N + P * T
XW = 68
GW = D + 2 * H
C1 = C + 1
W = C * D
BR = 8
BN = P * BR
FULL = N // BN
TP, TR = 112, 6
assert FULL * BN + TP * TR == N and FULL == 97
BIG = 1.0e30
SKIP = 200000.0
EPS = 1e-5


ILOADS = 6 + T - TB
WLOADS = 31


class Steps:

    def __init__(self, sem):
        self.sem, self.base, self.n, self.turns = sem, 0, 0, 0

    def enter(self, j, each):
        self.base, self.n, self.turns, self.each = self.base + self.n, 0, j, each

    def leave(self, count):
        assert self.n == self.each, (self.n, self.each)
        self.base, self.n, self.turns = self.base + self.each * count, 0, 0

    def on(self, engine, instruction):
        instruction.then_inc(self.sem, 1)
        self.n += 1
        at = self.base + self.n
        if not isinstance(self.turns, int):
            at = self.turns * self.each + at
        engine.wait_ge(self.sem, at)


def turns(engine, count, body, step=None, each=0):
    body(0)
    with engine.Fori(1, count) as j:
        if step:
            step.enter(j - 1, each)
        body(j)
        if step:
            step.leave(count - 1)


def build(nc, x, src, dst, edge_attr, edge_weight, W_node, W_edge, a_query, a_key, a_edge, bias,
          W0, b0, W1, b1, W2, b2, out):
    with ExitStack() as ctx:
        def sb(name, shape, dt=F32):
            return ctx.enter_context(nc.sbuf_tensor(name, shape, dt))

        def sem(name):
            return ctx.enter_context(nc.semaphore(name))

        def dram(name, shape):
            return nc.dram_tensor(name, shape, F32, kind="Internal").ap()

        xs_dram = dram("xs_dram", [N, XW])
        xd_dram = dram("xd_dram", [P * T, D])
        gat_dram = dram("gat_dram", [P * T, GW])
        x1_dram = dram("x1_dram", [P * T, D])
        pre_dram = [dram(f"pre{l}_dram", [P * T, D]) for l in range(3)]
        tab_dram = [dram(f"tab{l}_dram", [ROWS, D]) for l in range(3)]

        def slots(ap, k):
            return ap.rearrange("(p t) f -> p t f", t=T)[:, bass.ds(k * C, C), :]

        def tab_slots(l, k):
            return slots(tab_dram[l][SLOT0:ROWS, :], k)

        ident = sb("ident", [P, P])
        src_i, dst_i = sb("src_i", [P, T], I32), sb("dst_i", [P, T], I32)
        ew = sb("ew", [P, T])
        srcf, dstf = sb("srcf", [P, T]), sb("dstf", [P, T])
        prev_i, next_i = sb("prev_i", [P, 1], I32), sb("next_i", [P, 1], I32)
        same, breakf, isend, first = (sb(n, [P, T]) for n in ("same", "breakf", "isend", "first"))
        slot_i, slotf = sb("slot_i", [P, T], I32), sb("slotf", [P, T])
        shiftf, tmpT, onehot = sb("shiftf", [P, T]), sb("tmpT", [P, T]), sb("onehot", [P, T])
        map_i, out_i, row_i = (sb(n, [P, T], I32) for n in ("map_i", "out_i", "row_i"))
        deg, dis, padneg = sb("deg", [P, T]), sb("dis", [P, T]), sb("padneg", [P, T])
        negs = sb("negs", [PB, T - TB])
        col = sb("col", [P, 16])
        (c_prev, c_next, c_cont, c_whole, c_t1, c_slot, c_dis, c_end, c_run, c_tmp) = (
            col[:, i:i + 1] for i in range(10))
        seam_i = sb("seam_i", [P, 4], I32)
        i_slot, i_row, i_out = (seam_i[:, i:i + 1] for i in range(3))
        eps_c = sb("eps_c", [P, 1])
        ones_r, b2_r = sb("ones_r", [1, P]), sb("b2_r", [1, 4, 2, D])
        WN, W0b, W1b, W2b = (sb(n, [P, P]) for n in ("WN", "W0b", "W1b", "W2b"))
        Wn2, We2 = sb("Wn2", [P, D]), sb("We2", [P, D])
        wprod, wred = sb("wprod", [P, 3, D]), sb("wred", [P, 3, H])
        att_bc = sb("att_bc", [P, 3, D])
        WA = sb("WA", [P, 3, 2 * H])
        bias_bc = sb("bias_bc", [P, D])
        b_bc = [sb(f"b{l}_bc", [P, D]) for l in range(3)]
        b0c, b1c = sb("b0c", [P, 1]), sb("b1c", [P, 1])

        dX, dX1, dR1, dR2, dO = (sb(n, [P, 2, BR, D]) for n in ("dX", "dX1", "dR1", "dR2", "dO"))
        dC = sb("dC", [P, BR, D])
        dQ2 = sb("dQ2", [P, BR, D])
        dh0, dh1, dh2 = (sb(n, [P, 4, P]) for n in ("dh0", "dh1", "dh2"))
        dst8 = sb("dst8", [P, 8, BR])
        XM = sb("XM", [P, 4, BR, XW])

        ix, ix2, sv = sb("ix", [P, R4, C], I32), sb("ix2", [P, R4, C], I32), sb("sv", [P, R4, C])
        G = sb("G", [P, R4, C, XW])
        GX = sb("GX", [P, R4, C, D])
        XD, EA = sb("XD", [P, 2, C, D]), sb("EA", [P, 2, C, D])
        TS = [sb(f"TS{i}", [P, 7, P]) for i in range(3)]
        Z, LB, AM = sb("Z", [P, C, H]), sb("LB", [P, H, C1]), sb("AM", [P, H, C1])
        M = sb("M", [P, 2, H, C1])
        DE, RX = sb("DE", [P, 2 * H, C]), sb("RX", [P, 2 * H, C])
        AB, B = sb("AB", [P, SW, C1]), sb("B", [P, SW, C1])
        AS = sb("AS", [P, 2, D, C1])
        SS = sb("SS", [P, 2, SW, C1])
        RD = sb("RD", [P, H, C])
        NR = sb("NR", [P, 2, C, GW])
        U, Q = sb("U", [P, C, D]), sb("Q", [P, C, D])
        dU, dQ1 = U[:, 0:BR, :], Q[:, 0:BR, :]
        X1, Y0 = sb("X1", [P, 2, C, D]), sb("Y0", [P, 2, C, D])
        PR = sb("PR", [P, 2, C, D])
        XC = PR
        OB = G[:, :, :, 0:D]
        est = sb("est", [P, 4, C])

        bc = sb("bc", [P, 4, SW])
        run_r, cont_r, nrun_r, ncont_r = (sb(n, [SW, P]) for n in ("run_r", "cont_r", "nrun_r", "ncont_r"))
        LS, LM = sb("LS", [P, SW]), sb("LM", [P, SW])
        mE, mC, rE, bE, sE, sC = (sb(n, [SW, P]) for n in ("mE", "mC", "rE", "bE", "sE", "sC"))
        cS, cM = sb("cS", [P, SW]), sb("cM", [P, SW])
        grow, xrow, prow = sb("grow", [P, GW]), sb("xrow", [P, D]), sb("prow", [P, D])
        S68, M68, MM, wS, wC = (sb(n, [P, SW]) for n in ("S68", "M68", "MM", "wS", "wC"))
        sden = sb("sden", [P, H])
        su, sq, x1row, yrow = (sb(n, [P, D]) for n in ("su", "sq", "x1row", "yrow"))
        prT = sb("prT", [D, P])
        sst = sb("sst", [P, 4])

        ps = ctx.enter_context(nc.psum_tensor("ps", [P, 8, 512], F32))
        pT, pM1, pM2, pR1, pR2, pO = (ps[:, i, :] for i in range(6))
        flat = ps[:, :, :].rearrange("p a b -> p (a b)")
        TRP = [flat[:, 0:W], flat[:, 1024:1024 + W]]
        HS = flat[:, 2048:2048 + W].rearrange("p (t f) -> p t f", f=D)
        LG = ps[:, 6, 0:C * H].rearrange("p (t h) -> p t h", h=H)
        SM = ps[:, 7, :]

        names = """consts_set zeroed loaded_idx loaded_w filled ends_loaded seam_set flags_ready weights_ready
            vector_step rows_in rows_T chain_in chain_T chain_back_in chain_back deg_in deg_sqrt
            d_xfree d_c1 d_sq1 d_v1 d_sd1 d_x1 d_trx d_h0 d_m1 d_h1 d_m2 d_r1 d_h2 d_r2 d_o
            d_R1 d_R2 d_u2 d_c2 d_sq2 d_v2 d_sd2 d_O
            idx_staged turn
            g_shift g_xc g_trx g_trd g_tre g_evx g_evd g_eve g_hs g_lg g_z g_de g_ex g_ab g_hsfree g_S
            g_xdfree g_nr g_nrm g_c g_q g_v g_sd g_x1 g_y0
            l_gfree l_as l_scan l_pre l_tr l_ev l_z l_zfree l_u l_y l_c l_q l_v l_sd l_o
            s_row s_ex_in s_ex s_mid s_midT s_prT s_mm s_c s_q s_v s_sd s_out s_stored""".split()
        S = {n: sem(n) for n in names}
        d_xl = [sem(f"dense_x_loaded{b}") for b in range(2)]
        d_st = [[sem(f"dense_stored{j}_{b}") for b in range(2)] for j in range(4)]
        xm_ld = [sem(f"xs_loaded{b}") for b in range(4)]
        xm_st = [sem(f"xs_stored{b}") for b in range(4)]
        xg_ld = [sem(f"xdst_gathered{b}") for b in range(R4)]
        xg_st = [sem(f"xdst_stored{b}") for b in range(R4)]
        mp_st = [sem(f"shift_scattered{b}") for b in range(R4)]
        g_ld = [sem(f"gat_gathered{b}") for b in range(R4)]
        g_in = [sem(f"gat_inputs{b}") for b in range(2)]
        g_out = [[sem(f"gat_stored{j}_{b}") for b in range(2)] for j in range(3)]
        l_ld = [sem(f"gcn_gathered{b}") for b in range(R4)]
        l_in = [sem(f"gcn_inputs{b}") for b in range(2)]
        l_out = [[sem(f"gcn_stored{j}_{b}") for b in range(2)] for j in range(2)]
        o_st = [sem(f"rows_scattered{b}") for b in range(R4)]

        HALF = 16 * CH // 2
        BLOCKS = FULL + 1

        block = ctx.enter_context(nc.Block())

        @block.sync
        def _(sp):
            def need(sem_, value):
                sp.wait_ge(sem_, value)
                sp.sem_inc(S["turn"], 1)

            sp.wait_ge(S["zeroed"], 1)
            for tile, arr in ((src_i, src), (dst_i, dst), (ew, edge_weight)):
                sp.dma_start(tile[0:PA, :], arr[0:PA * TA].rearrange("(p t) -> p t", t=TA)).then_inc(S["loaded_idx"], 16)
                sp.dma_start(tile[PA:P, 0:TB], arr[PA * TA:E].rearrange("(p t) -> p t", t=TB)).then_inc(S["loaded_idx"], 16)
            with nc.allow_non_contiguous_dma(reason="one word per slot, 11 slots"):
                last = dst[PA * TA:E].rearrange("(p t) -> p t", t=TB)[:, TB - 1:TB]
                for t in range(TB, T):
                    sp.dma_start(dst_i[PA:P, t:t + 1], last).then_inc(S["loaded_idx"], 16)
            sp.dma_start(padneg[PA:P, TB:T], negs[:, :]).then_inc(S["filled"], 16)
            sp.wait_ge(S["loaded_idx"], ILOADS * 16)
            sp.dma_start(prev_i[1:P, :], dst_i[0:P - 1, T - 1:T]).then_inc(S["ends_loaded"], 16)
            sp.dma_start(next_i[0:P - 1, :], dst_i[1:P, 0:1]).then_inc(S["ends_loaded"], 16)
            n = 0
            for tile, w in ((WN, W_node), (W0b, W0), (W1b, W1), (W2b, W2)):
                for h in range(2):
                    sp.dma_start(tile[64 * h:64 * h + 64, 64 * h:64 * h + 64], w).then_inc(S["loaded_w"], 16)
                    n += 1
            for tile, w in ((Wn2, W_node), (We2, W_edge)):
                for h in range(2):
                    sp.dma_start(tile[64 * h:64 * h + 64, :], w).then_inc(S["loaded_w"], 16)
                    n += 1
            for j, a in enumerate((a_key, a_query, a_edge)):
                row = a.rearrange("h d -> (h d)").rearrange("(o n) -> o n", o=1)
                sp.dma_start(att_bc[:, j, :], row.to_broadcast([P, D])).then_inc(S["loaded_w"], 16)
                n += 1
            for tile, v in ((bias_bc, bias), (b_bc[0], b0), (b_bc[1], b1), (b_bc[2], b2)):
                sp.dma_start(tile[:, :], v.rearrange("(o n) -> o n", o=1).to_broadcast([P, D])).then_inc(S["loaded_w"], 16)
                n += 1
            with nc.allow_non_contiguous_dma(reason="128 words"):
                for tile, v in ((b0c, b0), (b1c, b1)):
                    for h in range(2):
                        sp.dma_start(tile[64 * h:64 * h + 64, :], v.rearrange("(n o) -> n o", o=1)).then_inc(S["loaded_w"], 16)
                        n += 1
            for j in range(8):
                sp.dma_start(b2_r[0:1, j // 2, j % 2, :], b2.rearrange("(o n) -> o n", o=1)).then_inc(S["loaded_w"], 16)
                n += 1
            assert n == WLOADS

            def rows(ap, i, np_, r):
                return ap[bass.ds(i * BN, np_ * r), :].rearrange("(p t) f -> p t f", t=r)

            def load_x(i, b, np_=P, r=BR, free=None):
                if free is not None:
                    need(S["d_xfree"], free)
                sp.dma_start(dX[0:np_, b, 0:r, :], rows(x, i, np_, r)).then_inc(d_xl[b], 16)

            def store_block(i, b, np_=P, r=BR):
                for j, (ready, buf) in enumerate((("d_x1", dX1), ("d_R1", dR1), ("d_R2", dR2), ("d_O", dO))):
                    need(S[ready], i + 1)
                    table = out if j == 3 else tab_dram[j]
                    sp.dma_start(rows(table, i, np_, r), buf[0:np_, b, 0:r, :]).then_inc(d_st[j][b], 16)

            def xs_load(i, b, np_=P, r=BR, before=None):
                if before is not None:
                    need(xm_st[b], before)
                sp.dma_start(XM[0:np_, b, 0:r, 0:D], rows(x, i, np_, r)).then_inc(xm_ld[b], 16)

            def xs_store(i, b, n, np_=P, r=BR):
                need(xm_ld[b], n)
                sp.dma_start(rows(xs_dram, i, np_, r), XM[0:np_, b, 0:r, :]).then_inc(xm_st[b], 16)

            load_x(0, 0)
            load_x(1, 1)
            def with_xs(j):
                for b in range(4):
                    xs_load(j * 4 + b, b, before=j * 16)
                for b in range(2):
                    load_x(j * 2 + b + 2, b, free=j * 2 + b + 1)
                    for b_ in range(2):
                        xs_store(j * 4 + 2 * b + b_, 2 * b + b_, j * 16 + 16)
                    store_block(j * 2 + b, b)

            turns(sp, 24, with_xs)
            xs_load(96, 0, before=24 * 16)
            xs_load(97, 1, TP, TR, before=24 * 16)
            xs_store(96, 0, 25 * 16)
            xs_store(97, 1, 25 * 16, TP, TR)
            with sp.Fori(24, 47) as j:
                for b in range(2):
                    load_x(j * 2 + b + 2, b, free=j * 2 + b + 1)
                    store_block(j * 2 + b, b)
            load_x(96, 0, free=95)
            store_block(94, 0)
            load_x(97, 1, TP, TR, free=96)
            store_block(95, 1)
            store_block(96, 0)
            store_block(97, 1, TP, TR)

            for b in range(R4):
                need(xg_st[b], NB4 * 16)

            ea_a = edge_attr[0:PA * TA, :].rearrange("(p t) f -> p t f", t=TA)
            ea_b = edge_attr[PA * TA:E, :].rearrange("(p t) f -> p t f", t=TB)

            def gat_load(k, b, cb=C, free=None):
                if free is not None:
                    need(S["g_xdfree"], free)
                    need(S["g_tre"], free)
                sp.dma_start(XD[:, b], slots(xd_dram, k)).then_inc(g_in[b], 16)
                sp.dma_start(EA[0:PA, b], ea_a[:, bass.ds(k * C, C), :]).then_inc(g_in[b], 16)
                sp.dma_start(EA[PA:P, b, 0:cb], ea_b[:, bass.ds(k * C, cb), :]).then_inc(g_in[b], 16)

            def gat_store(k, b):
                need(S["g_nrm"], k + 1)
                need(S["g_nr"], 2 * (k + 1))
                sp.dma_start(slots(gat_dram, k), NR[:, b]).then_inc(g_out[0][b], 16)
                need(S["g_x1"], k + 1)
                sp.dma_start(slots(x1_dram, k), X1[:, b]).then_inc(g_out[1][b], 16)
                need(S["g_y0"], k + 1)
                sp.dma_start(tab_slots(0, k), Y0[:, b]).then_inc(g_out[2][b], 16)

            gat_load(0, 0)
            gat_load(1, 1)
            with sp.Fori(0, NB4 - 1) as j:
                for b in range(R4):
                    k = j * R4 + b
                    gat_load(k + 2, b % 2, free=k + 1)
                    gat_store(k, b % 2)
            gat_load(CH - 2, 0, free=CH - 3)
            gat_store(CH - 4, 0)
            gat_load(CH - 1, 1, cb=TB - (CH - 1) * C, free=CH - 2)
            for k in range(CH - 3, CH):
                gat_store(k, k % 2)

            for l in range(3):
                need(S["s_stored"], 32 + 16 * l)

                def load(k, b, free=None):
                    if free is not None:
                        need(S["l_pre"], CH * l + free)
                        if l == 2:
                            need(S["l_u"], free)
                    sp.dma_start(XD[:, b], tab_slots(l, k)).then_inc(l_in[b], 16)
                    if l == 2:
                        sp.dma_start(EA[:, b], slots(x1_dram, k)).then_inc(l_in[b], 16)

                def store(k, b):
                    need(S["l_pre"], CH * l + k + 1)
                    sp.dma_start(slots(pre_dram[l], k), PR[:, b]).then_inc(l_out[0][b], 16)
                    if l < 2:
                        need(S["l_y"], CH * l + k + 1)
                        sp.dma_start(tab_slots(l + 1, k), Y0[:, b]).then_inc(l_out[1][b], 16)

                load(0, 0)
                load(1, 1)
                with sp.Fori(0, NB4 - 1) as j:
                    for b in range(R4):
                        load(j * R4 + b + 2, b % 2, free=j * R4 + b + 1)
                        store(j * R4 + b, b % 2)
                for k in range(CH - 4, CH):
                    if k + 2 < CH:
                        load(k + 2, k % 2, free=k + 1)
                    store(k, k % 2)

            for b in range(2):
                need(d_st[3][b], BLOCKS // 2 * 16)

        @block.gpsimd
        def _(pool):
            pool.wait_ge(S["zeroed"], 1)
            chain = Steps(S["consts_set"])
            chain.on(pool, nc.gpsimd.affine_select(out=ident[:, :], in_=ident[:, :], compare_op=ALU.not_equal, fill=1.0,
                                                   base=0, pattern=[[-1, P]], channel_multiplier=1))
            chain.on(pool, nc.gpsimd.iota(slot_i[:, :], pattern=[[1, T]], base=0, channel_multiplier=T))
            pool.wait_ge(S["loaded_idx"], ILOADS * 16)

            staged = [0]

            def take_turn():
                nc.gpsimd.sem_inc(S["turn"], 1)

            def stage(k, b, source, n, values=None):
                nc.gpsimd.tensor_copy(ix[:, b, :], source[:, bass.ds(k * C, C)]).then_inc(S["idx_staged"], 1)
                if values is not None:
                    nc.gpsimd.tensor_copy(sv[:, b, :], values[:, bass.ds(k * C, C)]).then_inc(S["idx_staged"], 1)
                pool.wait_ge(S["idx_staged"], n)
                take_turn()

            def gather(table, buf, b, landed):
                for t in range(C):
                    nc.gpsimd.indirect_dma_start(out=buf[:, b, t, :], out_offset=None, in_=table,
                                                 in_offset=bass.IndirectOffsetOnAxis(ap=ix[:, b, t:t + 1], axis=0)).then_inc(landed, 16)

            def xd_gather(k, b, before=None):
                if before is not None:
                    pool.wait_ge(xg_st[b], before)
                    take_turn()
                stage(k, b, dst_i, k + 1)
                gather(x, GX, b, xg_ld[b])

            def xd_store(k, b, n):
                pool.wait_ge(xg_ld[b], n * 16 * C)
                take_turn()
                nc.gpsimd.dma_start(slots(xd_dram, k), GX[:, b]).then_inc(xg_st[b], 16)

            xd_gather(0, 0)
            def xd_four(j):
                for b in range(R4):
                    nxt = (b + 1) % R4
                    xd_gather(j * R4 + b + 1, nxt, before=(j + (1 if b == R4 - 1 else 0)) * 16)
                    xd_store(j * R4 + b, b, j + 1)

            turns(pool, NB4 - 1, xd_four)
            for k in range(CH - 4, CH):
                if k + 1 < CH:
                    xd_gather(k + 1, (k + 1) % R4, before=((k + 1) // R4) * 16)
                xd_store(k, k % R4, k // R4 + 1)

            pool.wait_ge(S["flags_ready"], 1)
            for b in range(4):
                pool.wait_ge(xm_st[b], (25 if b < 2 else 24) * 16)
            base = CH

            def shift_four(j):
                for b in range(R4):
                    pool.wait_ge(mp_st[b], j * 16 * C)
                    take_turn()
                    stage(j * R4 + b, b, map_i, base + (j * R4 + b + 1) * 2, values=shiftf)
                    for t in range(C):
                        nc.gpsimd.indirect_dma_start(out=xs_dram, out_offset=bass.IndirectOffsetOnAxis(ap=ix[:, b, t:t + 1], axis=0),
                                                     in_=sv[:, b, t:t + 1], in_offset=None, element_offset=D,
                                                     bounds_check=N - 1, oob_is_err=False).then_inc(mp_st[b], 16)

            turns(pool, NB4, shift_four)
            base += 2 * CH
            for b in range(R4):
                pool.wait_ge(mp_st[b], NB4 * 16 * C)

            for k in range(R4):
                stage(k, k, src_i, base + k + 1)
                gather(xs_dram, G, k, g_ld[k])
            with pool.Fori(1, NB4) as j:
                for b in range(R4):
                    k = j * R4 + b
                    pool.wait_ge(S["g_xc"], k - R4 + 1)
                    pool.wait_ge(S["g_shift"], k - R4 + 1)
                    take_turn()
                    stage(k, b, src_i, base + k + 1)
                    gather(xs_dram, G, b, g_ld[b])
            base += CH

            for b in range(2):
                pool.wait_ge(g_out[0][b], HALF)
            pool.wait_ge(S["seam_set"], 1)
            for table, row in ((gat_dram, grow), (xd_dram, xrow)):
                nc.gpsimd.indirect_dma_start(out=row[:, :], out_offset=None, in_=table,
                                             in_offset=bass.IndirectOffsetOnAxis(ap=i_slot, axis=0)).then_inc(S["s_row"], 16)
            for b in range(2):
                pool.wait_ge(g_out[1][b], HALF)
                pool.wait_ge(g_out[2][b], HALF)
            pool.wait_ge(S["s_out"], 1)
            for table, row, idx in ((x1_dram, x1row, i_slot), (tab_dram[0], yrow, i_row)):
                nc.gpsimd.indirect_dma_start(out=table, out_offset=bass.IndirectOffsetOnAxis(ap=idx, axis=0),
                                             in_=row[:, :], in_offset=None).then_inc(S["s_stored"], 16)
            pool.wait_ge(S["s_stored"], 32)

            def scatter_out(b):
                for t in range(C):
                    nc.gpsimd.indirect_dma_start(out=out, out_offset=bass.IndirectOffsetOnAxis(ap=ix2[:, b, t:t + 1], axis=0),
                                                 in_=OB[:, b, t, :], in_offset=None,
                                                 bounds_check=N - 1, oob_is_err=False).then_inc(o_st[b], 16)

            for l in range(3):
                for b in range(2):
                    pool.wait_ge(d_st[l][b], BLOCKS // 2 * 16)
                if l == 2:
                    for b in range(2):
                        pool.wait_ge(d_st[3][b], BLOCKS // 2 * 16)

                def turn(k, b, j, n):
                    if j is not None:
                        pool.wait_ge(S["l_gfree"], CH * l + k - R4 + 1)
                        take_turn()
                    stage(k, b, row_i, n)
                    gather(tab_dram[l], GX, b, l_ld[b])

                if l < 2:
                    for k in range(R4):
                        turn(k, k, None, base + k + 1)
                    with pool.Fori(1, NB4) as j:
                        for b in range(R4):
                            turn(j * R4 + b, b, j, base + j * R4 + b + 1)
                    base += CH
                else:
                    for k in range(R4):
                        turn(k, k, None, base + k + 1)
                    base += R4

                    def scatter_chunk(k, b, n, before):
                        pool.wait_ge(o_st[b], before)
                        take_turn()
                        nc.gpsimd.tensor_copy(ix2[:, b, :], out_i[:, bass.ds(k * C, C)]).then_inc(S["idx_staged"], 1)
                        pool.wait_ge(S["idx_staged"], n)
                        pool.wait_ge(S["l_o"], k + 1)
                        take_turn()
                        scatter_out(b)

                    def gather_scatter(j):
                        for b in range(R4):
                            k = j * R4 + b
                            turn(k + R4, b, j, base + k * 2 + 1)
                            scatter_chunk(k, b, base + k * 2 + 2, j * 16 * C)

                    turns(pool, NB4 - 1, gather_scatter)
                    base += 2 * (CH - R4)
                    for k in range(CH - R4, CH):
                        scatter_chunk(k, k % R4, base + k - (CH - R4) + 1, (NB4 - 1) * 16 * C)

                for b in range(2):
                    pool.wait_ge(l_out[0][b], (l + 1) * HALF)
                nc.gpsimd.indirect_dma_start(out=prow[:, :], out_offset=None, in_=pre_dram[l],
                                             in_offset=bass.IndirectOffsetOnAxis(ap=i_slot, axis=0)).then_inc(S["s_row"], 16)
                if l < 2:
                    for b in range(2):
                        pool.wait_ge(l_out[1][b], (l + 1) * HALF)
                pool.wait_ge(S["s_out"], l + 2)
                if l < 2:
                    nc.gpsimd.indirect_dma_start(out=tab_dram[l + 1], out_offset=bass.IndirectOffsetOnAxis(ap=i_row, axis=0),
                                                 in_=yrow[:, :], in_offset=None).then_inc(S["s_stored"], 16)
                    pool.wait_ge(S["s_stored"], 48 + 16 * l)
                else:
                    nc.gpsimd.indirect_dma_start(out=out, out_offset=bass.IndirectOffsetOnAxis(ap=i_out, axis=0),
                                                 in_=yrow[:, :], in_offset=None,
                                                 bounds_check=N - 1, oob_is_err=False).then_inc(S["s_stored"], 16)
                    pool.wait_ge(S["s_stored"], 48 + 16 * l)
            for b in range(R4):
                pool.wait_ge(o_st[b], NB4 * 16 * C)

        def repeat(scalar_per_row, n):
            shape = list(scalar_per_row.shape) + [n]
            return scalar_per_row.unsqueeze(2).to_broadcast(shape)

        def over_rows(vec, r, np_=P):
            return vec.unsqueeze(1).to_broadcast([np_, r, D])

        @block.tensor
        def _(pe):
            mm, tr = nc.tensor.matmul, nc.tensor.transpose
            pe.wait_ge(S["consts_set"], 1)

            def pairs_T(dst_ps, rows_sb, signal, np_=P, n=7):
                for q in range(n):
                    last = tr(dst_ps[:, q * P:q * P + np_], rows_sb[0:np_, 2 * q:2 * q + 2, :].rearrange("p t f -> p (t f)"),
                              ident[0:np_, 0:np_])
                last.then_inc(signal, 1)

            pe.wait_ge(S["rows_in"], 1)
            for i in range(4):
                last = tr(SM[0:SW, i * P:(i + 1) * P], bc[:, i, :], ident[:, :])
            last.then_inc(S["rows_T"], 1)

            def chain(n, with_max=False):
                pe.wait_ge(S["chain_in"], n + 1)
                last = tr(SM[0:SW, 0:P], LS[:, :], ident[:, :])
                if with_max:
                    last = tr(SM[0:SW, P:2 * P], LM[:, :], ident[:, :])
                last.then_inc(S["chain_T"], 1)
                pe.wait_ge(S["chain_back_in"], n + 1)
                last = tr(SM[:, 2 * P:2 * P + SW], sC[:, :], ident[0:SW, 0:SW])
                if with_max:
                    last = tr(SM[:, 2 * P + SW:2 * P + 2 * SW], mC[:, :], ident[0:SW, 0:SW])
                last.then_inc(S["chain_back"], 1)

            chain(0)
            pe.wait_ge(S["loaded_w"], WLOADS * 16)

            def dense(i, np_=P, r=BR):
                n = r // 2

                def cols(a):
                    return a.rearrange("p (q m) -> p q m", m=P)[:, 0:n, 0:np_]

                first_ = isinstance(i, int) and i == 0
                pe.wait_ge(S["d_x1"], i + 1)
                if not first_:
                    pe.wait_ge(S["d_h0"], i)
                pairs_T(pT, dX1[:, db[0]], S["d_trx"], np_, n)
                pe.wait_ge(S["d_h0"], i + 1)
                if not first_:
                    pe.wait_ge(S["d_h1"], i)
                mm(cols(pM1), lhsT=W0b[:, :], rhs=dh0[:, 0:n, 0:np_], start=True, stop=True).then_inc(S["d_m1"], 1)
                pe.wait_ge(S["d_h1"], i + 1)
                if not first_:
                    pe.wait_ge(S["d_h2"], i)
                mm(cols(pM2), lhsT=W1b[:, :], rhs=dh1[:, 0:n, 0:np_], start=True, stop=True).then_inc(S["d_m2"], 1)
                if not first_:
                    pe.wait_ge(S["d_R1"], i)
                for q in range(n):
                    last = tr(pR1[0:np_, q * P:(q + 1) * P], dh1[:, q, 0:np_], ident[:, :])
                last.then_inc(S["d_r1"], 1)
                pe.wait_ge(S["d_h2"], i + 1)
                if not first_:
                    pe.wait_ge(S["d_u2"], i)
                mm(pO[0:np_, 0:n * P], lhsT=ones_r[0:1, 0:np_],
                   rhs=b2_r[0:1, 0:n].rearrange("o a s f -> o (a s f)"), start=True, stop=False)
                for q in range(n):
                    last = mm(pO[0:np_, q * P:(q + 1) * P], lhsT=dh2[:, q, 0:np_], rhs=W2b[:, :],
                              start=False, stop=(q == n - 1))
                last.then_inc(S["d_o"], 1)
                if not first_:
                    pe.wait_ge(S["d_R2"], i)
                for q in range(n):
                    last = tr(pR2[0:np_, q * P:(q + 1) * P], dh2[:, q, 0:np_], ident[:, :])
                last.then_inc(S["d_r2"], 1)

            db = [0]
            dense(0)
            with pe.Fori(0, 47) as j:
                for bb in range(2):
                    db[0] = 1 - bb
                    dense(j * 2 + (1 + bb))
            for i in (95, 96):
                db[0] = i % 2
                dense(i)
            db[0] = 1
            dense(97, TP, TR)

            pe.wait_ge(S["weights_ready"], 1)

            def gat(k, b, j, zero=False):
                b2 = b % 2
                pe.wait_ge(g_in[b2], (j * 2 + b // 2 + 1) * 48)
                if not zero:
                    pe.wait_ge(S["g_evd"], k)
                pairs_T(TRP[1], XD[:, b2], S["g_trd"])
                pe.wait_ge(S["g_xc"], k + 1)
                if not zero:
                    pe.wait_ge(S["g_eve"], k)
                pairs_T(TRP[0], XC[:, b2], S["g_trx"])
                pe.wait_ge(S["g_evx"], k + 1)
                pairs_T(TRP[0], EA[:, b2], S["g_tre"])
                if not zero:
                    pe.wait_ge(S["g_hsfree"], k)
                for q in range(7):
                    last = mm(HS[:, 2 * q:2 * q + 2, :].rearrange("p t f -> p (t f)"), lhsT=TS[0][:, q, :], rhs=WN[:, :],
                              start=True, stop=True)
                last.then_inc(S["g_hs"], 1)
                pe.wait_ge(S["g_evd"], k + 1)
                pe.wait_ge(S["g_eve"], k + 1)
                if not zero:
                    pe.wait_ge(S["g_z"], k)
                for q in range(7):
                    for i in range(3):
                        last = mm(LG[:, 2 * q:2 * q + 2, :].rearrange("p t h -> p (t h)"), lhsT=TS[i][:, q, :],
                                  rhs=WA[:, i, :], start=(i == 0), stop=(i == 2))
                last.then_inc(S["g_lg"], 1)

            gat(0, 0, 0, zero=True)
            for b in range(1, R4):
                gat(b, b, 0)
            with pe.Fori(1, NB4) as j:
                for b in range(R4):
                    gat(j * R4 + b, b, j)
            chain(1, with_max=True)

            for l in range(3):
                Wb = (W0b, W1b, W2b)[l]

                def gcn(k, b, k0=False):
                    at = CH * l + k
                    pe.wait_ge(S["l_pre"], at + 1)
                    if not (isinstance(k, int) and at < 2):
                        pe.wait_ge(S["l_ev"], at - 1)
                    pairs_T(TRP[b], PR[:, b], S["l_tr"])
                    pe.wait_ge(S["l_ev"], at + 1)
                    if not (isinstance(k, int) and at < 1):
                        pe.wait_ge(S["l_zfree"], at)
                    for q in range(7):
                        last = mm(HS[:, 2 * q:2 * q + 2, :].rearrange("p t f -> p (t f)"), lhsT=TS[b][:, q, :],
                                  rhs=Wb[:, :], start=True, stop=True)
                    last.then_inc(S["l_z"], 1)

                for k in range(R4):
                    gcn(k, k % 2)
                with pe.Fori(1, NB4) as j:
                    for b in range(R4):
                        gcn(j * R4 + b, b % 2)
                chain(2 + l)
                pe.wait_ge(S["s_mid"], l + 1)
                tr(SM[0:D, 0:P], su[:, :], ident[:, :]).then_inc(S["s_midT"], 1)
                pe.wait_ge(S["s_prT"], l + 1)
                mm(SM[:, 384:384 + D], lhsT=prT[:, :], rhs=Wb[0:D, 0:D], start=True, stop=True).then_inc(S["s_mm"], 1)

        @block.scalar
        def _(act):
            fn = nc.scalar.activation
            act.wait_ge(S["zeroed"], 1)
            act.wait_ge(S["deg_in"], 1)
            fn(dis[:, :], tmpT[:, :], ACT.Sqrt).then_inc(S["deg_sqrt"], 1)
            act.wait_ge(S["loaded_w"], WLOADS * 16)

            def sq1(m, np_=P, r=BR):
                act.wait_ge(S["d_c1"], m + 1)
                fn(dQ1[0:np_, 0:r], dC[0:np_, 0:r], ACT.Square).then_inc(S["d_sq1"], 1)

            def sd1(m, np_=P, r=BR):
                act.wait_ge(S["d_v1"], m + 1)
                fn(dst8[0:np_, 4, 0:r], dst8[0:np_, 5, 0:r], ACT.Sqrt, bias=eps_c[0:np_, :], scale=1.0 / D).then_inc(S["d_sd1"], 1)

            def sq2(m, np_=P, r=BR):
                act.wait_ge(S["d_c2"], m + 1)
                fn(dQ2[0:np_, 0:r], dU[0:np_, 0:r], ACT.Square).then_inc(S["d_sq2"], 1)

            def sd2(m, np_=P, r=BR):
                act.wait_ge(S["d_v2"], m + 1)
                fn(dst8[0:np_, 6, 0:r], dst8[0:np_, 7, 0:r], ACT.Sqrt, bias=eps_c[0:np_, :], scale=1.0 / D).then_inc(S["d_sd2"], 1)

            def dense(i, b, half, ln1=None, ln2=None, np_=P, r=BR):
                n = r // 2
                zero = isinstance(i, int) and i == 0

                def cols(a):
                    return a.rearrange("p (q m) -> p q m", m=P)[:, 0:n, 0:np_]

                if ln2:
                    sq2(i - 1, *ln2)
                act.wait_ge(S["d_trx"], i + 1)
                if not zero:
                    act.wait_ge(S["d_m1"], i)
                fn(dh0[:, 0:n, 0:np_], cols(pT), ACT.Copy).then_inc(S["d_h0"], 1)
                if ln1:
                    sq1(i + 1, *ln1)
                act.wait_ge(S["d_m1"], i + 1)
                if not zero:
                    act.wait_ge(S["d_r1"], i)
                fn(dh1[:, 0:n, 0:np_], cols(pM1), ACT.Relu, bias=b0c[:, :]).then_inc(S["d_h1"], 1)
                if ln2:
                    sd2(i - 1, *ln2)
                act.wait_ge(S["d_m2"], i + 1)
                if not zero:
                    act.wait_ge(S["d_r2"], i)
                fn(dh2[:, 0:n, 0:np_], cols(pM2), ACT.Relu, bias=b1c[:, :]).then_inc(S["d_h2"], 1)
                if ln1:
                    sd1(i + 1, *ln1)
                for j_, (ready, ps_, buf, done) in enumerate((("d_r1", pR1, dR1, "d_R1"), ("d_r2", pR2, dR2, "d_R2"))):
                    act.wait_ge(S[ready], i + 1)
                    act.wait_ge(d_st[1 + j_][b], half * 16)
                    fn(buf[0:np_, b, 0:r].rearrange("p t f -> p (t f)"), ps_[0:np_, 0:n * P], ACT.Copy).then_inc(S[done], 1)

            full = (P, BR)
            sq1(0)
            sd1(0)
            dense(0, 0, 0, ln1=full)

            def two(j):
                for bb in range(2):
                    dense(j * 2 + (1 + bb), 1 - bb, j + bb, ln1=full, ln2=full)

            turns(act, 47, two)
            dense(95, 1, 47, ln1=full, ln2=full)
            dense(96, 0, 48, ln1=(TP, TR), ln2=full)
            dense(97, 1, 48, ln2=full, np_=TP, r=TR)
            sq2(97, TP, TR)
            sd2(97, TP, TR)

            def evac(k, b, j, zero=False):
                act.wait_ge(g_ld[b], (j + 1) * 16 * C)
                if not (isinstance(k, int) and k < 2):
                    act.wait_ge(S["g_trx"], k - 1)
                fn(XC[:, b % 2], G[:, b, :, 0:D], ACT.Copy).then_inc(S["g_xc"], 1)
                for i, ready, bank, done in ((1, "g_trd", 1, "g_evd"), (0, "g_trx", 0, "g_evx"), (2, "g_tre", 0, "g_eve")):
                    act.wait_ge(S[ready], k + 1)
                    if not zero:
                        act.wait_ge(S["g_lg"], k)
                    fn(TS[i][:, :, :].rearrange("p q m -> p (q m)"), TRP[bank], ACT.Copy).then_inc(S[done], 1)

            def gat(k, b, j, last=False):
                b2, half = b % 2, j * 2 + b // 2
                act.wait_ge(S["g_de"], k + 1)
                fn(RX[:, :, :], DE[:, :, :], ACT.Exp).then_inc(S["g_ex"], 1)
                act.wait_ge(S["g_ex"], k + 1)
                fn(AB[:, 0:D, 1:C1].rearrange("p (h d) t -> p h d t", d=HD),
                   RX[:, 0:H, :].unsqueeze(2).to_broadcast([P, H, HD, C]), ACT.Copy).then_inc(S["g_ab"], 1)
                fn(AB[:, D:SW, 1:C1], RX[:, 0:H, :], ACT.Copy).then_inc(S["g_ab"], 1)
                fn(B[:, D:SW, 1:C1], RX[:, H:2 * H, :], ACT.Copy).then_inc(S["g_ab"], 1)
                if not last:
                    evac(k + 1, (b + 1) % R4, j + (1 if b == R4 - 1 else 0))
                act.wait_ge(S["g_S"], k + 1)
                act.wait_ge(g_out[0][b2], half * 16)
                fn(NR[:, b2, :, D:SW], SS[:, b2, D:SW, 1:C1].rearrange("p h t -> p t h"), ACT.Copy).then_inc(S["g_nr"], 1)
                fn(NR[:, b2, :, SW:GW], M[:, b2, :, 1:C1].rearrange("p h t -> p t h"), ACT.Copy).then_inc(S["g_nr"], 1)
                act.wait_ge(S["g_c"], k + 1)
                fn(Q[:, :, :], U[:, :, :], ACT.Square).then_inc(S["g_q"], 1)
                act.wait_ge(S["g_v"], k + 1)
                fn(est[:, 3, :], est[:, 2, :], ACT.Sqrt, bias=eps_c[:, :], scale=1.0 / D).then_inc(S["g_sd"], 1)

            evac(0, 0, 0, zero=True)
            for b in range(R4):
                gat(b, b, 0)
            with act.Fori(1, NB4 - 1) as j:
                for b in range(R4):
                    gat(j * R4 + b, b, j)
            for k in range(CH - R4, CH):
                gat(k, k % R4, k // R4, last=(k == CH - 1))

            def seam_exp(n, *tiles):
                act.wait_ge(S["s_ex_in"], n)
                for t in tiles:
                    fn(t, t, ACT.Exp).then_inc(S["s_ex"], 1)

            def seam_norm(n):
                act.wait_ge(S["s_c"], n)
                fn(sq[:, :], su[:, :], ACT.Square).then_inc(S["s_q"], 1)
                act.wait_ge(S["s_v"], n)
                fn(sst[:, 3:4], sst[:, 2:3], ACT.Sqrt, bias=eps_c[:, :], scale=1.0 / D).then_inc(S["s_sd"], 1)

            seam_exp(1, rE[:, :], bE[:, :])
            seam_exp(2, wS[:, :], wC[:, :])
            seam_norm(1)

            for l in range(3):
                def flags(k, b):
                    at = CH * l + k
                    if not (isinstance(k, int) and at < 2):
                        act.wait_ge(S["l_scan"], at - 1)
                    nc.scalar.sem_inc(S["turn"], 1)
                    fn(AS[:, b, :, 1:C1], same[:, bass.ds(k * C, C)].unsqueeze(1).to_broadcast([P, D, C]),
                       ACT.Copy).then_inc(S["l_as"], 1)

                def gcn(k, b, norm, more=True):
                    at = CH * l + k
                    act.wait_ge(S["l_tr"], at + 1)
                    if not (isinstance(k, int) and at < 2):
                        act.wait_ge(S["l_z"], at - 1)
                    fn(TS[b][:, :, :].rearrange("p q m -> p (q m)"), TRP[b], ACT.Copy).then_inc(S["l_ev"], 1)
                    if more:
                        flags(k + 2, b)
                    if norm:
                        norm_of(k - 1)

                def norm_of(k):
                    act.wait_ge(S["l_c"], k + 1)
                    fn(Q[:, :, :], U[:, :, :], ACT.Square).then_inc(S["l_q"], 1)
                    act.wait_ge(S["l_v"], k + 1)
                    fn(est[:, 3, :], est[:, 2, :], ACT.Sqrt, bias=eps_c[:, :], scale=1.0 / D).then_inc(S["l_sd"], 1)

                flags(0, 0)
                flags(1, 1)
                for k in range(R4):
                    gcn(k, k % 2, l == 2 and k > 0)
                with act.Fori(1, NB4 - 1) as j:
                    for b in range(R4):
                        gcn(j * R4 + b, b % 2, l == 2)
                for k in range(CH - R4, CH):
                    gcn(k, k % 2, l == 2, more=k + 2 < CH)
                if l == 2:
                    norm_of(CH - 1)
            seam_norm(2)

        @block.vector
        def _(dve):
            v = nc.vector
            tt, ts, stt = v.tensor_tensor, v.tensor_scalar, v.scalar_tensor_tensor
            step = Steps(S["vector_step"])

            def do(instruction):
                step.on(dve, instruction)

            for tile, value in ((ident, 0.0), (src_i, 0), (ew, 0.0), (padneg, 0.0), (negs, -BIG), (prev_i, -1), (next_i, -1),
                                (WN, 0.0), (W0b, 0.0), (W1b, 0.0), (W2b, 0.0), (eps_c, EPS), (ones_r, 1.0), (LS, 0.0)):
                v.memset(tile[:, :], value)
            v.memset(WA[:, :, :], 0.0)
            v.memset(XM[:, :, :, D:XW], 0.0)
            v.memset(AM[:, :, 0:1], -BIG)
            v.memset(AB[:, :, 0:1], 0.0)
            v.memset(AS[:, :, :, 0:1], 0.0)
            v.memset(M[:, 1], -BIG)
            v.memset(SS[:, 1], 0.0)
            v.memset(mC[:, 0:1], -BIG)
            v.memset(rE[:, 0:1], -BIG)
            v.memset(sC[:, 0:1], 0.0).then_inc(S["zeroed"], 1)
            dve.wait_ge(S["zeroed"], 1)

            dve.wait_ge(S["loaded_idx"], ILOADS * 16)
            dve.wait_ge(S["ends_loaded"], 32)
            dve.wait_ge(S["consts_set"], 2)
            dve.wait_ge(S["filled"], 16)
            v.tensor_copy(dstf[:, :], dst_i[:, :])
            v.tensor_copy(srcf[:, :], src_i[:, :])
            v.tensor_copy(slotf[:, :], slot_i[:, :])
            v.tensor_copy(c_prev, prev_i[:, :])
            v.memset(same[:, 0:1], 0.0)
            do(v.tensor_copy(c_next, next_i[:, :]))
            tt(same[:, 1:T], dstf[:, 1:T], dstf[:, 0:T - 1], ALU.is_equal)
            tt(isend[:, 0:T - 1], dstf[:, 1:T], dstf[:, 0:T - 1], ALU.not_equal)
            tt(isend[:, T - 1:T], dstf[:, T - 1:T], c_next, ALU.not_equal)
            ts(first[:, :], dstf[:, :], dstf[:, 0:1], None, ALU.is_equal)
            tt(c_cont, dstf[:, 0:1], c_prev, ALU.is_equal)
            do(tt(c_whole, dstf[:, 0:1], dstf[:, T - 1:T], ALU.is_equal))
            ts(breakf[:, :], same[:, :], BIG, -BIG, ALU.mult, ALU.add)
            tt(c_run, c_whole, c_cont, ALU.mult)
            v.tensor_reduce(c_t1, first[:, :], axis=AX.X, op=ALU.add)
            tt(shiftf[:, :], slotf[:, :], dstf[:, :], ALU.subtract)
            do(ts(tmpT[:, :], isend[:, :], -SKIP, SKIP, ALU.mult, ALU.add))
            ts(shiftf[:, :], shiftf[:, :], float(SLOT0), None, ALU.add)
            tt(map_i[:, :], tmpT[:, :], dstf[:, :], ALU.add)
            tt(c_slot, slotf[:, 0:1], c_t1, ALU.add)
            do(tt(onehot[:, :], isend[:, :], first[:, :], ALU.mult))
            tt(onehot[:, :], isend[:, :], onehot[:, :], ALU.subtract)
            do(ts(c_slot, c_slot, -1.0, None, ALU.add))
            do(ts(tmpT[:, :], onehot[:, :], -SKIP, SKIP, ALU.mult, ALU.add))
            tt(out_i[:, :], tmpT[:, :], dstf[:, :], ALU.add)
            v.tensor_copy(i_slot, c_slot)
            ts(i_row, c_slot, float(SLOT0), None, ALU.add)
            do(ts(onehot[:, :], slotf[:, :], c_slot, None, ALU.is_equal))
            do(tt(tmpT[:, :], onehot[:, :], isend[:, :], ALU.mult))
            do(v.tensor_reduce(c_end, tmpT[:, :], axis=AX.X, op=ALU.add))
            do(ts(c_tmp, c_end, -SKIP, SKIP, ALU.mult, ALU.add))
            tt(i_out, c_tmp, dstf[:, 0:1], ALU.add).then_inc(S["flags_ready"], 1)

            wide = [P, SW]
            v.tensor_copy(bc[:, 0, :], c_run.to_broadcast(wide))
            v.tensor_copy(bc[:, 1, :], c_cont.to_broadcast(wide))
            ts(bc[:, 2, :], c_run.to_broadcast(wide), BIG, -BIG, ALU.mult, ALU.add)
            ts(bc[:, 3, :], c_cont.to_broadcast(wide), BIG, -BIG, ALU.mult, ALU.add).then_inc(S["rows_in"], 1)
            dve.wait_ge(S["rows_T"], 1)
            for i, r in enumerate((run_r, cont_r, nrun_r, ncont_r)):
                last = v.tensor_copy(r[:, :], SM[0:SW, i * P:(i + 1) * P])
            do(last)

            def carry_sums(n):
                dve.wait_ge(S["chain_T"], n + 1)
                do(v.tensor_tensor_scan(sE[:, :], run_r[:, :], SM[0:SW, 0:P], 0.0, ALU.mult, ALU.add))
                tt(sC[:, 1:P], sE[:, 0:P - 1], cont_r[:, 1:P], ALU.mult).then_inc(S["chain_back_in"], 1)
                dve.wait_ge(S["chain_back"], n + 1)

            do(v.tensor_tensor_scan(deg[:, :], same[:, :], ew[:, :], 0.0, ALU.mult, ALU.add))
            v.tensor_copy(LS[:, :], deg[:, T - 1:T].to_broadcast(wide)).then_inc(S["chain_in"], 1)
            carry_sums(0)
            do(v.tensor_copy(c_tmp, SM[:, 2 * P:2 * P + 1]))
            do(stt(out=deg[:, :], in0=first[:, :], scalar=c_tmp, in1=deg[:, :], op0=ALU.mult, op1=ALU.add))
            do(ts(deg[:, :], deg[:, :], 1.0, None, ALU.add))
            ts(tmpT[:, :], deg[:, :], 1e-30, None, ALU.max).then_inc(S["deg_in"], 1)
            do(ts(deg[:, :], deg[:, :], 0.0, None, ALU.is_gt))
            dve.wait_ge(S["deg_sqrt"], 1)
            do(v.reciprocal(dis[:, :], dis[:, :]))
            do(tt(dis[:, :], dis[:, :], deg[:, :], ALU.mult))
            do(tt(tmpT[:, :], onehot[:, :], dis[:, :], ALU.mult))
            v.tensor_reduce(c_dis, tmpT[:, :], axis=AX.X, op=ALU.add).then_inc(S["seam_set"], 1)
            dve.wait_ge(S["seam_set"], 1)

            dve.wait_ge(S["loaded_w"], WLOADS * 16)
            for i, w in enumerate((Wn2, Wn2, We2)):
                last = tt(wprod[:, i, :], w[:, :], att_bc[:, i, :], ALU.mult)
            do(last)
            do(v.tensor_reduce(wred[:, :, :], wprod[:, :, :].rearrange("p i (h d) -> p i h d", d=HD), axis=AX.X, op=ALU.add))
            v.tensor_copy(WA[0:64, :, 0:H], wred[0:64, :, :])
            v.tensor_copy(WA[64:P, :, H:2 * H], wred[64:P, :, :]).then_inc(S["weights_ready"], 1)

            def center(u, st, i_sum, i_mean, r, np_):
                do(v.tensor_reduce(st[0:np_, i_sum, 0:r], u, axis=AX.X, op=ALU.add))
                do(ts(st[0:np_, i_mean, 0:r], st[0:np_, i_sum, 0:r], -1.0 / D, None, ALU.mult))
                return tt(u, u, repeat(st[0:np_, i_mean, 0:r], D), ALU.add)

            def ln1_a(m, b, half, np_=P, r=BR):
                dve.wait_ge(d_xl[b], half * 16 + 16)
                c_ = dC[0:np_, 0:r]
                if not (isinstance(m, int) and m == 0):
                    dve.wait_ge(S["d_x1"], m)
                stt(out=c_, in0=dX[0:np_, b, 0:r], scalar=2.0, in1=over_rows(bias_bc[0:np_, :], r, np_), op0=ALU.mult,
                    op1=ALU.add).then_inc(S["d_xfree"], 1)
                dve.wait_ge(S["d_xfree"], m + 1)
                center(c_, dst8, 0, 1, r, np_).then_inc(S["d_c1"], 1)

            def ln1_b(m, b, half, np_=P, r=BR):
                dve.wait_ge(S["d_sq1"], m + 1)
                v.tensor_reduce(dst8[0:np_, 5, 0:r], dQ1[0:np_, 0:r], axis=AX.X, op=ALU.add).then_inc(S["d_v1"], 1)

            def ln1_c(m, b, half, np_=P, r=BR):
                dve.wait_ge(S["d_sd1"], m + 1)
                do(v.reciprocal(dst8[0:np_, 4, 0:r], dst8[0:np_, 4, 0:r]))
                dve.wait_ge(d_st[0][b], half * 16)
                if not (isinstance(m, int) and m < 2):
                    dve.wait_ge(S["d_trx"], m - 1)
                tt(dX1[0:np_, b, 0:r], dC[0:np_, 0:r], repeat(dst8[0:np_, 4, 0:r], D), ALU.mult).then_inc(S["d_x1"], 1)

            def ln2_a(m, b, half, np_=P, r=BR):
                dve.wait_ge(S["d_o"], m + 1)
                u = dU[0:np_, 0:r]
                if not (isinstance(m, int) and m == 0):
                    dve.wait_ge(S["d_O"], m)
                stt(out=u, in0=pO[0:np_, 0:r * D].rearrange("p (t f) -> p t f", f=D), scalar=0.0, in1=dX1[0:np_, b, 0:r],
                    op0=ALU.max, op1=ALU.add).then_inc(S["d_u2"], 1)
                dve.wait_ge(S["d_u2"], m + 1)
                center(u, dst8, 2, 3, r, np_).then_inc(S["d_c2"], 1)

            def ln2_b(m, b, half, np_=P, r=BR):
                dve.wait_ge(S["d_sq2"], m + 1)
                v.tensor_reduce(dst8[0:np_, 7, 0:r], dQ2[0:np_, 0:r], axis=AX.X, op=ALU.add).then_inc(S["d_v2"], 1)

            def ln2_c(m, b, half, np_=P, r=BR):
                dve.wait_ge(S["d_sd2"], m + 1)
                do(v.reciprocal(dst8[0:np_, 6, 0:r], dst8[0:np_, 6, 0:r]))
                dve.wait_ge(d_st[3][b], half * 16)
                tt(dO[0:np_, b, 0:r], dU[0:np_, 0:r], repeat(dst8[0:np_, 6, 0:r], D), ALU.mult).then_inc(S["d_O"], 1)

            def both(a, c):
                for two, one in ((ln2_a, ln1_a), (ln2_b, ln1_b), (ln2_c, ln1_c)):
                    if a:
                        two(*a)
                    if c:
                        one(*c)

            both(None, (0, 0, 0))
            both(None, (1, 1, 0))

            def two(j):
                for bb in range(2):
                    both((j * 2 + bb, bb, j), (j * 2 + (2 + bb), bb, j + 1))

            turns(dve, 47, two, step, 12)
            both((94, 0, 47), (96, 0, 48))
            both((95, 1, 47), (97, 1, 48, TP, TR))
            both((96, 0, 48), None)
            both((97, 1, 48, TP, TR), None)

            def norm_rows(k, c_sem, q_sem, v_sem, sd_sem):
                center(U[:, :, :], est, 0, 1, C, P).then_inc(S[c_sem], 1)
                dve.wait_ge(S[q_sem], k + 1)
                v.tensor_reduce(est[:, 2, :], Q[:, :, :], axis=AX.X, op=ALU.add).then_inc(S[v_sem], 1)
                dve.wait_ge(S[sd_sem], k + 1)
                do(v.reciprocal(est[:, 3, :], est[:, 3, :]))

            def gat(k, b, j):
                b2, half, cs = b % 2, j * 2 + b // 2, bass.ds(k * C, C)
                dve.wait_ge(g_ld[b], (j + 1) * 16 * C)
                tt(row_i[:, cs], srcf[:, cs], G[:, b, :, D], ALU.add).then_inc(S["g_shift"], 1)
                do(v.tensor_copy(AM[:, :, 1:C1], breakf[:, cs].unsqueeze(1).to_broadcast([P, H, C])))
                v.tensor_copy(LB[:, :, 0], M[:, 1 - b2, :, C])
                dve.wait_ge(S["g_lg"], k + 1)
                tt(Z[:, :, :], LG, repeat(padneg[:, cs], H), ALU.add).then_inc(S["g_z"], 1)
                dve.wait_ge(S["g_z"], k + 1)
                do(stt(out=LB[:, :, 1:C1].rearrange("p h t -> p t h"), in0=Z[:, :, :], scalar=0.01, in1=Z[:, :, :],
                       op0=ALU.mult, op1=ALU.max))
                do(v.tensor_tensor_scan(M[:, b2].rearrange("p h t -> p (h t)"), AM[:, :, :].rearrange("p h t -> p (h t)"),
                                        LB[:, :, :].rearrange("p h t -> p (h t)"), 0.0, ALU.add, ALU.max))
                tt(DE[:, H:2 * H, :], LB[:, :, 1:C1], M[:, b2, :, 1:C1], ALU.subtract)
                do(tt(DE[:, 0:H, :], M[:, b2, :, 0:C], M[:, b2, :, 1:C1], ALU.subtract))
                tt(DE[:, 0:H, :], DE[:, 0:H, :], AM[:, :, 1:C1], ALU.add).then_inc(S["g_de"], 1)
                dve.wait_ge(g_in[b2], half * 48 + 48)
                stt(out=U[:, :, :], in0=XD[:, b2], scalar=2.0, in1=over_rows(bias_bc[:, :], C), op0=ALU.mult,
                    op1=ALU.add).then_inc(S["g_xdfree"], 1)
                v.tensor_copy(B[:, :, 0], SS[:, 1 - b2, :, C])
                dve.wait_ge(S["g_ex"], k + 1)
                dve.wait_ge(S["g_hs"], k + 1)
                tt(B[:, 0:D, 1:C1].rearrange("p (h d) t -> p h d t", d=HD), HS.rearrange("p t (h d) -> p h d t", d=HD),
                   RX[:, H:2 * H, :].unsqueeze(2).to_broadcast([P, H, HD, C]), ALU.mult).then_inc(S["g_hsfree"], 1)
                dve.wait_ge(S["g_hsfree"], k + 1)
                dve.wait_ge(S["g_ab"], k * 3 + 3)
                v.tensor_tensor_scan(SS[:, b2].rearrange("p f t -> p (f t)"), AB[:, :, :].rearrange("p f t -> p (f t)"),
                                     B[:, :, :].rearrange("p f t -> p (f t)"), 0.0, ALU.mult, ALU.add).then_inc(S["g_S"], 1)
                dve.wait_ge(S["g_S"], k + 1)
                do(v.reciprocal(RD[:, :, :], SS[:, b2, D:SW, 1:C1]))
                dve.wait_ge(g_out[0][b2], half * 16)
                tt(NR[:, b2, :, 0:D].rearrange("p t (h d) -> p h d t", d=HD),
                   SS[:, b2, 0:D, 1:C1].rearrange("p (h d) t -> p h d t", d=HD),
                   RD[:, :, :].unsqueeze(2).to_broadcast([P, H, HD, C]), ALU.mult).then_inc(S["g_nrm"], 1)
                dve.wait_ge(S["g_nrm"], k + 1)
                do(tt(U[:, :, :], U[:, :, :], NR[:, b2, :, 0:D], ALU.add))
                norm_rows(k, "g_c", "g_q", "g_v", "g_sd")
                dve.wait_ge(g_out[1][b2], half * 16)
                tt(X1[:, b2], U[:, :, :], repeat(est[:, 3, :], D), ALU.mult).then_inc(S["g_x1"], 1)
                dve.wait_ge(S["g_x1"], k + 1)
                dve.wait_ge(g_out[2][b2], half * 16)
                tt(Y0[:, b2], X1[:, b2], repeat(dis[:, cs], D), ALU.mult).then_inc(S["g_y0"], 1)

            def gat_four(j):
                for b in range(R4):
                    gat(j * R4 + b, b, j)

            turns(dve, NB4, gat_four, step, 9 * R4)

            def heads(ap4, n=HD):
                return ap4.unsqueeze(2).to_broadcast([P, H, n])

            def by_head(ap64):
                return ap64.rearrange("p (h d) -> p h d", d=HD)

            def seam_norm(n):
                do(v.tensor_reduce(sst[:, 0:1], su[:, :], axis=AX.X, op=ALU.add))
                do(ts(sst[:, 1:2], sst[:, 0:1], -1.0 / D, None, ALU.mult))
                ts(su[:, :], su[:, :], sst[:, 1:2], None, ALU.add).then_inc(S["s_c"], 1)
                dve.wait_ge(S["s_q"], n)
                v.tensor_reduce(sst[:, 2:3], sq[:, :], axis=AX.X, op=ALU.add).then_inc(S["s_v"], 1)
                dve.wait_ge(S["s_sd"], n)
                do(v.reciprocal(sst[:, 3:4], sst[:, 3:4]))

            v.tensor_copy(LS[:, :], SS[:, 1, :, C])
            v.tensor_copy(by_head(LM[:, 0:D]), heads(M[:, 1, :, C]))
            v.tensor_copy(LM[:, D:SW], M[:, 1, :, C]).then_inc(S["chain_in"], 1)
            dve.wait_ge(S["chain_T"], 2)
            do(v.tensor_tensor_scan(mE[:, :], nrun_r[:, :], SM[0:SW, P:2 * P], -BIG, ALU.add, ALU.max))
            tt(bE[:, :], SM[0:SW, P:2 * P], mE[:, :], ALU.subtract)
            tt(mC[:, 1:P], mE[:, 0:P - 1], ncont_r[:, 1:P], ALU.add)
            do(tt(rE[:, 1:P], mE[:, 0:P - 1], mE[:, 1:P], ALU.subtract))
            tt(rE[:, 1:P], rE[:, 1:P], nrun_r[:, 1:P], ALU.add).then_inc(S["s_ex_in"], 1)
            dve.wait_ge(S["s_ex"], 2)
            do(tt(bE[:, :], SM[0:SW, 0:P], bE[:, :], ALU.mult))
            do(v.tensor_tensor_scan(sE[:, :], rE[:, :], bE[:, :], 0.0, ALU.mult, ALU.add))
            tt(sC[:, 1:P], sE[:, 0:P - 1], cont_r[:, 1:P], ALU.mult).then_inc(S["chain_back_in"], 1)
            dve.wait_ge(S["s_row"], 32)
            tt(by_head(S68[:, 0:D]), by_head(grow[:, 0:D]), heads(grow[:, D:SW]), ALU.mult)
            v.tensor_copy(S68[:, D:SW], grow[:, D:SW])
            v.tensor_copy(by_head(M68[:, 0:D]), heads(grow[:, SW:GW]))
            do(v.tensor_copy(M68[:, D:SW], grow[:, SW:GW]))
            dve.wait_ge(S["chain_back"], 2)
            carS, carM = SM[:, 2 * P:2 * P + SW], SM[:, 2 * P + SW:2 * P + 2 * SW]
            do(tt(MM[:, :], M68[:, :], carM, ALU.max))
            tt(wS[:, :], M68[:, :], MM[:, :], ALU.subtract)
            tt(wC[:, :], carM, MM[:, :], ALU.subtract).then_inc(S["s_ex_in"], 1)
            dve.wait_ge(S["s_ex"], 4)
            tt(S68[:, :], S68[:, :], wS[:, :], ALU.mult)
            do(tt(wC[:, :], carS, wC[:, :], ALU.mult))
            do(tt(S68[:, :], S68[:, :], wC[:, :], ALU.add))
            do(v.reciprocal(sden[:, :], S68[:, D:SW]))
            do(tt(by_head(su[:, :]), by_head(S68[:, 0:D]), heads(sden[:, :]), ALU.mult))
            do(stt(out=su[:, :], in0=xrow[:, :], scalar=2.0, in1=su[:, :], op0=ALU.mult, op1=ALU.add))
            do(tt(su[:, :], su[:, :], bias_bc[:, :], ALU.add))
            seam_norm(1)
            do(ts(x1row[:, :], su[:, :], sst[:, 3:4], None, ALU.mult))
            ts(yrow[:, :], x1row[:, :], c_dis, None, ALU.mult).then_inc(S["s_out"], 1)

            for l in range(3):
                def sums(k, b, j):
                    b2, half, cs, at = b % 2, j * 2 + b // 2, bass.ds(k * C, C), CH * l + k
                    dve.wait_ge(l_ld[b], (j + (1 + l * NB4)) * 16 * C)
                    v.tensor_copy(B[:, 0:D, 0], SS[:, 1 - b2, 0:D, C])
                    tt(B[:, 0:D, 1:C1].rearrange("p f t -> p t f"), GX[:, b], repeat(ew[:, cs], D), ALU.mult).then_inc(S["l_gfree"], 1)
                    dve.wait_ge(S["l_gfree"], at + 1)
                    dve.wait_ge(S["l_as"], at + 1)
                    v.tensor_tensor_scan(SS[:, b2, 0:D].rearrange("p f t -> p (f t)"), AS[:, b2].rearrange("p f t -> p (f t)"),
                                         B[:, 0:D].rearrange("p f t -> p (f t)"), 0.0, ALU.mult, ALU.add).then_inc(S["l_scan"], 1)
                    dve.wait_ge(S["l_scan"], at + 1)
                    dve.wait_ge(l_in[b2], l * HALF + (half + 1) * (32 if l == 2 else 16))
                    dve.wait_ge(l_out[0][b2], l * HALF + half * 16)
                    if not (isinstance(k, int) and at < 2):
                        dve.wait_ge(S["l_tr"], at - 1)
                    tt(PR[:, b2], SS[:, b2, 0:D, 1:C1].rearrange("p f t -> p t f"), XD[:, b2], ALU.add).then_inc(S["l_pre"], 1)

                def rows_of(k, b, j):
                    b2, half, cs, at = b % 2, j * 2 + b // 2, bass.ds(k * C, C), CH * l + k
                    if not (isinstance(k, int) and k == 0):
                        dve.wait_ge(S["l_y"] if l < 2 else S["l_o"], at if l < 2 else k)
                    dve.wait_ge(S["l_z"], at + 1)
                    tt(U[:, :, :], HS, repeat(dis[:, cs], D), ALU.mult).then_inc(S["l_zfree"], 1)
                    dve.wait_ge(S["l_zfree"], at + 1)
                    do(tt(U[:, :, :], U[:, :, :], over_rows(b_bc[l][:, :], C), ALU.add))
                    if l < 2:
                        dve.wait_ge(l_out[1][b2], l * HALF + half * 16)
                        stt(out=Y0[:, b2], in0=U[:, :, :], scalar=0.0, in1=repeat(dis[:, cs], D), op0=ALU.max,
                            op1=ALU.mult).then_inc(S["l_y"], 1)
                    else:
                        stt(out=U[:, :, :], in0=U[:, :, :], scalar=0.0, in1=EA[:, b2], op0=ALU.max,
                            op1=ALU.add).then_inc(S["l_u"], 1)
                        dve.wait_ge(S["l_u"], k + 1)
                        norm_rows(k, "l_c", "l_q", "l_v", "l_sd")
                        dve.wait_ge(o_st[b], j * 16 * C)
                        tt(OB[:, b], U[:, :, :], repeat(est[:, 3, :], D), ALU.mult).then_inc(S["l_o"], 1)

                each = 1 if l < 2 else 4
                sums(0, 0, 0)

                def gcn_four(j):
                    for b in range(R4):
                        sums(j * R4 + (b + 1), (b + 1) % R4, j + (1 if b == R4 - 1 else 0))
                        rows_of(j * R4 + b, b, j)

                turns(dve, NB4 - 1, gcn_four, step, each * R4)
                for k in range(CH - R4, CH):
                    if k + 1 < CH:
                        sums(k + 1, (k + 1) % R4, (k + 1) // R4)
                    rows_of(k, k % R4, k // R4)

                v.tensor_copy(LS[:, 0:D], SS[:, 1, 0:D, C]).then_inc(S["chain_in"], 1)
                carry_sums(2 + l)
                dve.wait_ge(S["s_row"], 48 + 16 * l)
                tt(su[:, :], prow[:, :], SM[:, 2 * P:2 * P + D], ALU.add).then_inc(S["s_mid"], 1)
                dve.wait_ge(S["s_midT"], l + 1)
                v.tensor_copy(prT[:, :], SM[0:D, 0:P]).then_inc(S["s_prT"], 1)
                dve.wait_ge(S["s_mm"], l + 1)
                do(ts(su[:, :], SM[:, 384:384 + D], c_dis, None, ALU.mult))
                do(tt(su[:, :], su[:, :], b_bc[l][:, :], ALU.add))
                dve.wait_ge(S["s_stored"], 32 + 16 * l)
                if l < 2:
                    ts(yrow[:, :], su[:, :], 0.0, c_dis, ALU.max, ALU.mult).then_inc(S["s_out"], 1)
                else:
                    do(stt(out=su[:, :], in0=su[:, :], scalar=0.0, in1=x1row[:, :], op0=ALU.max, op1=ALU.add))
                    seam_norm(2)
                    ts(yrow[:, :], su[:, :], sst[:, 3:4], None, ALU.mult).then_inc(S["s_out"], 1)


_INS = ["x", "src", "dst", "edge_attr_64", "edge_weight", "L0_gnn_W_node", "L0_gnn_W_edge", "L0_gnn_attn_query",
        "L0_gnn_attn_key", "L0_gnn_attn_edge", "L0_gnn_bias", "L1_gnn_W0", "L1_gnn_b0", "L1_gnn_W1", "L1_gnn_b1",
        "L1_gnn_W2", "L1_gnn_b2"]


def kernel(**inputs):
    import numpy as np
    import concourse.bacc as bacc
    from concourse import mybir
    from concourse.bass_utils import run_bass_kernel_spmd

    nc = bacc.Bacc("TRN2", target_bir_lowering=False, num_devices=1)
    arrays, ap = {}, {}
    for name in _INS:
        a = np.ascontiguousarray(inputs[name])
        arrays[f"in_{name}"] = a
        ap[name] = nc.dram_tensor(f"in_{name}", a.shape, mybir.dt.from_np(a.dtype), kind="ExternalInput").ap()
    out = nc.dram_tensor("out_rows", [N, D], F32, kind="ExternalOutput").ap()
    build(nc, ap["x"], ap["src"], ap["dst"], ap["edge_attr_64"], ap["edge_weight"], ap["L0_gnn_W_node"], ap["L0_gnn_W_edge"],
          ap["L0_gnn_attn_query"], ap["L0_gnn_attn_key"], ap["L0_gnn_attn_edge"], ap["L0_gnn_bias"],
          ap["L1_gnn_W0"], ap["L1_gnn_b0"], ap["L1_gnn_W1"], ap["L1_gnn_b1"], ap["L1_gnn_W2"], ap["L1_gnn_b2"], out)
    r = run_bass_kernel_spmd(nc, [arrays], core_ids=[0])
    return r.results[0]["out_rows"]
```

```python
from contextlib import ExitStack

import concourse.bass as bass
from concourse import mybir

F32 = mybir.dt.float32
I32 = mybir.dt.int32
ALU = mybir.AluOpType
ACT = mybir.ActivationFunctionType
AX = mybir.AxisListType

P = 128
N, E, D, H = 100000, 50000, 64, 4
PC = 2 * (D + H)
HD = D // H
T = 392
PA, TA = 112, 392
PB, TB = 16, 381
assert PA * TA + PB * TB == E and PA + PB == P
C = 14
TX = T + C
CH = T // C
R4 = 4
NB4 = CH // R4
SW = D + H
SLOT0 = N
ROWS = N + P * T
XW = 68
GW = D + 2 * H
C1 = C + 1
W = C * D
BR = 8
BN = P * BR
FULL = N // BN
TP, TR = 112, 6
assert FULL * BN + TP * TR == N and FULL == 97
BIG = 1.0e30
SKIP = 200000.0
EPS = 1e-5


ILOADS = 6 + T - TB
WLOADS = 25


class Steps:

    def __init__(self, sem):
        self.sem, self.base, self.n, self.turns = sem, 0, 0, 0

    def enter(self, j, each):
        self.base, self.n, self.turns, self.each = self.base + self.n, 0, j, each

    def leave(self, count):
        assert self.n == self.each, (self.n, self.each)
        self.base, self.n, self.turns = self.base + self.each * count, 0, 0

    def on(self, engine, instruction):
        instruction.then_inc(self.sem, 1)
        self.n += 1
        at = self.base + self.n
        if not isinstance(self.turns, int):
            at = self.turns * self.each + at
        engine.wait_ge(self.sem, at)


def turns(engine, count, body, step=None, each=0, peel=1):
    for j in range(peel):
        body(j)
    with engine.Fori(peel, count) as j:
        if step:
            step.enter(j - peel, each)
        body(j)
        if step:
            step.leave(count - peel)


def build(nc, x, src, dst, edge_attr, edge_weight, W_node, W_edge, a_query, a_key, a_edge, bias,
          W0, b0, W1, b1, W2, b2, out):
    with ExitStack() as ctx:
        def sb(name, shape, dt=F32):
            return ctx.enter_context(nc.sbuf_tensor(name, shape, dt))

        def sem(name):
            return ctx.enter_context(nc.semaphore(name))

        def dram(name, shape):
            return nc.dram_tensor(name, shape, F32, kind="Internal").ap()

        xs_dram = dram("xs_dram", [N, XW])
        xd_dram = dram("xd_dram", [P * T, D])
        gat_dram = dram("gat_dram", [P * T, GW])
        x1_dram = dram("x1_dram", [P * T, D])
        pre_dram = [dram(f"pre{l}_dram", [P * T, D]) for l in range(3)]
        tab_dram = [dram(f"tab{l}_dram", [ROWS, D]) for l in range(3)]

        def slots(ap, k):
            return ap.rearrange("(p t) f -> p t f", t=T)[:, bass.ds(k * C, C), :]

        def tab_slots(l, k):
            return slots(tab_dram[l][SLOT0:ROWS, :], k)

        ident = sb("ident", [P, P])
        src_i, dst_i = sb("src_i", [P, TX], I32), sb("dst_i", [P, TX], I32)
        ew = sb("ew", [P, T])
        srcf, dstf = sb("srcf", [P, T]), sb("dstf", [P, T])
        prev_i, next_i = sb("prev_i", [P, 1], I32), sb("next_i", [P, 1], I32)
        same, breakf, isend, first = (sb(n, [P, T]) for n in ("same", "breakf", "isend", "first"))
        slot_i, slotf = sb("slot_i", [P, T], I32), sb("slotf", [P, T])
        shiftf, tmpT, onehot = sb("shiftf", [P, TX]), sb("tmpT", [P, T]), sb("onehot", [P, T])
        map_i, out_i, row_i = (sb(n, [P, TX], I32) for n in ("map_i", "out_i", "row_i"))
        deg, dis, padneg = sb("deg", [P, T]), sb("dis", [P, T]), sb("padneg", [P, T])
        negs = sb("negs", [PB, T - TB])
        col = sb("col", [P, 16])
        (c_prev, c_next, c_cont, c_whole, c_t1, c_slot, c_dis, c_end, c_run, c_tmp) = (
            col[:, i:i + 1] for i in range(10))
        seam_i = sb("seam_i", [P, 4], I32)
        i_slot, i_row, i_out = (seam_i[:, i:i + 1] for i in range(3))
        eps_c = sb("eps_c", [P, 1])
        W0b, W1b, W2b = (sb(n, [P, P]) for n in ("W0b", "W1b", "W2b"))
        WM = sb("WM", [P, PC])
        WN = WM[:, 0:2 * D]
        Wn2, We2 = sb("Wn2", [P, D]), sb("We2", [P, D])
        wprod, wred = sb("wprod", [P, 3, D]), sb("wred", [P, 3, H])
        att_bc = sb("att_bc", [P, 3, D])
        WA = sb("WA", [P, 3, 2 * H])
        bias_bc = sb("bias_bc", [P, D])
        b_bc = [sb(f"b{l}_bc", [P, D]) for l in range(3)]
        b0c, b1c, b2c = (sb(n, [P, 1]) for n in ("b0c", "b1c", "b2c"))

        ix, ix2, sv = sb("ix", [P, R4, C], I32), sb("ix2", [P, R4, C], I32), sb("sv", [P, R4, C])
        G = sb("G", [P, R4, C, XW])
        GX = sb("GX", [P, R4, C, D])
        IN = sb("IN", [P, 4, W])
        XD, EA = (IN[:, 2 * i:2 * i + 2, :].rearrange("p b (t f) -> p b t f", f=D) for i in range(2))
        TS = [sb(f"TS{i}", [P, 2, 7, P]) for i in range(3)]
        Z, LB, AM = sb("Z", [P, C, H]), sb("LB", [P, H, C1]), sb("AM", [P, H, C1])
        M = sb("M", [P, 2, H, C1])
        DE, RX = sb("DE", [P, 2 * H, C]), sb("RX", [P, 2 * H, C])
        AB, B = sb("AB", [P, SW, C1]), sb("B", [P, SW, C1])
        AS = sb("AS", [P, 2, D, C1])
        SS = sb("SS", [P, 2, SW, C1])
        RD = sb("RD", [P, H, C])
        NR = sb("NR", [P, 2, C, GW])
        U, Q = sb("U", [P, C, D]), sb("Q", [P, C, D])
        X1, Y0 = sb("X1", [P, 2, C, D]), sb("Y0", [P, 2, C, D])
        PR = sb("PR", [P, 2, C, D])
        XC = PR
        OB = G[:, :, :, 0:D]
        est = sb("est", [P, 4, C])

        def early(tile, pattern):
            flat_ = tile.rearrange(pattern)
            return flat_[:, 0:2 * BR * D].rearrange("p (b t f) -> p b t f", b=2, f=D)

        dX1 = IN[:, :, 0:BR * D].rearrange("p b (t f) -> p b t f", f=D)
        dR1, dR2 = early(PR[:, :, :, :], "p b t f -> p (b t f)"), early(Y0[:, :, :, :], "p b t f -> p (b t f)")
        dO, dX = early(X1[:, :, :, :], "p b t f -> p (b t f)"), early(AS[:, :, :, :], "p b f t -> p (b f t)")
        dC, dQ2 = sb("dC", [P, BR, D]), sb("dQ2", [P, BR, D])
        dU, dQ1 = U[:, 0:BR, :], Q[:, 0:BR, :]
        dh0, dh1, dh2, dh3 = (sb(n, [P, 4, P]) for n in ("dh0", "dh1", "dh2", "dh3"))
        dst8 = sb("dst8", [P, 8, BR])
        XM = sb("XM", [P, 4, BR, XW])

        bc = sb("bc", [P, 4, SW])
        run_r, cont_r, nrun_r, ncont_r = (sb(n, [SW, P]) for n in ("run_r", "cont_r", "nrun_r", "ncont_r"))
        LS, LM = sb("LS", [P, SW]), sb("LM", [P, SW])
        mE, mC, rE, bE, sE, sC = (sb(n, [SW, P]) for n in ("mE", "mC", "rE", "bE", "sE", "sC"))
        cS, cM = sb("cS", [P, SW]), sb("cM", [P, SW])
        grow, xrow, prow = sb("grow", [P, GW]), sb("xrow", [P, D]), sb("prow", [P, D])
        S68, M68, MM, wS, wC = (sb(n, [P, SW]) for n in ("S68", "M68", "MM", "wS", "wC"))
        sden = sb("sden", [P, H])
        su, sq, x1row, yrow = (sb(n, [P, D]) for n in ("su", "sq", "x1row", "yrow"))
        prT = sb("prT", [D, P])
        sst = sb("sst", [P, 4])

        ps = ctx.enter_context(nc.psum_tensor("ps", [P, 8, 512], F32))
        pT, pM1, pM2, pM3, pR1, pR2, pO = (ps[:, i, :] for i in range(7))
        flat = ps[:, :, :].rearrange("p a b -> p (a b)")
        TRP = [flat[:, 0:W], flat[:, 1024:1024 + W]]
        HS = flat[:, 2048:2048 + W].rearrange("p (t f) -> p t f", f=D)

        def hl(q0, q1):
            at = 2048 + 512 * (q0 // 3) + PC * (q0 % 3)
            return flat[:, at:at + PC * (q1 - q0)].rearrange("p (q c) -> p q c", c=PC)

        SM = ps[:, 7, :]

        names = """consts_set zeroed loaded_idx loaded_w filled ends_loaded seam_set flags_ready weights_ready
            vector_step rows_in rows_T chain_in chain_T chain_back_in chain_back deg_in deg_sqrt
            d_xfree d_c1 d_sq1 d_v1 d_sd1 d_x1 d_trx d_h0 d_m1 d_h1 d_m2 d_r1 d_h2 d_r2 d_m3 d_h3 d_o
            d_R1 d_R2 d_u2 d_c2 d_sq2 d_v2 d_sd2 d_O
            idx_staged out_idx_staged turn
            g_shift g_xc g_trx g_trd g_tre g_evx g_evd g_eve g_lg g_z g_de g_ex g_ab g_hsfree g_S
            g_xdfree g_nr g_nrm g_c g_q g_v g_sd g_x1 g_y0
            l_gfree l_as l_scan l_pre l_tr l_ev l_z l_zfree l_u l_y l_c l_q l_v l_sd l_o
            s_row s_ex_in s_ex s_mid s_midT s_prT s_mm s_c s_q s_v s_sd s_out s_stored""".split()
        S = {n: sem(n) for n in names}
        d_xl = [sem(f"dense_x_loaded{b}") for b in range(2)]
        d_st = [[sem(f"dense_stored{j}_{b}") for b in range(2)] for j in range(4)]
        xm_ld = [sem(f"xs_loaded{b}") for b in range(4)]
        xm_st = [sem(f"xs_stored{b}") for b in range(4)]
        xg_ld = [sem(f"xdst_gathered{b}") for b in range(R4)]
        xg_st = [sem(f"xdst_stored{b}") for b in range(R4)]
        mp_st = [sem(f"shift_scattered{b}") for b in range(R4)]
        g_ld = [sem(f"gat_gathered{b}") for b in range(R4)]
        g_in = [sem(f"gat_inputs{b}") for b in range(2)]
        g_out = [[sem(f"gat_stored{j}_{b}") for b in range(2)] for j in range(3)]
        l_ld = [sem(f"gcn_gathered{b}") for b in range(R4)]
        l_in = [sem(f"gcn_inputs{b}") for b in range(2)]
        l_out = [[sem(f"gcn_stored{j}_{b}") for b in range(2)] for j in range(2)]
        o_st = [sem(f"rows_scattered{b}") for b in range(R4)]

        HALF = 16 * CH // 2
        BLOCKS = FULL + 1

        block = ctx.enter_context(nc.Block())

        @block.sync
        def _(sp):
            def need(sem_, value):
                sp.wait_ge(sem_, value)
                sp.sem_inc(S["turn"], 1)

            sp.wait_ge(S["zeroed"], 1)
            for tile, arr in ((src_i, src), (dst_i, dst), (ew, edge_weight)):
                sp.dma_start(tile[0:PA, 0:TA], arr[0:PA * TA].rearrange("(p t) -> p t", t=TA)).then_inc(S["loaded_idx"], 16)
                sp.dma_start(tile[PA:P, 0:TB], arr[PA * TA:E].rearrange("(p t) -> p t", t=TB)).then_inc(S["loaded_idx"], 16)
            with nc.allow_non_contiguous_dma(reason="one word per slot, 11 slots"):
                last = dst[PA * TA:E].rearrange("(p t) -> p t", t=TB)[:, TB - 1:TB]
                for t in range(TB, T):
                    sp.dma_start(dst_i[PA:P, t:t + 1], last).then_inc(S["loaded_idx"], 16)
            sp.dma_start(padneg[PA:P, TB:T], negs[:, :]).then_inc(S["filled"], 16)
            sp.wait_ge(S["loaded_idx"], ILOADS * 16)
            sp.dma_start(prev_i[1:P, :], dst_i[0:P - 1, T - 1:T]).then_inc(S["ends_loaded"], 16)
            sp.dma_start(next_i[0:P - 1, :], dst_i[1:P, 0:1]).then_inc(S["ends_loaded"], 16)
            n = 0
            for tile, w in ((WN, W_node), (W0b, W0), (W1b, W1), (W2b, W2)):
                for h in range(2):
                    sp.dma_start(tile[64 * h:64 * h + 64, 64 * h:64 * h + 64], w).then_inc(S["loaded_w"], 16)
                    n += 1
            for tile, w in ((Wn2, W_node), (We2, W_edge)):
                for h in range(2):
                    sp.dma_start(tile[64 * h:64 * h + 64, :], w).then_inc(S["loaded_w"], 16)
                    n += 1
            for j, a in enumerate((a_key, a_query, a_edge)):
                row = a.rearrange("h d -> (h d)").rearrange("(o n) -> o n", o=1)
                sp.dma_start(att_bc[:, j, :], row.to_broadcast([P, D])).then_inc(S["loaded_w"], 16)
                n += 1
            for tile, v in ((bias_bc, bias), (b_bc[0], b0), (b_bc[1], b1), (b_bc[2], b2)):
                sp.dma_start(tile[:, :], v.rearrange("(o n) -> o n", o=1).to_broadcast([P, D])).then_inc(S["loaded_w"], 16)
                n += 1
            with nc.allow_non_contiguous_dma(reason="128 words"):
                for tile, v in ((b0c, b0), (b1c, b1), (b2c, b2)):
                    for h in range(2):
                        sp.dma_start(tile[64 * h:64 * h + 64, :], v.rearrange("(n o) -> n o", o=1)).then_inc(S["loaded_w"], 16)
                        n += 1
            assert n == WLOADS

            def shape(m):
                return (TP, TR) if isinstance(m, int) and m == BLOCKS - 1 else (P, BR)

            def rows(ap, i, np_, r):
                return ap[bass.ds(i * BN, np_ * r), :].rearrange("(p t) f -> p t f", t=r)

            def load_x(m, b, free=None):
                np_, r = shape(m)
                if free is not None:
                    need(S["d_xfree"], free)
                sp.dma_start(dX[0:np_, b, 0:r, :], rows(x, m, np_, r)).then_inc(d_xl[b], 16)

            def store(j_, m, b, buf, ready):
                np_, r = shape(m)
                need(S[ready], m + 1)
                table = out if j_ == 3 else tab_dram[j_]
                sp.dma_start(rows(table, m, np_, r), buf[0:np_, b, 0:r, :]).then_inc(d_st[j_][b % 2], 16)

            def step_loads(j, c):
                if not isinstance(j, int) or 4 * j + c + 3 < BLOCKS:
                    load_x(j * 4 + (c + 3), (c + 3) % 2, free=j * 4 + (c + 2))

            def step_stores(j, c):
                for j_, d, buf, ready in ((0, 1, dX1, "d_x1"), (1, 0, dR1, "d_R1"), (2, -1, dR2, "d_R2"), (3, -2, dO, "d_O")):
                    if not isinstance(j, int) or 0 <= 4 * j + c + d < BLOCKS:
                        store(j_, j * 4 + (c + d), (c + d) % (4 if j_ == 0 else 2), buf, ready)

            def xs_load(m, b, before):
                np_, r = shape(m)
                if not (isinstance(before, int) and before <= 0):
                    need(xm_st[b], before)
                sp.dma_start(XM[0:np_, b, 0:r, 0:D], rows(x, m, np_, r)).then_inc(xm_ld[b], 16)

            def xs_store(m, b, n):
                np_, r = shape(m)
                need(xm_ld[b], n)
                sp.dma_start(rows(xs_dram, m, np_, r), XM[0:np_, b, 0:r, :]).then_inc(xm_st[b], 16)

            def with_xs(j, c):
                two = [(j * 8 + (2 * c + i), (2 * c + i) % 4, j * 2 + c // 2) for i in range(2)]
                for m, b, n in two:
                    xs_load(m, b, before=n * 16)
                step_loads(j, c)
                for m, b, n in two:
                    xs_store(m, b, n * 16 + 16)
                step_stores(j, c)

            for m in range(3):
                load_x(m, m % 2, free=None if m < 2 else 1)
            store(0, 0, 0, dX1, "d_x1")
            for c in range(4):
                with_xs(0, c)
            with sp.Fori(1, 12) as j:
                for c in range(4):
                    with_xs(j, c)
            with_xs(12, 0)
            for c in range(1, 4):
                step_loads(12, c)
                step_stores(12, c)
            with sp.Fori(13, 23) as j:
                for c in range(4):
                    step_loads(j, c)
                    step_stores(j, c)
            for c in range(8):
                step_loads(23, c)
                step_stores(23, c)

            for b in range(R4):
                need(xg_st[b], NB4 * 16)

            ea_a = edge_attr[0:PA * TA, :].rearrange("(p t) f -> p t f", t=TA)
            ea_b = edge_attr[PA * TA:E, :].rearrange("(p t) f -> p t f", t=TB)

            def gat_load(k, b, cb=C, free=None):
                if free is not None:
                    need(S["g_xdfree"], free)
                    need(S["g_tre"], free)
                sp.dma_start(XD[:, b], slots(xd_dram, k)).then_inc(g_in[b], 16)
                sp.dma_start(EA[0:PA, b], ea_a[:, bass.ds(k * C, C), :]).then_inc(g_in[b], 16)
                sp.dma_start(EA[PA:P, b, 0:cb], ea_b[:, bass.ds(k * C, cb), :]).then_inc(g_in[b], 16)

            def gat_store(k, b):
                need(S["g_nrm"], k + 1)
                need(S["g_nr"], 2 * (k + 1))
                sp.dma_start(slots(gat_dram, k), NR[:, b]).then_inc(g_out[0][b], 16)
                need(S["g_x1"], k + 1)
                sp.dma_start(slots(x1_dram, k), X1[:, b]).then_inc(g_out[1][b], 16)
                need(S["g_y0"], k + 1)
                sp.dma_start(tab_slots(0, k), Y0[:, b]).then_inc(g_out[2][b], 16)

            gat_load(0, 0)
            gat_load(1, 1)
            with sp.Fori(0, NB4 - 1) as j:
                for b in range(R4):
                    k = j * R4 + b
                    gat_load(k + 2, b % 2, free=k + 1)
                    gat_store(k, b % 2)
            gat_load(CH - 2, 0, free=CH - 3)
            gat_store(CH - 4, 0)
            gat_load(CH - 1, 1, cb=TB - (CH - 1) * C, free=CH - 2)
            for k in range(CH - 3, CH):
                gat_store(k, k % 2)

            for l in range(3):
                need(S["s_stored"], 32 + 16 * l)

                def load(k, b, free=None):
                    if free is not None:
                        need(S["l_pre"], CH * l + free)
                        if l == 2:
                            need(S["l_u"], free)
                    sp.dma_start(XD[:, b], tab_slots(l, k)).then_inc(l_in[b], 16)
                    if l == 2:
                        sp.dma_start(EA[:, b], slots(x1_dram, k)).then_inc(l_in[b], 16)

                def store(k, b):
                    need(S["l_pre"], CH * l + k + 1)
                    sp.dma_start(slots(pre_dram[l], k), PR[:, b]).then_inc(l_out[0][b], 16)
                    if l < 2:
                        need(S["l_y"], CH * l + k + 1)
                        sp.dma_start(tab_slots(l + 1, k), Y0[:, b]).then_inc(l_out[1][b], 16)

                load(0, 0)
                load(1, 1)
                with sp.Fori(0, NB4 - 1) as j:
                    for b in range(R4):
                        load(j * R4 + b + 2, b % 2, free=j * R4 + b + 1)
                        store(j * R4 + b, b % 2)
                for k in range(CH - 4, CH):
                    if k + 2 < CH:
                        load(k + 2, k % 2, free=k + 1)
                    store(k, k % 2)

            for b in range(2):
                need(d_st[3][b], BLOCKS // 2 * 16)

        @block.gpsimd
        def _(pool):
            pool.wait_ge(S["zeroed"], 1)
            chain = Steps(S["consts_set"])
            chain.on(pool, nc.gpsimd.affine_select(out=ident[:, :], in_=ident[:, :], compare_op=ALU.not_equal, fill=1.0,
                                                   base=0, pattern=[[-1, P]], channel_multiplier=1))
            chain.on(pool, nc.gpsimd.iota(slot_i[:, :], pattern=[[1, T]], base=0, channel_multiplier=T))
            pool.wait_ge(S["loaded_idx"], ILOADS * 16)

            def take_turn():
                nc.gpsimd.sem_inc(S["turn"], 1)

            staged = [0]

            def stage(k, b, source, values):
                if values is not None:
                    nc.gpsimd.tensor_copy(sv[:, b, :], values[:, bass.ds(k * C, C)])
                nc.gpsimd.tensor_copy(ix[:, b, :], source[:, bass.ds(k * C, C)]).then_inc(S["idx_staged"], 1)

            def chunks(source, ready, fire, landed, landed0=0, values=None, peel=1):
                def four(j):
                    for b in range(R4):
                        k = j * R4 + b
                        ready(k, b, j)
                        pool.wait_ge(S["idx_staged"], k + (staged[0] + 1))
                        n = j + (1 if b == R4 - 1 else 0)
                        if not (isinstance(n, int) and n == 0):
                            pool.wait_ge(landed[(b + 1) % R4], n * (16 * C) + landed0)
                        take_turn()
                        stage(k + 1, (b + 1) % R4, source, values)
                        fire(k, b, j)

                if staged[0]:
                    pool.wait_ge(S["idx_staged"], staged[0])
                    take_turn()
                stage(0, 0, source, values)
                turns(pool, NB4, four, peel=peel)
                staged[0] += CH + 1

            def gather(table, buf, b, landed):
                for t in range(C):
                    nc.gpsimd.indirect_dma_start(out=buf[:, b, t, :], out_offset=None, in_=table,
                                                 in_offset=bass.IndirectOffsetOnAxis(ap=ix[:, b, t:t + 1], axis=0)).then_inc(landed, 16)

            def xd_store(k, b, n):
                pool.wait_ge(xg_ld[b], n * 16 * C)
                take_turn()
                nc.gpsimd.dma_start(slots(xd_dram, k), GX[:, b]).then_inc(xg_st[b], 16)

            def xd_ready(k, b, j):
                if not (isinstance(j, int) and j == 0):
                    pool.wait_ge(xg_st[b], j * 16)

            def xd_fire(k, b, j):
                gather(x, GX, b, xg_ld[b])
                if not (isinstance(k, int) and k == 0):
                    xd_store(k - 1, (b - 1) % R4, j + (0 if b == 0 else 1))

            chunks(dst_i, xd_ready, xd_fire, xg_ld)
            xd_store(CH - 1, R4 - 1, NB4)

            pool.wait_ge(S["flags_ready"], 1)
            for b in range(4):
                pool.wait_ge(xm_st[b], (25 if b < 2 else 24) * 16)

            def shift_fire(k, b, j):
                for t in range(C):
                    nc.gpsimd.indirect_dma_start(out=xs_dram, out_offset=bass.IndirectOffsetOnAxis(ap=ix[:, b, t:t + 1], axis=0),
                                                 in_=sv[:, b, t:t + 1], in_offset=None, element_offset=D,
                                                 bounds_check=N - 1, oob_is_err=False).then_inc(mp_st[b], 16)

            chunks(map_i, lambda k, b, j: None, shift_fire, mp_st, values=shiftf)
            for b in range(R4):
                pool.wait_ge(mp_st[b], NB4 * 16 * C)

            def gat_ready(k, b, j):
                if not (isinstance(j, int) and j == 0):
                    pool.wait_ge(S["g_xc"], k - R4 + 1)
                    pool.wait_ge(S["g_shift"], k - R4 + 1)
                    take_turn()

            chunks(src_i, gat_ready, lambda k, b, j: gather(xs_dram, G, b, g_ld[b]), g_ld)

            for b in range(2):
                pool.wait_ge(g_out[0][b], HALF)
            pool.wait_ge(S["seam_set"], 1)
            for table, row in ((gat_dram, grow), (xd_dram, xrow)):
                nc.gpsimd.indirect_dma_start(out=row[:, :], out_offset=None, in_=table,
                                             in_offset=bass.IndirectOffsetOnAxis(ap=i_slot, axis=0)).then_inc(S["s_row"], 16)
            for b in range(2):
                pool.wait_ge(g_out[1][b], HALF)
                pool.wait_ge(g_out[2][b], HALF)
            pool.wait_ge(S["s_out"], 1)
            for table, row, idx in ((x1_dram, x1row, i_slot), (tab_dram[0], yrow, i_row)):
                nc.gpsimd.indirect_dma_start(out=table, out_offset=bass.IndirectOffsetOnAxis(ap=idx, axis=0),
                                             in_=row[:, :], in_offset=None).then_inc(S["s_stored"], 16)
            pool.wait_ge(S["s_stored"], 32)

            def scatter_chunk(k, b, j):
                pool.wait_ge(S["out_idx_staged"], k + 1)
                n = j + (1 if b == R4 - 1 else 0)
                if not (isinstance(n, int) and n == 0):
                    pool.wait_ge(o_st[(b + 1) % R4], n * (16 * C))
                take_turn()
                stage_out(k + 1, (b + 1) % R4)
                pool.wait_ge(S["l_o"], k + 1)
                take_turn()
                for t in range(C):
                    nc.gpsimd.indirect_dma_start(out=out, out_offset=bass.IndirectOffsetOnAxis(ap=ix2[:, b, t:t + 1], axis=0),
                                                 in_=OB[:, b, t, :], in_offset=None,
                                                 bounds_check=N - 1, oob_is_err=False).then_inc(o_st[b], 16)

            def stage_out(k, b):
                nc.gpsimd.tensor_copy(ix2[:, b, :], out_i[:, bass.ds(k * C, C)]).then_inc(S["out_idx_staged"], 1)

            for l in range(3):
                for b in range(2):
                    pool.wait_ge(d_st[l][b], BLOCKS // 2 * 16)
                if l == 2:
                    for b in range(2):
                        pool.wait_ge(d_st[3][b], BLOCKS // 2 * 16)

                def ready(k, b, j):
                    if not (isinstance(j, int) and j == 0):
                        pool.wait_ge(S["l_gfree"], k + (CH * l - R4 + 1))

                def fire(k, b, j):
                    gather(tab_dram[l], GX, b, l_ld[b])
                    if l == 2 and not (isinstance(j, int) and j == 0):
                        scatter_chunk(k - R4, b, j - 1)

                if l == 2:
                    stage_out(0, 0)
                chunks(row_i, ready, fire, l_ld, landed0=l * NB4 * 16 * C, peel=2 if l == 2 else 1)
                if l == 2:
                    for k in range(CH - R4, CH):
                        scatter_chunk(k, k % R4, k // R4)

                for b in range(2):
                    pool.wait_ge(l_out[0][b], (l + 1) * HALF)
                nc.gpsimd.indirect_dma_start(out=prow[:, :], out_offset=None, in_=pre_dram[l],
                                             in_offset=bass.IndirectOffsetOnAxis(ap=i_slot, axis=0)).then_inc(S["s_row"], 16)
                if l < 2:
                    for b in range(2):
                        pool.wait_ge(l_out[1][b], (l + 1) * HALF)
                pool.wait_ge(S["s_out"], l + 2)
                if l < 2:
                    nc.gpsimd.indirect_dma_start(out=tab_dram[l + 1], out_offset=bass.IndirectOffsetOnAxis(ap=i_row, axis=0),
                                                 in_=yrow[:, :], in_offset=None).then_inc(S["s_stored"], 16)
                    pool.wait_ge(S["s_stored"], 48 + 16 * l)
                else:
                    nc.gpsimd.indirect_dma_start(out=out, out_offset=bass.IndirectOffsetOnAxis(ap=i_out, axis=0),
                                                 in_=yrow[:, :], in_offset=None,
                                                 bounds_check=N - 1, oob_is_err=False).then_inc(S["s_stored"], 16)
                    pool.wait_ge(S["s_stored"], 48 + 16 * l)
            for b in range(R4):
                pool.wait_ge(o_st[b], NB4 * 16 * C)

        def repeat(scalar_per_row, n):
            shape = list(scalar_per_row.shape)
            return scalar_per_row.unsqueeze(len(shape)).to_broadcast(shape + [n])

        def over_rows(vec, r, np_=P):
            return vec.unsqueeze(1).to_broadcast([np_, r, D])

        @block.tensor
        def _(pe):
            mm, tr = nc.tensor.matmul, nc.tensor.transpose
            pe.wait_ge(S["consts_set"], 1)

            def pairs_T(dst_ps, rows_sb, signal, np_=P, n=7):
                for q in range(n):
                    last = tr(dst_ps[:, q * P:q * P + np_], rows_sb[0:np_, 2 * q:2 * q + 2, :].rearrange("p t f -> p (t f)"),
                              ident[0:np_, 0:np_])
                last.then_inc(signal, 1)

            pe.wait_ge(S["rows_in"], 1)
            for i in range(4):
                last = tr(SM[0:SW, i * P:(i + 1) * P], bc[:, i, :], ident[:, :])
            last.then_inc(S["rows_T"], 1)

            def chain(n, with_max=False):
                pe.wait_ge(S["chain_in"], n + 1)
                last = tr(SM[0:SW, 0:P], LS[:, :], ident[:, :])
                if with_max:
                    last = tr(SM[0:SW, P:2 * P], LM[:, :], ident[:, :])
                last.then_inc(S["chain_T"], 1)
                pe.wait_ge(S["chain_back_in"], n + 1)
                last = tr(SM[:, 2 * P:2 * P + SW], sC[:, :], ident[0:SW, 0:SW])
                if with_max:
                    last = tr(SM[:, 2 * P + SW:2 * P + 2 * SW], mC[:, :], ident[0:SW, 0:SW])
                last.then_inc(S["chain_back"], 1)

            chain(0)
            pe.wait_ge(S["loaded_w"], WLOADS * 16)

            def shape(m):
                return (TP, TR) if isinstance(m, int) and m == BLOCKS - 1 else (P, BR)

            def cols(a, np_, n):
                return a.rearrange("p (q m) -> p q m", m=P)[:, 0:n, 0:np_]

            def since(sem_, value):
                if not (isinstance(value, int) and value <= 0):
                    pe.wait_ge(sem_, value)

            def dense(j, c):
                s_ = j * 4 + c
                new = not isinstance(s_, int) or s_ < BLOCKS
                old = not isinstance(s_, int) or s_ >= 1
                if new:
                    np_, r = shape(s_)
                    n = r // 2
                    pe.wait_ge(S["d_x1"], s_ + 1)
                    since(S["d_h0"], s_)
                    pairs_T(pT, dX1[:, c % 4], S["d_trx"], np_, n)
                if old:
                    np1, r1 = shape(s_ - 1)
                    n1 = r1 // 2
                    pe.wait_ge(S["d_h1"], s_)
                    since(S["d_h2"], s_ - 1)
                    mm(cols(pM2, np1, n1), lhsT=W1b[:, :], rhs=dh1[:, 0:n1, 0:np1], start=True, stop=True).then_inc(S["d_m2"], 1)
                if new:
                    pe.wait_ge(S["d_h0"], s_ + 1)
                    since(S["d_h1"], s_)
                    mm(cols(pM1, np_, n), lhsT=W0b[:, :], rhs=dh0[:, 0:n, 0:np_], start=True, stop=True).then_inc(S["d_m1"], 1)
                if old:
                    pe.wait_ge(S["d_h2"], s_)
                    since(S["d_h3"], s_ - 1)
                    mm(cols(pM3, np1, n1), lhsT=W2b[:, :], rhs=dh2[:, 0:n1, 0:np1], start=True, stop=True).then_inc(S["d_m3"], 1)
                    since(S["d_R2"], s_ - 1)
                    for q in range(n1):
                        last = tr(pR2[0:np1, q * P:(q + 1) * P], dh2[:, q, 0:np1], ident[:, :])
                    last.then_inc(S["d_r2"], 1)
                if new:
                    pe.wait_ge(S["d_h1"], s_ + 1)
                    since(S["d_R1"], s_)
                    for q in range(n):
                        last = tr(pR1[0:np_, q * P:(q + 1) * P], dh1[:, q, 0:np_], ident[:, :])
                    last.then_inc(S["d_r1"], 1)
                if old:
                    pe.wait_ge(S["d_h3"], s_)
                    since(S["d_u2"], s_ - 1)
                    for q in range(n1):
                        last = tr(pO[0:np1, q * P:(q + 1) * P], dh3[:, q, 0:np1], ident[:, :])
                    last.then_inc(S["d_o"], 1)

            for c in range(4):
                dense(0, c)
            with pe.Fori(1, 23) as j:
                for c in range(4):
                    dense(j, c)
            for c in range(7):
                dense(23, c)

            pe.wait_ge(S["weights_ready"], 1)

            def gat(k, b, j, zero=False):
                b2 = b % 2
                pe.wait_ge(g_in[b2], (j * 2 + b // 2 + 1) * 48)
                if not zero:
                    pe.wait_ge(S["g_evd"], k)
                pairs_T(TRP[1], XD[:, b2], S["g_trd"])
                pe.wait_ge(S["g_xc"], k + 1)
                if not zero:
                    pe.wait_ge(S["g_eve"], k)
                pairs_T(TRP[0], XC[:, b2], S["g_trx"])
                pe.wait_ge(S["g_evx"], k + 1)
                pairs_T(TRP[0], EA[:, b2], S["g_tre"])
                pe.wait_ge(S["g_evd"], k + 1)
                if not zero:
                    pe.wait_ge(S["g_z"], k)
                    pe.wait_ge(S["g_hsfree"], k)
                pe.wait_ge(S["g_eve"], k + 1)
                for q in range(7):
                    for i in range(3):
                        if i == 0:
                            last = mm(hl(q, q + 1)[:, 0, :], lhsT=TS[0][:, b2, q, :], rhs=WM[:, :],
                                      start=True, stop=False, skip_group_check=True)
                        else:
                            last = mm(hl(q, q + 1)[:, 0, 2 * D:PC], lhsT=TS[i][:, b2, q, :], rhs=WA[:, i, :],
                                      start=False, stop=(i == 2), skip_group_check=True)
                last.then_inc(S["g_lg"], 1)

            gat(0, 0, 0, zero=True)
            for b in range(1, R4):
                gat(b, b, 0)
            with pe.Fori(1, NB4) as j:
                for b in range(R4):
                    gat(j * R4 + b, b, j)
            chain(1, with_max=True)

            for l in range(3):
                Wb = (W0b, W1b, W2b)[l]

                def gcn(k, b, k0=False):
                    at = CH * l + k
                    pe.wait_ge(S["l_pre"], at + 1)
                    if not (isinstance(k, int) and at < 2):
                        pe.wait_ge(S["l_ev"], at - 1)
                    pairs_T(TRP[b], PR[:, b], S["l_tr"])
                    pe.wait_ge(S["l_ev"], at + 1)
                    if not (isinstance(k, int) and at < 1):
                        pe.wait_ge(S["l_zfree"], at)
                    for q in range(7):
                        last = mm(HS[:, 2 * q:2 * q + 2, :].rearrange("p t f -> p (t f)"), lhsT=TS[b][:, 0, q, :],
                                  rhs=Wb[:, :], start=True, stop=True)
                    last.then_inc(S["l_z"], 1)

                for k in range(R4):
                    gcn(k, k % 2)
                with pe.Fori(1, NB4) as j:
                    for b in range(R4):
                        gcn(j * R4 + b, b % 2)
                chain(2 + l)
                pe.wait_ge(S["s_mid"], l + 1)
                tr(SM[0:D, 0:P], su[:, :], ident[:, :]).then_inc(S["s_midT"], 1)
                pe.wait_ge(S["s_prT"], l + 1)
                mm(SM[:, 384:384 + D], lhsT=prT[:, :], rhs=Wb[0:D, 0:D], start=True, stop=True).then_inc(S["s_mm"], 1)

        @block.scalar
        def _(act):
            fn = nc.scalar.activation
            act.wait_ge(S["zeroed"], 1)
            act.wait_ge(S["deg_in"], 1)
            fn(dis[:, :], tmpT[:, :], ACT.Sqrt).then_inc(S["deg_sqrt"], 1)
            act.wait_ge(S["loaded_w"], WLOADS * 16)

            def sq1(m, np_=P, r=BR):
                act.wait_ge(S["d_c1"], m + 1)
                fn(dQ1[0:np_, 0:r], dC[0:np_, 0:r], ACT.Square).then_inc(S["d_sq1"], 1)

            def sd1(m, np_=P, r=BR):
                act.wait_ge(S["d_v1"], m + 1)
                fn(dst8[0:np_, 4, 0:r], dst8[0:np_, 5, 0:r], ACT.Sqrt, bias=eps_c[0:np_, :], scale=1.0 / D).then_inc(S["d_sd1"], 1)

            def sq2(m, np_=P, r=BR):
                act.wait_ge(S["d_c2"], m + 1)
                fn(dQ2[0:np_, 0:r], dU[0:np_, 0:r], ACT.Square).then_inc(S["d_sq2"], 1)

            def sd2(m, np_=P, r=BR):
                act.wait_ge(S["d_v2"], m + 1)
                fn(dst8[0:np_, 6, 0:r], dst8[0:np_, 7, 0:r], ACT.Sqrt, bias=eps_c[0:np_, :], scale=1.0 / D).then_inc(S["d_sd2"], 1)

            def since(sem_, value):
                if not (isinstance(value, int) and value <= 0):
                    act.wait_ge(sem_, value)

            def shape(m):
                return (TP, TR) if isinstance(m, int) and m == BLOCKS - 1 else (P, BR)

            def cols(a, np_, n):
                return a.rearrange("p (q m) -> p q m", m=P)[:, 0:n, 0:np_]

            def dense(j, c):
                s_ = j * 4 + c
                known = isinstance(s_, int)
                new = not known or 0 <= s_ < BLOCKS
                old = not known or 1 <= s_ <= BLOCKS
                ln1 = not known or s_ + 1 < BLOCKS
                ln2 = not known or 2 <= s_
                if new:
                    np_, r = shape(s_)
                    n = r // 2
                    act.wait_ge(S["d_trx"], s_ + 1)
                    since(S["d_m1"], s_)
                    fn(dh0[:, 0:n, 0:np_], cols(pT, np_, n), ACT.Copy).then_inc(S["d_h0"], 1)
                if ln2:
                    sq2(s_ - 2, *shape(s_ - 2))
                if old:
                    np1, r1 = shape(s_ - 1)
                    n1 = r1 // 2
                    act.wait_ge(S["d_m2"], s_)
                    since(S["d_r2"], s_ - 1)
                    fn(dh2[:, 0:n1, 0:np1], cols(pM2, np1, n1), ACT.Relu, bias=b1c[:, :]).then_inc(S["d_h2"], 1)
                if ln1:
                    sq1(s_ + 1, *shape(s_ + 1))
                if new:
                    act.wait_ge(S["d_m1"], s_ + 1)
                    since(S["d_m2"], s_)
                    since(S["d_r1"], s_)
                    fn(dh1[:, 0:n, 0:np_], cols(pM1, np_, n), ACT.Relu, bias=b0c[:, :]).then_inc(S["d_h1"], 1)
                if ln2:
                    sd2(s_ - 2, *shape(s_ - 2))
                if old:
                    act.wait_ge(S["d_m3"], s_)
                    since(S["d_o"], s_ - 1)
                    fn(dh3[:, 0:n1, 0:np1], cols(pM3, np1, n1), ACT.Relu, bias=b2c[:, :]).then_inc(S["d_h3"], 1)
                if ln1:
                    sd1(s_ + 1, *shape(s_ + 1))
                if old:
                    act.wait_ge(S["d_r2"], s_)
                    since(d_st[2][(c - 1) % 2], (j * 2 + (c - 1) // 2) * 16)
                    fn(dR2[0:np1, (c - 1) % 2, 0:r1].rearrange("p t f -> p (t f)"), pR2[0:np1, 0:n1 * P],
                       ACT.Copy).then_inc(S["d_R2"], 1)
                if new:
                    act.wait_ge(S["d_r1"], s_ + 1)
                    since(d_st[1][c % 2], (j * 2 + c // 2) * 16)
                    fn(dR1[0:np_, c % 2, 0:r].rearrange("p t f -> p (t f)"), pR1[0:np_, 0:n * P],
                       ACT.Copy).then_inc(S["d_R1"], 1)

            sq1(0)
            sd1(0)
            for c in range(4):
                dense(0, c)
            with act.Fori(1, 23) as j:
                for c in range(4):
                    dense(j, c)
            for c in range(8):
                dense(23, c)
            for b in range(2):
                act.wait_ge(d_st[1][b], BLOCKS // 2 * 16)

            def evac(k, b, j):
                act.wait_ge(g_ld[b], (j + 1) * 16 * C)
                if not (isinstance(k, int) and k < 2):
                    act.wait_ge(S["g_trx"], k - 1)
                fn(XC[:, b % 2], G[:, b, :, 0:D], ACT.Copy).then_inc(S["g_xc"], 1)
                for i, ready, bank, done in ((1, "g_trd", 1, "g_evd"), (0, "g_trx", 0, "g_evx"), (2, "g_tre", 0, "g_eve")):
                    act.wait_ge(S[ready], k + 1)
                    if not (isinstance(k, int) and k < 2):
                        act.wait_ge(S["g_lg"], k - 1)
                    fn(TS[i][:, b % 2].rearrange("p q m -> p (q m)"), TRP[bank], ACT.Copy).then_inc(S[done], 1)

            def deviation(k):
                act.wait_ge(S["g_v"], k + 1)
                fn(est[:, 3, :], est[:, 2, :], ACT.Sqrt, bias=eps_c[:, :], scale=1.0 / D).then_inc(S["g_sd"], 1)

            def gat(k, b, j, last=False):
                b2, half = b % 2, j * 2 + b // 2
                act.wait_ge(S["g_de"], k + 1)
                fn(RX[:, :, :], DE[:, :, :], ACT.Exp).then_inc(S["g_ex"], 1)
                act.wait_ge(S["g_ex"], k + 1)
                fn(AB[:, 0:D, 1:C1].rearrange("p (h d) t -> p h d t", d=HD),
                   RX[:, 0:H, :].unsqueeze(2).to_broadcast([P, H, HD, C]), ACT.Copy).then_inc(S["g_ab"], 1)
                fn(AB[:, D:SW, 1:C1], RX[:, 0:H, :], ACT.Copy).then_inc(S["g_ab"], 1)
                fn(B[:, D:SW, 1:C1], RX[:, H:2 * H, :], ACT.Copy).then_inc(S["g_ab"], 1)
                if not (isinstance(k, int) and k == 0):
                    deviation(k - 1)
                if not last:
                    evac(k + 1, (b + 1) % R4, j + (1 if b == R4 - 1 else 0))
                act.wait_ge(S["g_S"], k + 1)
                act.wait_ge(g_out[0][b2], half * 16)
                fn(NR[:, b2, :, D:SW], SS[:, b2, D:SW, 1:C1].rearrange("p h t -> p t h"), ACT.Copy).then_inc(S["g_nr"], 1)
                fn(NR[:, b2, :, SW:GW], M[:, b2, :, 1:C1].rearrange("p h t -> p t h"), ACT.Copy).then_inc(S["g_nr"], 1)
                act.wait_ge(S["g_c"], k + 1)
                fn(Q[:, :, :], U[:, :, :], ACT.Square).then_inc(S["g_q"], 1)

            evac(0, 0, 0)
            for b in range(R4):
                gat(b, b, 0)
            with act.Fori(1, NB4 - 1) as j:
                for b in range(R4):
                    gat(j * R4 + b, b, j)
            for k in range(CH - R4, CH):
                gat(k, k % R4, k // R4, last=(k == CH - 1))
            deviation(CH - 1)

            def seam_exp(n, *tiles):
                act.wait_ge(S["s_ex_in"], n)
                for t in tiles:
                    fn(t, t, ACT.Exp).then_inc(S["s_ex"], 1)

            def seam_norm(n):
                act.wait_ge(S["s_c"], n)
                fn(sq[:, :], su[:, :], ACT.Square).then_inc(S["s_q"], 1)
                act.wait_ge(S["s_v"], n)
                fn(sst[:, 3:4], sst[:, 2:3], ACT.Sqrt, bias=eps_c[:, :], scale=1.0 / D).then_inc(S["s_sd"], 1)

            seam_exp(1, rE[:, :], bE[:, :])
            seam_exp(2, wS[:, :], wC[:, :])
            seam_norm(1)

            for l in range(3):
                def flags(k, b):
                    at = CH * l + k
                    if not (isinstance(k, int) and at < 2):
                        act.wait_ge(S["l_scan"], at - 1)
                    nc.scalar.sem_inc(S["turn"], 1)
                    fn(AS[:, b, :, 1:C1], same[:, bass.ds(k * C, C)].unsqueeze(1).to_broadcast([P, D, C]),
                       ACT.Copy).then_inc(S["l_as"], 1)

                def gcn(k, b, norm, more=True):
                    at = CH * l + k
                    act.wait_ge(S["l_tr"], at + 1)
                    if not (isinstance(k, int) and at < 2):
                        act.wait_ge(S["l_z"], at - 1)
                    fn(TS[b][:, 0].rearrange("p q m -> p (q m)"), TRP[b], ACT.Copy).then_inc(S["l_ev"], 1)
                    if more:
                        flags(k + 2, b)
                    if norm:
                        norm_of(k - 1)

                def norm_of(k):
                    act.wait_ge(S["l_c"], k + 1)
                    fn(Q[:, :, :], U[:, :, :], ACT.Square).then_inc(S["l_q"], 1)
                    act.wait_ge(S["l_v"], k + 1)
                    fn(est[:, 3, :], est[:, 2, :], ACT.Sqrt, bias=eps_c[:, :], scale=1.0 / D).then_inc(S["l_sd"], 1)

                flags(0, 0)
                flags(1, 1)
                for k in range(R4):
                    gcn(k, k % 2, l == 2 and k > 0)
                with act.Fori(1, NB4 - 1) as j:
                    for b in range(R4):
                        gcn(j * R4 + b, b % 2, l == 2)
                for k in range(CH - R4, CH):
                    gcn(k, k % 2, l == 2, more=k + 2 < CH)
                if l == 2:
                    norm_of(CH - 1)
            seam_norm(2)

        @block.vector
        def _(dve):
            v = nc.vector
            tt, ts, stt = v.tensor_tensor, v.tensor_scalar, v.scalar_tensor_tensor
            step = Steps(S["vector_step"])

            def do(instruction):
                step.on(dve, instruction)

            for tile, value in ((ident, 0.0), (src_i, 0), (ew, 0.0), (padneg, 0.0), (negs, -BIG), (prev_i, -1), (next_i, -1),
                                (WM, 0.0), (W0b, 0.0), (W1b, 0.0), (W2b, 0.0), (eps_c, EPS), (LS, 0.0), (dst_i, 0)):
                v.memset(tile[:, :], value)
            v.memset(WA[:, :, :], 0.0)
            v.memset(XM[:, :, :, D:XW], 0.0)
            v.memset(AM[:, :, 0:1], -BIG)
            v.memset(AB[:, :, 0:1], 0.0)
            for tile in (shiftf, map_i, out_i, row_i):
                v.memset(tile[:, T:TX], 0)
            v.memset(M[:, 1], -BIG)
            v.memset(SS[:, 1], 0.0)
            v.memset(mC[:, 0:1], -BIG)
            v.memset(rE[:, 0:1], -BIG)
            v.memset(sC[:, 0:1], 0.0).then_inc(S["zeroed"], 1)
            dve.wait_ge(S["zeroed"], 1)

            dve.wait_ge(S["loaded_idx"], ILOADS * 16)
            dve.wait_ge(S["ends_loaded"], 32)
            dve.wait_ge(S["consts_set"], 2)
            dve.wait_ge(S["filled"], 16)
            v.tensor_copy(dstf[:, :], dst_i[:, 0:T])
            v.tensor_copy(srcf[:, :], src_i[:, 0:T])
            v.tensor_copy(slotf[:, :], slot_i[:, :])
            v.tensor_copy(c_prev, prev_i[:, :])
            v.memset(same[:, 0:1], 0.0)
            do(v.tensor_copy(c_next, next_i[:, :]))
            tt(same[:, 1:T], dstf[:, 1:T], dstf[:, 0:T - 1], ALU.is_equal)
            tt(isend[:, 0:T - 1], dstf[:, 1:T], dstf[:, 0:T - 1], ALU.not_equal)
            tt(isend[:, T - 1:T], dstf[:, T - 1:T], c_next, ALU.not_equal)
            ts(first[:, :], dstf[:, :], dstf[:, 0:1], None, ALU.is_equal)
            tt(c_cont, dstf[:, 0:1], c_prev, ALU.is_equal)
            do(tt(c_whole, dstf[:, 0:1], dstf[:, T - 1:T], ALU.is_equal))
            ts(breakf[:, :], same[:, :], BIG, -BIG, ALU.mult, ALU.add)
            tt(c_run, c_whole, c_cont, ALU.mult)
            v.tensor_reduce(c_t1, first[:, :], axis=AX.X, op=ALU.add)
            tt(shiftf[:, 0:T], slotf[:, :], dstf[:, :], ALU.subtract)
            do(ts(tmpT[:, :], isend[:, :], -SKIP, SKIP, ALU.mult, ALU.add))
            ts(shiftf[:, 0:T], shiftf[:, 0:T], float(SLOT0), None, ALU.add)
            tt(map_i[:, 0:T], tmpT[:, :], dstf[:, :], ALU.add)
            tt(c_slot, slotf[:, 0:1], c_t1, ALU.add)
            do(tt(onehot[:, :], isend[:, :], first[:, :], ALU.mult))
            tt(onehot[:, :], isend[:, :], onehot[:, :], ALU.subtract)
            do(ts(c_slot, c_slot, -1.0, None, ALU.add))
            do(ts(tmpT[:, :], onehot[:, :], -SKIP, SKIP, ALU.mult, ALU.add))
            tt(out_i[:, 0:T], tmpT[:, :], dstf[:, :], ALU.add)
            v.tensor_copy(i_slot, c_slot)
            ts(i_row, c_slot, float(SLOT0), None, ALU.add)
            do(ts(onehot[:, :], slotf[:, :], c_slot, None, ALU.is_equal))
            do(tt(tmpT[:, :], onehot[:, :], isend[:, :], ALU.mult))
            do(v.tensor_reduce(c_end, tmpT[:, :], axis=AX.X, op=ALU.add))
            do(ts(c_tmp, c_end, -SKIP, SKIP, ALU.mult, ALU.add))
            tt(i_out, c_tmp, dstf[:, 0:1], ALU.add).then_inc(S["flags_ready"], 1)

            wide = [P, SW]
            v.tensor_copy(bc[:, 0, :], c_run.to_broadcast(wide))
            v.tensor_copy(bc[:, 1, :], c_cont.to_broadcast(wide))
            ts(bc[:, 2, :], c_run.to_broadcast(wide), BIG, -BIG, ALU.mult, ALU.add)
            ts(bc[:, 3, :], c_cont.to_broadcast(wide), BIG, -BIG, ALU.mult, ALU.add).then_inc(S["rows_in"], 1)
            dve.wait_ge(S["rows_T"], 1)
            for i, r in enumerate((run_r, cont_r, nrun_r, ncont_r)):
                last = v.tensor_copy(r[:, :], SM[0:SW, i * P:(i + 1) * P])
            do(last)

            def carry_sums(n):
                dve.wait_ge(S["chain_T"], n + 1)
                do(v.tensor_tensor_scan(sE[:, :], run_r[:, :], SM[0:SW, 0:P], 0.0, ALU.mult, ALU.add))
                tt(sC[:, 1:P], sE[:, 0:P - 1], cont_r[:, 1:P], ALU.mult).then_inc(S["chain_back_in"], 1)
                dve.wait_ge(S["chain_back"], n + 1)

            do(v.tensor_tensor_scan(deg[:, :], same[:, :], ew[:, :], 0.0, ALU.mult, ALU.add))
            v.tensor_copy(LS[:, :], deg[:, T - 1:T].to_broadcast(wide)).then_inc(S["chain_in"], 1)
            carry_sums(0)
            do(v.tensor_copy(c_tmp, SM[:, 2 * P:2 * P + 1]))
            do(stt(out=deg[:, :], in0=first[:, :], scalar=c_tmp, in1=deg[:, :], op0=ALU.mult, op1=ALU.add))
            do(ts(deg[:, :], deg[:, :], 1.0, None, ALU.add))
            ts(tmpT[:, :], deg[:, :], 1e-30, None, ALU.max).then_inc(S["deg_in"], 1)
            do(ts(deg[:, :], deg[:, :], 0.0, None, ALU.is_gt))
            dve.wait_ge(S["deg_sqrt"], 1)
            do(v.reciprocal(dis[:, :], dis[:, :]))
            do(tt(dis[:, :], dis[:, :], deg[:, :], ALU.mult))
            do(tt(tmpT[:, :], onehot[:, :], dis[:, :], ALU.mult))
            v.tensor_reduce(c_dis, tmpT[:, :], axis=AX.X, op=ALU.add).then_inc(S["seam_set"], 1)
            dve.wait_ge(S["seam_set"], 1)

            dve.wait_ge(S["loaded_w"], WLOADS * 16)
            for i, w in enumerate((Wn2, Wn2, We2)):
                last = tt(wprod[:, i, :], w[:, :], att_bc[:, i, :], ALU.mult)
            do(last)
            do(v.tensor_reduce(wred[:, :, :], wprod[:, :, :].rearrange("p i (h d) -> p i h d", d=HD), axis=AX.X, op=ALU.add))
            for s_ in range(2):
                half_ = slice(64 * s_, 64 * s_ + 64)
                v.tensor_copy(WA[half_, :, H * s_:H * s_ + H], wred[half_, :, :])
                last = v.tensor_copy(WM[half_, 2 * D + H * s_:2 * D + H * s_ + H], wred[half_, 0, :])
            last.then_inc(S["weights_ready"], 1)

            def center(u, st, i_sum, i_mean, r, np_):
                do(v.tensor_reduce(st[0:np_, i_sum, 0:r], u, axis=AX.X, op=ALU.add))
                do(ts(st[0:np_, i_mean, 0:r], st[0:np_, i_sum, 0:r], -1.0 / D, None, ALU.mult))
                return tt(u, u, repeat(st[0:np_, i_mean, 0:r], D), ALU.add)

            def since(sem_, value):
                if not (isinstance(value, int) and value <= 0):
                    dve.wait_ge(sem_, value)

            def shape(m):
                return (TP, TR) if isinstance(m, int) and m == BLOCKS - 1 else (P, BR)

            def norms(j, c):
                s_ = j * 4 + c
                known = isinstance(s_, int)
                ln1 = not known or s_ + 1 < BLOCKS
                ln2 = not known or s_ >= 2
                m1, h1, b1_ = s_ + 1, j * 2 + (c + 1) // 2, (c + 1) % 2
                m2, h2, b2_ = s_ - 2, j * 2 + (c - 2) // 2, c % 2
                (n1, r1), (n2, r2) = shape(m1), shape(m2)
                if ln2:
                    dve.wait_ge(S["d_o"], m2 + 1)
                    since(S["d_O"], m2)
                    u = dU[0:n2, 0:r2]
                    tt(u, pO[0:n2, 0:r2 * D].rearrange("p (t f) -> p t f", f=D), dX1[0:n2, (c + 2) % 4, 0:r2],
                       ALU.add).then_inc(S["d_u2"], 1)
                    dve.wait_ge(S["d_u2"], m2 + 1)
                    center(u, dst8, 2, 3, r2, n2).then_inc(S["d_c2"], 1)
                if ln1:
                    dve.wait_ge(d_xl[b1_], h1 * 16 + 16)
                    since(S["d_x1"], m1)
                    c_ = dC[0:n1, 0:r1]
                    stt(out=c_, in0=dX[0:n1, b1_, 0:r1], scalar=2.0, in1=over_rows(bias_bc[0:n1, :], r1, n1), op0=ALU.mult,
                        op1=ALU.add).then_inc(S["d_xfree"], 1)
                    dve.wait_ge(S["d_xfree"], m1 + 1)
                    center(c_, dst8, 0, 1, r1, n1).then_inc(S["d_c1"], 1)
                if ln2:
                    dve.wait_ge(S["d_sq2"], m2 + 1)
                    v.tensor_reduce(dst8[0:n2, 7, 0:r2], dQ2[0:n2, 0:r2], axis=AX.X, op=ALU.add).then_inc(S["d_v2"], 1)
                if ln1:
                    dve.wait_ge(S["d_sq1"], m1 + 1)
                    v.tensor_reduce(dst8[0:n1, 5, 0:r1], dQ1[0:n1, 0:r1], axis=AX.X, op=ALU.add).then_inc(S["d_v1"], 1)
                if ln2:
                    dve.wait_ge(S["d_sd2"], m2 + 1)
                    do(v.reciprocal(dst8[0:n2, 6, 0:r2], dst8[0:n2, 6, 0:r2]))
                    since(d_st[3][b2_], h2 * 16)
                    tt(dO[0:n2, b2_, 0:r2], u, repeat(dst8[0:n2, 6, 0:r2], D), ALU.mult).then_inc(S["d_O"], 1)
                if ln1:
                    dve.wait_ge(S["d_sd1"], m1 + 1)
                    do(v.reciprocal(dst8[0:n1, 4, 0:r1], dst8[0:n1, 4, 0:r1]))
                    since(d_st[0][b1_], h1 * 16)
                    since(S["d_trx"], m1 - 3)
                    tt(dX1[0:n1, (c + 1) % 4, 0:r1], c_, repeat(dst8[0:n1, 4, 0:r1], D), ALU.mult).then_inc(S["d_x1"], 1)

            norms(0, -1)
            for c in range(4):
                norms(0, c)
            with dve.Fori(1, 23) as j:
                step.enter(j - 1, 24)
                for c in range(4):
                    norms(j, c)
                step.leave(22)
            for c in range(8):
                norms(23, c)
            for j_ in range(4):
                for b in range(2):
                    dve.wait_ge(d_st[j_][b], BLOCKS // 2 * 16)
            do(v.memset(AS[:, :, :, 0:1], 0.0))

            def norm_rows(k, c_sem, q_sem, v_sem, sd_sem):
                center(U[:, :, :], est, 0, 1, C, P).then_inc(S[c_sem], 1)
                dve.wait_ge(S[q_sem], k + 1)
                v.tensor_reduce(est[:, 2, :], Q[:, :, :], axis=AX.X, op=ALU.add).then_inc(S[v_sem], 1)
                dve.wait_ge(S[sd_sem], k + 1)
                do(v.reciprocal(est[:, 3, :], est[:, 3, :]))

            def variance(k):
                dve.wait_ge(S["g_q"], k + 1)
                v.tensor_reduce(est[:, 2, :], Q[:, :, :], axis=AX.X, op=ALU.add).then_inc(S["g_v"], 1)

            def normed(k, b2, half):
                dve.wait_ge(S["g_sd"], k + 1)
                do(v.reciprocal(est[:, 3, :], est[:, 3, :]))
                since(g_out[1][b2], half * 16)
                tt(X1[:, b2], U[:, :, :], repeat(est[:, 3, :], D), ALU.mult).then_inc(S["g_x1"], 1)
                dve.wait_ge(S["g_x1"], k + 1)
                since(g_out[2][b2], half * 16)
                tt(Y0[:, b2], X1[:, b2], repeat(dis[:, bass.ds(k * C, C)], D), ALU.mult).then_inc(S["g_y0"], 1)

            def gat(k, b, j):
                b2, half, cs = b % 2, j * 2 + b // 2, bass.ds(k * C, C)
                before = not (isinstance(k, int) and k == 0)
                dve.wait_ge(g_ld[b], (j + 1) * 16 * C)
                tt(row_i[:, cs], srcf[:, cs], G[:, b, :, D], ALU.add).then_inc(S["g_shift"], 1)
                do(v.tensor_copy(AM[:, :, 1:C1], breakf[:, cs].unsqueeze(1).to_broadcast([P, H, C])))
                v.tensor_copy(LB[:, :, 0], M[:, 1 - b2, :, C])
                dve.wait_ge(S["g_lg"], k + 1)
                for q0, q1 in ((0, 3), (3, 6), (6, 7)):
                    last = tt(Z[:, 2 * q0:2 * q1, :].rearrange("p (q s) h -> p q s h", s=2),
                              hl(q0, q1)[:, :, 2 * D:PC].rearrange("p q (s h) -> p q s h", h=H),
                              repeat(padneg[:, bass.ds(k * C + 2 * q0, 2 * (q1 - q0))].rearrange("p (q s) -> p q s", s=2), H), ALU.add)
                last.then_inc(S["g_z"], 1)
                dve.wait_ge(S["g_z"], k + 1)
                do(stt(out=LB[:, :, 1:C1].rearrange("p h t -> p t h"), in0=Z[:, :, :], scalar=0.01, in1=Z[:, :, :],
                       op0=ALU.mult, op1=ALU.max))
                do(v.tensor_tensor_scan(M[:, b2].rearrange("p h t -> p (h t)"), AM[:, :, :].rearrange("p h t -> p (h t)"),
                                        LB[:, :, :].rearrange("p h t -> p (h t)"), 0.0, ALU.add, ALU.max))
                tt(DE[:, H:2 * H, :], LB[:, :, 1:C1], M[:, b2, :, 1:C1], ALU.subtract)
                do(tt(DE[:, 0:H, :], M[:, b2, :, 0:C], M[:, b2, :, 1:C1], ALU.subtract))
                tt(DE[:, 0:H, :], DE[:, 0:H, :], AM[:, :, 1:C1], ALU.add).then_inc(S["g_de"], 1)
                v.tensor_copy(B[:, :, 0], SS[:, 1 - b2, :, C])
                if before:
                    variance(k - 1)
                dve.wait_ge(S["g_ex"], k + 1)
                for q0, q1 in ((0, 3), (3, 6), (6, 7)):
                    t0, t1 = 2 * q0, 2 * q1
                    for s_ in range(2):
                        last = tt(B[:, 0:D, 1 + t0 + s_:1 + t1:2].rearrange("p (h d) q -> p q h d", d=HD),
                                  hl(q0, q1)[:, :, D * s_:D * s_ + D].rearrange("p q (h d) -> p q h d", d=HD),
                                  RX[:, H:2 * H, t0 + s_:t1:2].rearrange("p h q -> p q h").unsqueeze(3).to_broadcast([P, q1 - q0, H, HD]),
                                  ALU.mult)
                last.then_inc(S["g_hsfree"], 1)
                dve.wait_ge(S["g_hsfree"], k + 1)
                dve.wait_ge(S["g_ab"], k * 3 + 3)
                v.tensor_tensor_scan(SS[:, b2].rearrange("p f t -> p (f t)"), AB[:, :, :].rearrange("p f t -> p (f t)"),
                                     B[:, :, :].rearrange("p f t -> p (f t)"), 0.0, ALU.mult, ALU.add).then_inc(S["g_S"], 1)
                if before:
                    b_ = (b - 1) % R4
                    normed(k - 1, b_ % 2, j * 2 + (b - 1) // 2)
                dve.wait_ge(S["g_S"], k + 1)
                do(v.reciprocal(RD[:, :, :], SS[:, b2, D:SW, 1:C1]))
                since(g_out[0][b2], half * 16)
                tt(NR[:, b2, :, 0:D].rearrange("p t (h d) -> p h d t", d=HD),
                   SS[:, b2, 0:D, 1:C1].rearrange("p (h d) t -> p h d t", d=HD),
                   RD[:, :, :].unsqueeze(2).to_broadcast([P, H, HD, C]), ALU.mult).then_inc(S["g_nrm"], 1)
                if before:
                    dve.wait_ge(S["g_x1"], k)
                dve.wait_ge(g_in[b2], half * 48 + 48)
                stt(out=U[:, :, :], in0=XD[:, b2], scalar=2.0, in1=over_rows(bias_bc[:, :], C), op0=ALU.mult,
                    op1=ALU.add).then_inc(S["g_xdfree"], 1)
                dve.wait_ge(S["g_xdfree"], k + 1)
                dve.wait_ge(S["g_nrm"], k + 1)
                do(tt(U[:, :, :], U[:, :, :], NR[:, b2, :, 0:D], ALU.add))
                center(U[:, :, :], est, 0, 1, C, P).then_inc(S["g_c"], 1)

            def gat_four(j):
                for b in range(R4):
                    gat(j * R4 + b, b, j)

            turns(dve, NB4, gat_four, step, 9 * R4)
            variance(CH - 1)
            normed(CH - 1, 1, CH // 2 - 1)

            def heads(ap4, n=HD):
                return ap4.unsqueeze(2).to_broadcast([P, H, n])

            def by_head(ap64):
                return ap64.rearrange("p (h d) -> p h d", d=HD)

            def seam_norm(n):
                do(v.tensor_reduce(sst[:, 0:1], su[:, :], axis=AX.X, op=ALU.add))
                do(ts(sst[:, 1:2], sst[:, 0:1], -1.0 / D, None, ALU.mult))
                ts(su[:, :], su[:, :], sst[:, 1:2], None, ALU.add).then_inc(S["s_c"], 1)
                dve.wait_ge(S["s_q"], n)
                v.tensor_reduce(sst[:, 2:3], sq[:, :], axis=AX.X, op=ALU.add).then_inc(S["s_v"], 1)
                dve.wait_ge(S["s_sd"], n)
                do(v.reciprocal(sst[:, 3:4], sst[:, 3:4]))

            v.tensor_copy(LS[:, :], SS[:, 1, :, C])
            v.tensor_copy(by_head(LM[:, 0:D]), heads(M[:, 1, :, C]))
            v.tensor_copy(LM[:, D:SW], M[:, 1, :, C]).then_inc(S["chain_in"], 1)
            dve.wait_ge(S["chain_T"], 2)
            do(v.tensor_tensor_scan(mE[:, :], nrun_r[:, :], SM[0:SW, P:2 * P], -BIG, ALU.add, ALU.max))
            tt(bE[:, :], SM[0:SW, P:2 * P], mE[:, :], ALU.subtract)
            tt(mC[:, 1:P], mE[:, 0:P - 1], ncont_r[:, 1:P], ALU.add)
            do(tt(rE[:, 1:P], mE[:, 0:P - 1], mE[:, 1:P], ALU.subtract))
            tt(rE[:, 1:P], rE[:, 1:P], nrun_r[:, 1:P], ALU.add).then_inc(S["s_ex_in"], 1)
            dve.wait_ge(S["s_ex"], 2)
            do(tt(bE[:, :], SM[0:SW, 0:P], bE[:, :], ALU.mult))
            do(v.tensor_tensor_scan(sE[:, :], rE[:, :], bE[:, :], 0.0, ALU.mult, ALU.add))
            tt(sC[:, 1:P], sE[:, 0:P - 1], cont_r[:, 1:P], ALU.mult).then_inc(S["chain_back_in"], 1)
            dve.wait_ge(S["s_row"], 32)
            tt(by_head(S68[:, 0:D]), by_head(grow[:, 0:D]), heads(grow[:, D:SW]), ALU.mult)
            v.tensor_copy(S68[:, D:SW], grow[:, D:SW])
            v.tensor_copy(by_head(M68[:, 0:D]), heads(grow[:, SW:GW]))
            do(v.tensor_copy(M68[:, D:SW], grow[:, SW:GW]))
            dve.wait_ge(S["chain_back"], 2)
            carS, carM = SM[:, 2 * P:2 * P + SW], SM[:, 2 * P + SW:2 * P + 2 * SW]
            do(tt(MM[:, :], M68[:, :], carM, ALU.max))
            tt(wS[:, :], M68[:, :], MM[:, :], ALU.subtract)
            tt(wC[:, :], carM, MM[:, :], ALU.subtract).then_inc(S["s_ex_in"], 1)
            dve.wait_ge(S["s_ex"], 4)
            tt(S68[:, :], S68[:, :], wS[:, :], ALU.mult)
            do(tt(wC[:, :], carS, wC[:, :], ALU.mult))
            do(tt(S68[:, :], S68[:, :], wC[:, :], ALU.add))
            do(v.reciprocal(sden[:, :], S68[:, D:SW]))
            do(tt(by_head(su[:, :]), by_head(S68[:, 0:D]), heads(sden[:, :]), ALU.mult))
            do(stt(out=su[:, :], in0=xrow[:, :], scalar=2.0, in1=su[:, :], op0=ALU.mult, op1=ALU.add))
            do(tt(su[:, :], su[:, :], bias_bc[:, :], ALU.add))
            seam_norm(1)
            do(ts(x1row[:, :], su[:, :], sst[:, 3:4], None, ALU.mult))
            ts(yrow[:, :], x1row[:, :], c_dis, None, ALU.mult).then_inc(S["s_out"], 1)

            for l in range(3):
                def sums(k, b, j):
                    b2, half, cs, at = b % 2, j * 2 + b // 2, bass.ds(k * C, C), CH * l + k
                    dve.wait_ge(l_ld[b], (j + (1 + l * NB4)) * 16 * C)
                    v.tensor_copy(B[:, 0:D, 0], SS[:, 1 - b2, 0:D, C])
                    tt(B[:, 0:D, 1:C1].rearrange("p f t -> p t f"), GX[:, b], repeat(ew[:, cs], D), ALU.mult).then_inc(S["l_gfree"], 1)
                    dve.wait_ge(S["l_gfree"], at + 1)
                    dve.wait_ge(S["l_as"], at + 1)
                    v.tensor_tensor_scan(SS[:, b2, 0:D].rearrange("p f t -> p (f t)"), AS[:, b2].rearrange("p f t -> p (f t)"),
                                         B[:, 0:D].rearrange("p f t -> p (f t)"), 0.0, ALU.mult, ALU.add).then_inc(S["l_scan"], 1)
                    dve.wait_ge(S["l_scan"], at + 1)
                    dve.wait_ge(l_in[b2], l * HALF + (half + 1) * (32 if l == 2 else 16))
                    dve.wait_ge(l_out[0][b2], l * HALF + half * 16)
                    if not (isinstance(k, int) and at < 2):
                        dve.wait_ge(S["l_tr"], at - 1)
                    tt(PR[:, b2], SS[:, b2, 0:D, 1:C1].rearrange("p f t -> p t f"), XD[:, b2], ALU.add).then_inc(S["l_pre"], 1)

                def rows_of(k, b, j):
                    b2, half, cs, at = b % 2, j * 2 + b // 2, bass.ds(k * C, C), CH * l + k
                    if not (isinstance(k, int) and k == 0):
                        dve.wait_ge(S["l_y"] if l < 2 else S["l_o"], at if l < 2 else k)
                    dve.wait_ge(S["l_z"], at + 1)
                    tt(U[:, :, :], HS, repeat(dis[:, cs], D), ALU.mult).then_inc(S["l_zfree"], 1)
                    dve.wait_ge(S["l_zfree"], at + 1)
                    do(tt(U[:, :, :], U[:, :, :], over_rows(b_bc[l][:, :], C), ALU.add))
                    if l < 2:
                        dve.wait_ge(l_out[1][b2], l * HALF + half * 16)
                        stt(out=Y0[:, b2], in0=U[:, :, :], scalar=0.0, in1=repeat(dis[:, cs], D), op0=ALU.max,
                            op1=ALU.mult).then_inc(S["l_y"], 1)
                    else:
                        stt(out=U[:, :, :], in0=U[:, :, :], scalar=0.0, in1=EA[:, b2], op0=ALU.max,
                            op1=ALU.add).then_inc(S["l_u"], 1)
                        dve.wait_ge(S["l_u"], k + 1)
                        norm_rows(k, "l_c", "l_q", "l_v", "l_sd")
                        dve.wait_ge(o_st[b], j * 16 * C)
                        tt(OB[:, b], U[:, :, :], repeat(est[:, 3, :], D), ALU.mult).then_inc(S["l_o"], 1)

                each = 1 if l < 2 else 4
                sums(0, 0, 0)

                def gcn_four(j):
                    for b in range(R4):
                        sums(j * R4 + (b + 1), (b + 1) % R4, j + (1 if b == R4 - 1 else 0))
                        rows_of(j * R4 + b, b, j)

                turns(dve, NB4 - 1, gcn_four, step, each * R4)
                for k in range(CH - R4, CH):
                    if k + 1 < CH:
                        sums(k + 1, (k + 1) % R4, (k + 1) // R4)
                    rows_of(k, k % R4, k // R4)

                v.tensor_copy(LS[:, 0:D], SS[:, 1, 0:D, C]).then_inc(S["chain_in"], 1)
                carry_sums(2 + l)
                dve.wait_ge(S["s_row"], 48 + 16 * l)
                tt(su[:, :], prow[:, :], SM[:, 2 * P:2 * P + D], ALU.add).then_inc(S["s_mid"], 1)
                dve.wait_ge(S["s_midT"], l + 1)
                v.tensor_copy(prT[:, :], SM[0:D, 0:P]).then_inc(S["s_prT"], 1)
                dve.wait_ge(S["s_mm"], l + 1)
                do(ts(su[:, :], SM[:, 384:384 + D], c_dis, None, ALU.mult))
                do(tt(su[:, :], su[:, :], b_bc[l][:, :], ALU.add))
                dve.wait_ge(S["s_stored"], 32 + 16 * l)
                if l < 2:
                    ts(yrow[:, :], su[:, :], 0.0, c_dis, ALU.max, ALU.mult).then_inc(S["s_out"], 1)
                else:
                    do(stt(out=su[:, :], in0=su[:, :], scalar=0.0, in1=x1row[:, :], op0=ALU.max, op1=ALU.add))
                    seam_norm(2)
                    ts(yrow[:, :], su[:, :], sst[:, 3:4], None, ALU.mult).then_inc(S["s_out"], 1)


_INS = ["x", "src", "dst", "edge_attr_64", "edge_weight", "L0_gnn_W_node", "L0_gnn_W_edge", "L0_gnn_attn_query",
        "L0_gnn_attn_key", "L0_gnn_attn_edge", "L0_gnn_bias", "L1_gnn_W0", "L1_gnn_b0", "L1_gnn_W1", "L1_gnn_b1",
        "L1_gnn_W2", "L1_gnn_b2"]


def kernel(**inputs):
    import numpy as np
    import concourse.bacc as bacc
    from concourse import mybir
    from concourse.bass_utils import run_bass_kernel_spmd

    nc = bacc.Bacc("TRN2", target_bir_lowering=False, num_devices=1)
    arrays, ap = {}, {}
    for name in _INS:
        a = np.ascontiguousarray(inputs[name])
        arrays[f"in_{name}"] = a
        ap[name] = nc.dram_tensor(f"in_{name}", a.shape, mybir.dt.from_np(a.dtype), kind="ExternalInput").ap()
    out = nc.dram_tensor("out_rows", [N, D], F32, kind="ExternalOutput").ap()
    build(nc, ap["x"], ap["src"], ap["dst"], ap["edge_attr_64"], ap["edge_weight"], ap["L0_gnn_W_node"], ap["L0_gnn_W_edge"],
          ap["L0_gnn_attn_query"], ap["L0_gnn_attn_key"], ap["L0_gnn_attn_edge"], ap["L0_gnn_bias"],
          ap["L1_gnn_W0"], ap["L1_gnn_b0"], ap["L1_gnn_W1"], ap["L1_gnn_b1"], ap["L1_gnn_W2"], ap["L1_gnn_b2"], out)
    r = run_bass_kernel_spmd(nc, [arrays], core_ids=[0])
    return r.results[0]["out_rows"]
```

```python
from contextlib import ExitStack

import concourse.bass as bass
from concourse import mybir

F32 = mybir.dt.float32
I32 = mybir.dt.int32
ALU = mybir.AluOpType
ACT = mybir.ActivationFunctionType
AX = mybir.AxisListType

P = 128
N, E, D, H = 100000, 50000, 64, 4
PC = 2 * (D + H)
HD = D // H
T = 392
PA, TA = 112, 392
PB, TB = 16, 381
assert PA * TA + PB * TB == E and PA + PB == P
C = 14
TX = T + 2 * C
CH = T // C
R4 = 4
NB4 = CH // R4
SW = D + H
SLOT0 = N
ROWS = N + P * T
XW = 68
GW = D + 2 * H
C1 = C + 1
W = C * D
BR = 8
BN = P * BR
FULL = N // BN
TP, TR = 112, 6
assert FULL * BN + TP * TR == N and FULL == 97
XS = 3
XS_TURNS = (FULL + 1) // (4 * XS)
assert 0 < FULL + 1 - 4 * XS * XS_TURNS <= XS
DT = (FULL + 1) // 4 - 1
assert 4 * DT + 6 == FULL + 1
BIG = 1.0e30
SKIP = 200000.0
EPS = 1e-5


DLOADS = 2 + T - TB
WLOADS = 25


class Steps:

    def __init__(self, sem):
        self.sem, self.base, self.n, self.turns = sem, 0, 0, 0

    def enter(self, j, each):
        self.base, self.n, self.turns, self.each = self.base + self.n, 0, j, each

    def leave(self, count):
        assert self.n == self.each, (self.n, self.each)
        self.base, self.n, self.turns = self.base + self.each * count, 0, 0

    def mark(self, instruction):
        instruction.then_inc(self.sem, 1)
        self.n += 1
        at = self.base + self.n
        return at if isinstance(self.turns, int) else self.turns * self.each + at

    def on(self, engine, instruction):
        engine.wait_ge(self.sem, self.mark(instruction))


def turns(engine, count, body, step=None, each=0, peel=1):
    for j in range(peel):
        body(j)
    with engine.Fori(peel, count) as j:
        if step:
            step.enter(j - peel, each)
        body(j)
        if step:
            step.leave(count - peel)


def build(nc, x, src, dst, edge_attr, edge_weight, W_node, W_edge, a_query, a_key, a_edge, bias,
          W0, b0, W1, b1, W2, b2, out):
    with ExitStack() as ctx:
        def sb(name, shape, dt=F32):
            return ctx.enter_context(nc.sbuf_tensor(name, shape, dt))

        def sem(name):
            return ctx.enter_context(nc.semaphore(name))

        def dram(name, shape):
            return nc.dram_tensor(name, shape, F32, kind="Internal").ap()

        xs_dram = dram("xs_dram", [N, XW])
        xd_dram = dram("xd_dram", [P * T, D])
        gat_dram = dram("gat_dram", [P * T, GW])
        x1_dram = dram("x1_dram", [P * T, D])
        pre_dram = [dram(f"pre{l}_dram", [P * T, D]) for l in range(3)]
        tab_dram = [dram(f"tab{l}_dram", [ROWS, D]) for l in range(3)]

        def slots(ap, k):
            return ap.rearrange("(p t) f -> p t f", t=T)[:, bass.ds(k * C, C), :]

        def tab_slots(l, k):
            return slots(tab_dram[l][SLOT0:ROWS, :], k)

        ident = sb("ident", [P, P])
        src_i, dst_i = sb("src_i", [P, TX], I32), sb("dst_i", [P, TX], I32)
        ew = sb("ew", [P, T])
        srcf, dstf = sb("srcf", [P, T]), sb("dstf", [P, T])
        prev_i, next_i = sb("prev_i", [P, 1], I32), sb("next_i", [P, 1], I32)
        same, breakf, isend, first = (sb(n, [P, T]) for n in ("same", "breakf", "isend", "first"))
        slot_i, slotf = sb("slot_i", [P, T], I32), sb("slotf", [P, T])
        shiftf, tmpT, onehot = sb("shiftf", [P, TX]), sb("tmpT", [P, T]), sb("onehot", [P, T])
        map_i, out_i, row_i = (sb(n, [P, TX], I32) for n in ("map_i", "out_i", "row_i"))
        deg, dis, padneg = sb("deg", [P, T]), sb("dis", [P, T]), sb("padneg", [P, T])
        negs = sb("negs", [PB, T - TB])
        col = sb("col", [P, 16])
        (c_prev, c_next, c_cont, c_whole, c_t1, c_slot, c_dis, c_end, c_run, c_tmp) = (
            col[:, i:i + 1] for i in range(10))
        seam_i = sb("seam_i", [P, 4], I32)
        i_slot, i_row, i_out = (seam_i[:, i:i + 1] for i in range(3))
        eps_c = sb("eps_c", [P, 1])
        W0b, W1b, W2b = (sb(n, [P, P]) for n in ("W0b", "W1b", "W2b"))
        WM = sb("WM", [P, PC])
        WN = WM[:, 0:2 * D]
        Wn2, We2 = sb("Wn2", [P, D]), sb("We2", [P, D])
        wprod, wred = sb("wprod", [P, 3, D]), sb("wred", [P, 3, H])
        att_bc = sb("att_bc", [P, 3, D])
        WA = sb("WA", [P, 3, 2 * H])
        bias_bc = sb("bias_bc", [P, D])
        b_bc = [sb(f"b{l}_bc", [P, D]) for l in range(3)]
        b0c, b1c, b2c = (sb(n, [P, 1]) for n in ("b0c", "b1c", "b2c"))

        ix, ix2, sv = sb("ix", [P, R4, C], I32), sb("ix2", [P, R4, C], I32), sb("sv", [P, R4, C])
        PAIR = 2 * C
        G = sb("G", [P, R4, C, XW])
        GX = sb("GX", [P, R4, C, D])
        IN = sb("IN", [P, 4, W])
        XD, EA = (IN[:, 2 * i:2 * i + 2, :].rearrange("p b (t f) -> p b t f", f=D) for i in range(2))
        TS = [sb(f"TS{i}", [P, 2, 7, P]) for i in range(3)]
        Z, LB, AM = sb("Z", [P, C, H]), sb("LB", [P, H, C1]), sb("AM", [P, H, C1])
        M = sb("M", [P, 2, H, C1])
        DE, RX = sb("DE", [P, 2 * H, C]), sb("RX", [P, 2 * H, C])
        AB, B = sb("AB", [P, SW, C1]), sb("B", [P, SW, C1])
        AS = sb("AS", [P, 2, D, C1])
        SS = sb("SS", [P, 2, SW, C1])
        RD = sb("RD", [P, H, C])
        NR = sb("NR", [P, 2, C, GW])
        UU, Q = sb("UU", [P, 2, C, D]), sb("Q", [P, C, D])
        U = UU[:, 0]
        X1, Y0 = sb("X1", [P, 2, C, D]), sb("Y0", [P, 2, C, D])
        PR = sb("PR", [P, 2, C, D])
        XD4 = IN[:, :, :].rearrange("p b (t f) -> p b t f", f=D)
        XC, EF = PR[:, 0], PR[:, 1]
        OB = G[:, :, :, 0:D]
        est = sb("est", [P, 4, C])

        def early(tile, pattern):
            flat_ = tile.rearrange(pattern)
            return flat_[:, 0:2 * BR * D].rearrange("p (b t f) -> p b t f", b=2, f=D)

        dX1 = IN[:, :, 0:BR * D].rearrange("p b (t f) -> p b t f", f=D)
        dR1, dR2 = early(PR[:, :, :, :], "p b t f -> p (b t f)"), early(Y0[:, :, :, :], "p b t f -> p (b t f)")
        dO, dX = early(X1[:, :, :, :], "p b t f -> p (b t f)"), early(AS[:, :, :, :], "p b f t -> p (b f t)")
        dC, dQ2 = sb("dC", [P, BR, D]), sb("dQ2", [P, BR, D])
        dU, dQ1 = U[:, 0:BR, :], Q[:, 0:BR, :]
        dh0, dh1, dh2, dh3 = (sb(n, [P, 4, P]) for n in ("dh0", "dh1", "dh2", "dh3"))
        dst8 = sb("dst8", [P, 8, BR])
        XM = sb("XM", [P, 4, BR, XW])
        XL = G[:, :, :, :].rearrange("p b t f -> p b (t f)")[:, :, 0:BR * D].rearrange("p b (t f) -> p b t f", f=D)

        bc = sb("bc", [P, 4, SW])
        run_r, cont_r, nrun_r, ncont_r = (sb(n, [SW, P]) for n in ("run_r", "cont_r", "nrun_r", "ncont_r"))
        LS, LM = sb("LS", [P, SW]), sb("LM", [P, SW])
        mE, mC, rE, bE, sE, sC = (sb(n, [SW, P]) for n in ("mE", "mC", "rE", "bE", "sE", "sC"))
        cS, cM = sb("cS", [P, SW]), sb("cM", [P, SW])
        grow, xrow, prow = sb("grow", [P, GW]), sb("xrow", [P, D]), sb("prow", [P, D])
        S68, M68, MM, wS, wC = (sb(n, [P, SW]) for n in ("S68", "M68", "MM", "wS", "wC"))
        sden = sb("sden", [P, H])
        su, sq, x1row, yrow = (sb(n, [P, D]) for n in ("su", "sq", "x1row", "yrow"))
        prT = sb("prT", [D, P])
        sst = sb("sst", [P, 4])

        ps = ctx.enter_context(nc.psum_tensor("ps", [P, 8, 512], F32))
        pT, pM1, pM2, pM3, pR1, pR2, pO = (ps[:, i, :] for i in range(7))
        flat = ps[:, :, :].rearrange("p a b -> p (a b)")
        TRP = [flat[:, 0:W], flat[:, 1024:1024 + W]]
        HS = flat[:, 2048:2048 + W].rearrange("p (t f) -> p t f", f=D)

        def hl(q0, q1):
            at = 2048 + 512 * (q0 // 3) + PC * (q0 % 3)
            return flat[:, at:at + PC * (q1 - q0)].rearrange("p (q c) -> p q c", c=PC)

        SM = ps[:, 7, :]

        names = """consts_set zeroed loaded_dst loaded_idx loaded_w filled ends_loaded seam_set flags_ready weights_ready
            vector_step rows_in rows_T chain_in chain_T chain_back_in chain_back deg_in deg_sqrt
            d_xfree d_c1 d_sq1 d_v1 d_sd1 d_x1 d_trx d_h0 d_m1 d_h1 d_m2 d_r1 d_h2 d_r2 d_m3 d_h3 d_o
            d_R1 d_R2 d_u2 d_c2 d_sq2 d_v2 d_sd2 d_O
            xs_copied idx_staged out_idx_staged turn
            g_shift g_xc g_trx g_trd g_tre g_ev g_lg g_z g_de g_ex g_ab g_hsfree g_S
            g_xdfree g_nr g_nrm g_c g_q g_v g_sd g_x1 g_y0
            l_gfree l_as l_scan l_pre l_tr l_ev l_z l_zfree l_u l_y l_c l_q l_v l_sd l_o
            s_row s_ex_in s_ex s_mid s_midT s_prT s_mm s_c s_q s_v s_sd s_out s_stored""".split()
        S = {n: sem(n) for n in names}
        d_xl = [sem(f"dense_x_loaded{b}") for b in range(2)]
        d_st = [[sem(f"dense_stored{j}_{b}") for b in range(2)] for j in range(4)]
        xm_ld = [sem(f"xs_loaded{b}") for b in range(4)]
        xm_st = [sem(f"xs_stored{b}") for b in range(4)]
        xg_ld = [sem(f"xdst_gathered{b}") for b in range(R4)]
        xg_st = [sem(f"xdst_stored{b}") for b in range(R4)]
        mp_st = [sem(f"shift_scattered{b}") for b in range(R4)]
        g_ld = [sem(f"gat_gathered{b}") for b in range(R4)]
        g_in = [sem(f"gat_inputs{b}") for b in range(2)]
        g_out = [[sem(f"gat_stored{j}_{b}") for b in range(2)] for j in range(3)]
        l_ld = [sem(f"gcn_gathered{b}") for b in range(R4)]
        l_in = [sem(f"gcn_inputs{b}") for b in range(2)]
        l_out = [[sem(f"gcn_stored{j}_{b}") for b in range(2)] for j in range(2)]
        o_st = [sem(f"rows_scattered{b}") for b in range(R4)]

        HALF = 16 * CH // 2
        BLOCKS = FULL + 1

        block = ctx.enter_context(nc.Block())

        @block.sync
        def _(sp):
            def need(sem_, value):
                sp.wait_ge(sem_, value)
                sp.sem_inc(S["turn"], 1)

            def load_slots(tile, arr, signal):
                sp.dma_start(tile[0:PA, 0:TA], arr[0:PA * TA].rearrange("(p t) -> p t", t=TA)).then_inc(signal, 16)
                sp.dma_start(tile[PA:P, 0:TB], arr[PA * TA:E].rearrange("(p t) -> p t", t=TB)).then_inc(signal, 16)

            load_slots(dst_i, dst, S["loaded_dst"])
            with nc.allow_non_contiguous_dma(reason="one word per slot, 11 slots"):
                last = dst[PA * TA:E].rearrange("(p t) -> p t", t=TB)[:, TB - 1:TB]
                for t in range(TB, T):
                    sp.dma_start(dst_i[PA:P, t:t + 1], last).then_inc(S["loaded_dst"], 16)
            sp.wait_ge(S["zeroed"], 1)
            load_slots(src_i, src, S["loaded_idx"])
            load_slots(ew, edge_weight, S["loaded_idx"])
            sp.dma_start(padneg[PA:P, TB:T], negs[:, :]).then_inc(S["filled"], 16)
            sp.wait_ge(S["loaded_dst"], DLOADS * 16)
            sp.dma_start(prev_i[1:P, :], dst_i[0:P - 1, T - 1:T]).then_inc(S["ends_loaded"], 16)
            sp.dma_start(next_i[0:P - 1, :], dst_i[1:P, 0:1]).then_inc(S["ends_loaded"], 16)
            n = 0
            for tile, w in ((WN, W_node), (W0b, W0), (W1b, W1), (W2b, W2)):
                for h in range(2):
                    sp.dma_start(tile[64 * h:64 * h + 64, 64 * h:64 * h + 64], w).then_inc(S["loaded_w"], 16)
                    n += 1
            for tile, w in ((Wn2, W_node), (We2, W_edge)):
                for h in range(2):
                    sp.dma_start(tile[64 * h:64 * h + 64, :], w).then_inc(S["loaded_w"], 16)
                    n += 1
            for j, a in enumerate((a_key, a_query, a_edge)):
                row = a.rearrange("h d -> (h d)").rearrange("(o n) -> o n", o=1)
                sp.dma_start(att_bc[:, j, :], row.to_broadcast([P, D])).then_inc(S["loaded_w"], 16)
                n += 1
            for tile, v in ((bias_bc, bias), (b_bc[0], b0), (b_bc[1], b1), (b_bc[2], b2)):
                sp.dma_start(tile[:, :], v.rearrange("(o n) -> o n", o=1).to_broadcast([P, D])).then_inc(S["loaded_w"], 16)
                n += 1
            with nc.allow_non_contiguous_dma(reason="128 words"):
                for tile, v in ((b0c, b0), (b1c, b1), (b2c, b2)):
                    for h in range(2):
                        sp.dma_start(tile[64 * h:64 * h + 64, :], v.rearrange("(n o) -> n o", o=1)).then_inc(S["loaded_w"], 16)
                        n += 1
            assert n == WLOADS

            def shape(m):
                return (TP, TR) if isinstance(m, int) and m == BLOCKS - 1 else (P, BR)

            def rows(ap, i, np_, r):
                return ap[bass.ds(i * BN, np_ * r), :].rearrange("(p t) f -> p t f", t=r)

            def load_x(m, b, free=None):
                np_, r = shape(m)
                if free is not None:
                    need(S["d_xfree"], free)
                sp.dma_start(dX[0:np_, b, 0:r, :], rows(x, m, np_, r)).then_inc(d_xl[b], 16)

            def store(j_, m, b, buf, ready):
                np_, r = shape(m)
                need(S[ready], m + 1)
                table = out if j_ == 3 else tab_dram[j_]
                sp.dma_start(rows(table, m, np_, r), buf[0:np_, b, 0:r, :]).then_inc(d_st[j_][b % 2], 16)

            def step_loads(j, c):
                if not isinstance(j, int) or 4 * j + c + 3 < BLOCKS:
                    load_x(j * 4 + (c + 3), (c + 3) % 2, free=j * 4 + (c + 2))

            def step_stores(j, c):
                for j_, d, buf, ready in ((0, 1, dX1, "d_x1"), (1, 0, dR1, "d_R1"), (2, -1, dR2, "d_R2"), (3, -2, dO, "d_O")):
                    if not isinstance(j, int) or 0 <= 4 * j + c + d < BLOCKS:
                        store(j_, j * 4 + (c + d), (c + d) % (4 if j_ == 0 else 2), buf, ready)

            def xs_loads(j, c):
                for i in range(XS if not isinstance(j, int) else min(XS, BLOCKS - XS * (4 * j + c))):
                    m, b = j * (4 * XS) + (XS * c + i), (XS * c + i) % 4
                    np_, r = shape(m)
                    if not (isinstance(m, int) and m < 4):
                        need(S["xs_copied"], m - 3)
                    sp.dma_start(XL[0:np_, b, 0:r, :], rows(x, m, np_, r)).then_inc(xm_ld[b], 16)

            def xs_stores(j, c):
                for i in range(XS):
                    m, b = j * (4 * XS) + (XS * (c - 1) + i), (XS * (c - 1) + i) % 4
                    if isinstance(m, int) and not 0 <= m < BLOCKS:
                        continue
                    np_, r = shape(m)
                    need(S["xs_copied"], m + 1)
                    sp.dma_start(rows(xs_dram, m, np_, r), XM[0:np_, b, 0:r, :]).then_inc(xm_st[b], 16)

            def with_xs(j, c):
                xs_loads(j, c)
                step_loads(j, c)
                xs_stores(j, c)
                step_stores(j, c)

            for m in range(3):
                load_x(m, m % 2, free=None if m < 2 else 1)
            store(0, 0, 0, dX1, "d_x1")
            for c in range(4):
                with_xs(0, c)
            with sp.Fori(1, XS_TURNS) as j:
                for c in range(4):
                    with_xs(j, c)
            with_xs(XS_TURNS, 0)
            for c in range(1, 4):
                step_loads(XS_TURNS, c)
                if c == 1:
                    xs_stores(XS_TURNS, c)
                step_stores(XS_TURNS, c)
            with sp.Fori(XS_TURNS + 1, DT) as j:
                for c in range(4):
                    step_loads(j, c)
                    step_stores(j, c)
            for c in range(8):
                step_loads(DT, c)
                step_stores(DT, c)

            for b in range(R4):
                need(xg_st[b], NB4 * 16)
            for b in range(2):
                need(d_st[0][b], BLOCKS // 2 * 16)

            ea_a = edge_attr[0:PA * TA, :].rearrange("(p t) f -> p t f", t=TA)
            ea_b = edge_attr[PA * TA:E, :].rearrange("(p t) f -> p t f", t=TB)

            def gat_load(k, b, cb=C):
                if not (isinstance(k, int) and k < R4):
                    need(S["g_xdfree"], k - R4 + 1)
                if not (isinstance(k, int) and k < 1):
                    need(S["g_tre"], k)
                sp.dma_start(XD4[:, b], slots(xd_dram, k)).then_inc(g_in[b % 2], 16)
                sp.dma_start(EF[0:PA], ea_a[:, bass.ds(k * C, C), :]).then_inc(g_in[b % 2], 16)
                sp.dma_start(EF[PA:P, 0:cb], ea_b[:, bass.ds(k * C, cb), :]).then_inc(g_in[b % 2], 16)

            def store_state(k, b):
                need(S["g_nrm"], k + 1)
                need(S["g_nr"], 2 * (k + 1))
                sp.dma_start(slots(gat_dram, k), NR[:, b]).then_inc(g_out[0][b], 16)

            def store_normed(k, b):
                need(S["g_x1"], k + 1)
                sp.dma_start(slots(x1_dram, k), X1[:, b]).then_inc(g_out[1][b], 16)
                need(S["g_y0"], k + 1)
                sp.dma_start(tab_slots(0, k), Y0[:, b]).then_inc(g_out[2][b], 16)

            for k in range(3):
                gat_load(k, k)

            def gat_four(j):
                for b in range(R4):
                    k = j * R4 + b
                    gat_load(k + 3, (b + 3) % R4)
                    store_state(k, b % 2)
                    if not (isinstance(k, int) and k == 0):
                        store_normed(k - 1, (b - 1) % 2)

            turns(sp, NB4 - 1, gat_four)
            for k in range(CH - R4, CH):
                if k == CH - R4:
                    gat_load(CH - 1, 3, cb=TB - (CH - 1) * C)
                store_state(k, k % 2)
                store_normed(k - 1, (k - 1) % 2)
            store_normed(CH - 1, 1)

            for l in range(3):
                need(S["s_stored"], 32 + 16 * l)

                def load(k, b, free=None):
                    if free is not None:
                        need(S["l_pre"], CH * l + free)
                        if l == 2:
                            need(S["l_u"], free)
                    sp.dma_start(XD[:, b], tab_slots(l, k)).then_inc(l_in[b], 16)
                    if l == 2:
                        sp.dma_start(EA[:, b], slots(x1_dram, k)).then_inc(l_in[b], 16)

                def store_sums(k, b):
                    need(S["l_pre"], CH * l + k + 1)
                    sp.dma_start(slots(pre_dram[l], k), PR[:, b]).then_inc(l_out[0][b], 16)

                def store_rows(k, b):
                    if l < 2:
                        need(S["l_y"], CH * l + k + 1)
                        sp.dma_start(tab_slots(l + 1, k), Y0[:, b]).then_inc(l_out[1][b], 16)

                def store(k, b):
                    store_sums(k, b)
                    store_rows(k, b)

                load(0, 0)
                load(1, 1)
                with sp.Fori(0, NB4 - 1) as j:
                    for b in range(R4):
                        load(j * R4 + b + 2, b % 2, free=j * R4 + b + 1)
                        store(j * R4 + b, b % 2)
                for k in range(CH - 4, CH):
                    if k + 2 < CH:
                        load(k + 2, k % 2, free=k + 1)
                        store(k, k % 2)
                for k in range(CH - 2, CH):
                    store_sums(k, k % 2)
                for k in range(CH - 2, CH):
                    store_rows(k, k % 2)

            for b in range(2):
                need(d_st[3][b], BLOCKS // 2 * 16)

        @block.gpsimd
        def _(pool):
            pool.wait_ge(S["zeroed"], 1)
            chain = Steps(S["consts_set"])
            chain.on(pool, nc.gpsimd.affine_select(out=ident[:, :], in_=ident[:, :], compare_op=ALU.not_equal, fill=1.0,
                                                   base=0, pattern=[[-1, P]], channel_multiplier=1))
            chain.on(pool, nc.gpsimd.iota(slot_i[:, :], pattern=[[1, T]], base=0, channel_multiplier=T))
            pool.wait_ge(S["loaded_dst"], DLOADS * 16)

            def take_turn():
                nc.gpsimd.sem_inc(S["turn"], 1)

            staged = [0]

            def pair_of(tile, b):
                return tile[:, b:b + 2, :].rearrange("p b t -> p (b t)")

            def stage(k, b, source, values):
                if values is not None:
                    nc.gpsimd.tensor_copy(pair_of(sv, b), values[:, bass.ds(k * C, PAIR)])
                nc.gpsimd.tensor_copy(pair_of(ix, b), source[:, bass.ds(k * C, PAIR)]).then_inc(S["idx_staged"], 1)

            def chunks(source, ready, fire, landed, landed0=0, values=None, peel=1):
                def four(j):
                    for b in range(R4):
                        k = j * R4 + b
                        ready(k, b, j)
                        if b % 2 == 0:
                            pool.wait_ge(S["idx_staged"], j * 2 + (staged[0] + b // 2 + 1))
                        take_turn()
                        fire(k, b, j)
                        if b % 2 == 0:
                            n = j + (1 if b == 2 else 0)
                            if not (isinstance(n, int) and n == 0):
                                pool.wait_ge(landed[(b + 2) % R4], n * (16 * C) + landed0)
                                pool.wait_ge(landed[(b + 3) % R4], n * (16 * C) + landed0)
                            take_turn()
                            stage(k + 2, (b + 2) % R4, source, values)

                if staged[0]:
                    pool.wait_ge(S["idx_staged"], staged[0])
                    take_turn()
                stage(0, 0, source, values)
                turns(pool, NB4, four, peel=peel)
                staged[0] += CH // 2 + 1

            def gather(table, buf, b, landed):
                for t in range(C):
                    nc.gpsimd.indirect_dma_start(out=buf[:, b, t, :], out_offset=None, in_=table,
                                                 in_offset=bass.IndirectOffsetOnAxis(ap=ix[:, b, t:t + 1], axis=0)).then_inc(landed, 16)

            def xd_store(k, b, n):
                pool.wait_ge(xg_ld[b], n * 16 * C)
                take_turn()
                nc.gpsimd.dma_start(slots(xd_dram, k), GX[:, b]).then_inc(xg_st[b], 16)

            def xd_ready(k, b, j):
                if not (isinstance(j, int) and j == 0):
                    pool.wait_ge(xg_st[b], j * 16)

            def xd_fire(k, b, j):
                gather(x, GX, b, xg_ld[b])
                if not (isinstance(k, int) and k == 0):
                    xd_store(k - 1, (b - 1) % R4, j + (0 if b == 0 else 1))

            chunks(dst_i, xd_ready, xd_fire, xg_ld)
            xd_store(CH - 1, R4 - 1, NB4)

            pool.wait_ge(S["flags_ready"], 1)
            for b in range(4):
                pool.wait_ge(xm_st[b], (25 if b < 2 else 24) * 16)

            def shift_fire(k, b, j):
                for t in range(C):
                    nc.gpsimd.indirect_dma_start(out=xs_dram, out_offset=bass.IndirectOffsetOnAxis(ap=ix[:, b, t:t + 1], axis=0),
                                                 in_=sv[:, b, t:t + 1], in_offset=None, element_offset=D,
                                                 bounds_check=N - 1, oob_is_err=False).then_inc(mp_st[b], 16)

            chunks(map_i, lambda k, b, j: None, shift_fire, mp_st, values=shiftf)
            for b in range(R4):
                pool.wait_ge(mp_st[b], NB4 * 16 * C)

            def gat_ready(k, b, j):
                if not (isinstance(j, int) and j == 0):
                    pool.wait_ge(S["g_xc"], k - R4 + 1)
                    pool.wait_ge(S["g_shift"], k - R4 + 1)
                    take_turn()

            chunks(src_i, gat_ready, lambda k, b, j: gather(xs_dram, G, b, g_ld[b]), g_ld)

            for b in range(2):
                pool.wait_ge(g_out[0][b], HALF)
            pool.wait_ge(S["seam_set"], 1)
            for table, row in ((gat_dram, grow), (xd_dram, xrow)):
                nc.gpsimd.indirect_dma_start(out=row[:, :], out_offset=None, in_=table,
                                             in_offset=bass.IndirectOffsetOnAxis(ap=i_slot, axis=0)).then_inc(S["s_row"], 16)
            for b in range(2):
                pool.wait_ge(g_out[1][b], HALF)
                pool.wait_ge(g_out[2][b], HALF)
            pool.wait_ge(S["s_out"], 1)
            for table, row, idx in ((x1_dram, x1row, i_slot), (tab_dram[0], yrow, i_row)):
                nc.gpsimd.indirect_dma_start(out=table, out_offset=bass.IndirectOffsetOnAxis(ap=idx, axis=0),
                                             in_=row[:, :], in_offset=None).then_inc(S["s_stored"], 16)
            pool.wait_ge(S["s_stored"], 32)

            def scatter_chunk(k, b, j):
                if b % 2 == 0:
                    pool.wait_ge(S["out_idx_staged"], j * 2 + (b // 2 + 1))
                    take_turn()
                pool.wait_ge(S["l_o"], k + 1)
                take_turn()
                for t in range(C):
                    nc.gpsimd.indirect_dma_start(out=out, out_offset=bass.IndirectOffsetOnAxis(ap=ix2[:, b, t:t + 1], axis=0),
                                                 in_=OB[:, b, t, :], in_offset=None,
                                                 bounds_check=N - 1, oob_is_err=False).then_inc(o_st[b], 16)
                if b % 2 == 0:
                    n = j + (1 if b == 2 else 0)
                    if not (isinstance(n, int) and n == 0):
                        pool.wait_ge(o_st[(b + 2) % R4], n * (16 * C))
                        pool.wait_ge(o_st[(b + 3) % R4], n * (16 * C))
                    take_turn()
                    stage_out(k + 2, (b + 2) % R4)

            def stage_out(k, b):
                nc.gpsimd.tensor_copy(pair_of(ix2, b), out_i[:, bass.ds(k * C, PAIR)]).then_inc(S["out_idx_staged"], 1)

            for l in range(3):
                for b in range(2):
                    pool.wait_ge(d_st[l][b], BLOCKS // 2 * 16)
                if l == 2:
                    for b in range(2):
                        pool.wait_ge(d_st[3][b], BLOCKS // 2 * 16)

                def ready(k, b, j):
                    if not (isinstance(j, int) and j == 0):
                        pool.wait_ge(S["l_gfree"], k + (CH * l - R4 + 1))

                def fire(k, b, j):
                    gather(tab_dram[l], GX, b, l_ld[b])
                    if l == 2 and not (isinstance(j, int) and j == 0):
                        scatter_chunk(k - R4, b, j - 1)

                if l == 2:
                    stage_out(0, 0)
                chunks(row_i, ready, fire, l_ld, landed0=l * NB4 * 16 * C, peel=2 if l == 2 else 1)
                if l == 2:
                    for k in range(CH - R4, CH - 2):
                        scatter_chunk(k, k % R4, k // R4)

                for b in range(2):
                    pool.wait_ge(l_out[0][b], (l + 1) * HALF)
                nc.gpsimd.indirect_dma_start(out=prow[:, :], out_offset=None, in_=pre_dram[l],
                                             in_offset=bass.IndirectOffsetOnAxis(ap=i_slot, axis=0)).then_inc(S["s_row"], 16)
                if l < 2:
                    for b in range(2):
                        pool.wait_ge(l_out[1][b], (l + 1) * HALF)
                else:
                    for k in range(CH - 2, CH):
                        scatter_chunk(k, k % R4, k // R4)
                pool.wait_ge(S["s_out"], l + 2)
                if l < 2:
                    nc.gpsimd.indirect_dma_start(out=tab_dram[l + 1], out_offset=bass.IndirectOffsetOnAxis(ap=i_row, axis=0),
                                                 in_=yrow[:, :], in_offset=None).then_inc(S["s_stored"], 16)
                    pool.wait_ge(S["s_stored"], 48 + 16 * l)
                else:
                    nc.gpsimd.indirect_dma_start(out=out, out_offset=bass.IndirectOffsetOnAxis(ap=i_out, axis=0),
                                                 in_=yrow[:, :], in_offset=None,
                                                 bounds_check=N - 1, oob_is_err=False).then_inc(S["s_stored"], 16)
                    pool.wait_ge(S["s_stored"], 48 + 16 * l)
            for b in range(R4):
                pool.wait_ge(o_st[b], NB4 * 16 * C)

        def repeat(scalar_per_row, n):
            shape = list(scalar_per_row.shape)
            return scalar_per_row.unsqueeze(len(shape)).to_broadcast(shape + [n])

        def over_rows(vec, r, np_=P):
            return vec.unsqueeze(1).to_broadcast([np_, r, D])

        @block.tensor
        def _(pe):
            mm, tr = nc.tensor.matmul, nc.tensor.transpose
            pe.wait_ge(S["consts_set"], 1)

            def pairs_T(dst_ps, rows_sb, signal, np_=P, n=7):
                for q in range(n):
                    last = tr(dst_ps[:, q * P:q * P + np_], rows_sb[0:np_, 2 * q:2 * q + 2, :].rearrange("p t f -> p (t f)"),
                              ident[0:np_, 0:np_])
                last.then_inc(signal, 1)

            pe.wait_ge(S["rows_in"], 1)
            for i in range(4):
                last = tr(SM[0:SW, i * P:(i + 1) * P], bc[:, i, :], ident[:, :])
            last.then_inc(S["rows_T"], 1)

            def chain(n, with_max=False):
                pe.wait_ge(S["chain_in"], n + 1)
                last = tr(SM[0:SW, 0:P], LS[:, :], ident[:, :])
                if with_max:
                    last = tr(SM[0:SW, P:2 * P], LM[:, :], ident[:, :])
                last.then_inc(S["chain_T"], 1)
                pe.wait_ge(S["chain_back_in"], n + 1)
                last = tr(SM[:, 2 * P:2 * P + SW], sC[:, :], ident[0:SW, 0:SW])
                if with_max:
                    last = tr(SM[:, 2 * P + SW:2 * P + 2 * SW], mC[:, :], ident[0:SW, 0:SW])
                last.then_inc(S["chain_back"], 1)

            chain(0)
            pe.wait_ge(S["loaded_w"], WLOADS * 16)

            def shape(m):
                return (TP, TR) if isinstance(m, int) and m == BLOCKS - 1 else (P, BR)

            def cols(a, np_, n):
                return a.rearrange("p (q m) -> p q m", m=P)[:, 0:n, 0:np_]

            def since(sem_, value):
                if not (isinstance(value, int) and value <= 0):
                    pe.wait_ge(sem_, value)

            def dense(j, c):
                s_ = j * 4 + c
                new = not isinstance(s_, int) or s_ < BLOCKS
                old = not isinstance(s_, int) or s_ >= 1
                if new:
                    np_, r = shape(s_)
                    n = r // 2
                    pe.wait_ge(S["d_x1"], s_ + 1)
                    since(S["d_h0"], s_)
                    pairs_T(pT, dX1[:, c % 4], S["d_trx"], np_, n)
                if old:
                    np1, r1 = shape(s_ - 1)
                    n1 = r1 // 2
                    pe.wait_ge(S["d_h1"], s_)
                    since(S["d_h2"], s_ - 1)
                    mm(cols(pM2, np1, n1), lhsT=W1b[:, :], rhs=dh1[:, 0:n1, 0:np1], start=True, stop=True).then_inc(S["d_m2"], 1)
                if new:
                    pe.wait_ge(S["d_h0"], s_ + 1)
                    since(S["d_h1"], s_)
                    mm(cols(pM1, np_, n), lhsT=W0b[:, :], rhs=dh0[:, 0:n, 0:np_], start=True, stop=True).then_inc(S["d_m1"], 1)
                if old:
                    pe.wait_ge(S["d_h2"], s_)
                    since(S["d_h3"], s_ - 1)
                    mm(cols(pM3, np1, n1), lhsT=W2b[:, :], rhs=dh2[:, 0:n1, 0:np1], start=True, stop=True).then_inc(S["d_m3"], 1)
                    since(S["d_R2"], s_ - 1)
                    for q in range(n1):
                        last = tr(pR2[0:np1, q * P:(q + 1) * P], dh2[:, q, 0:np1], ident[:, :])
                    last.then_inc(S["d_r2"], 1)
                if new:
                    pe.wait_ge(S["d_h1"], s_ + 1)
                    since(S["d_R1"], s_)
                    for q in range(n):
                        last = tr(pR1[0:np_, q * P:(q + 1) * P], dh1[:, q, 0:np_], ident[:, :])
                    last.then_inc(S["d_r1"], 1)
                if old:
                    pe.wait_ge(S["d_h3"], s_)
                    since(S["d_u2"], s_ - 1)
                    for q in range(n1):
                        last = tr(pO[0:np1, q * P:(q + 1) * P], dh3[:, q, 0:np1], ident[:, :])
                    last.then_inc(S["d_o"], 1)

            for c in range(4):
                dense(0, c)
            with pe.Fori(1, DT) as j:
                for c in range(4):
                    dense(j, c)
            for c in range(7):
                dense(DT, c)

            pe.wait_ge(S["weights_ready"], 1)

            def transposed(k, b, j, i):
                rows_sb, signal = ((XD4[:, b], "g_trd"), (EF, "g_tre"), (XC, "g_trx"))[i]
                if i == 0:
                    pe.wait_ge(g_in[b % 2], (j * 2 + b // 2 + 1) * 48)
                if i == 2:
                    pe.wait_ge(S["g_xc"], k + 1)
                n = k * 3 + i
                if not (isinstance(n, int) and n < 2):
                    pe.wait_ge(S["g_ev"], n - 1)
                pairs_T(TRP[(3 * b + i) % 2], rows_sb, S[signal])

            def products(k, b):
                b2 = b % 2
                pe.wait_ge(S["g_ev"], k * 3 + 3)
                if not (isinstance(k, int) and k == 0):
                    pe.wait_ge(S["g_z"], k)
                    pe.wait_ge(S["g_hsfree"], k)
                for q in range(7):
                    for i in range(3):
                        if i == 0:
                            last = mm(hl(q, q + 1)[:, 0, :], lhsT=TS[0][:, b2, q, :], rhs=WM[:, :],
                                      start=True, stop=False, skip_group_check=True)
                        else:
                            last = mm(hl(q, q + 1)[:, 0, 2 * D:PC], lhsT=TS[i][:, b2, q, :], rhs=WA[:, i, :],
                                      start=False, stop=(i == 2), skip_group_check=True)
                last.then_inc(S["g_lg"], 1)

            def gat_four(j):
                for b in range(R4):
                    k = j * R4 + b
                    transposed(k, b, j, 2)
                    if not (isinstance(k, int) and k == CH - 1):
                        for i in range(2):
                            transposed(k + 1, (b + 1) % R4, j + (1 if b == R4 - 1 else 0), i)
                    products(k, b)

            for i in range(2):
                transposed(0, 0, 0, i)
            turns(pe, NB4 - 1, gat_four)
            gat_four(NB4 - 1)
            chain(1, with_max=True)

            for l in range(3):
                Wb = (W0b, W1b, W2b)[l]

                def gcn(k, b, k0=False):
                    at = CH * l + k
                    pe.wait_ge(S["l_pre"], at + 1)
                    if not (isinstance(k, int) and at < 2):
                        pe.wait_ge(S["l_ev"], at - 1)
                    pairs_T(TRP[b], PR[:, b], S["l_tr"])
                    pe.wait_ge(S["l_ev"], at + 1)
                    if not (isinstance(k, int) and at < 1):
                        pe.wait_ge(S["l_zfree"], at)
                    for q in range(7):
                        last = mm(HS[:, 2 * q:2 * q + 2, :].rearrange("p t f -> p (t f)"), lhsT=TS[b][:, 0, q, :],
                                  rhs=Wb[:, :], start=True, stop=True)
                    last.then_inc(S["l_z"], 1)

                for k in range(R4):
                    gcn(k, k % 2)
                with pe.Fori(1, NB4) as j:
                    for b in range(R4):
                        gcn(j * R4 + b, b % 2)
                chain(2 + l)
                pe.wait_ge(S["s_mid"], l + 1)
                tr(SM[0:D, 0:P], su[:, :], ident[:, :]).then_inc(S["s_midT"], 1)
                pe.wait_ge(S["s_prT"], l + 1)
                mm(SM[:, 384:384 + D], lhsT=prT[:, :], rhs=Wb[0:D, 0:D], start=True, stop=True).then_inc(S["s_mm"], 1)

        @block.scalar
        def _(act):
            fn = nc.scalar.activation
            act.wait_ge(S["zeroed"], 1)
            act.wait_ge(S["deg_in"], 1)
            fn(dis[:, :], tmpT[:, :], ACT.Sqrt).then_inc(S["deg_sqrt"], 1)
            act.wait_ge(S["loaded_w"], WLOADS * 16)

            def sq1(m, np_=P, r=BR):
                act.wait_ge(S["d_c1"], m + 1)
                fn(dQ1[0:np_, 0:r], dC[0:np_, 0:r], ACT.Square).then_inc(S["d_sq1"], 1)

            def sd1(m, np_=P, r=BR):
                act.wait_ge(S["d_v1"], m + 1)
                fn(dst8[0:np_, 4, 0:r], dst8[0:np_, 5, 0:r], ACT.Sqrt, bias=eps_c[0:np_, :], scale=1.0 / D).then_inc(S["d_sd1"], 1)

            def sq2(m, np_=P, r=BR):
                act.wait_ge(S["d_c2"], m + 1)
                fn(dQ2[0:np_, 0:r], dU[0:np_, 0:r], ACT.Square).then_inc(S["d_sq2"], 1)

            def sd2(m, np_=P, r=BR):
                act.wait_ge(S["d_v2"], m + 1)
                fn(dst8[0:np_, 6, 0:r], dst8[0:np_, 7, 0:r], ACT.Sqrt, bias=eps_c[0:np_, :], scale=1.0 / D).then_inc(S["d_sd2"], 1)

            def since(sem_, value):
                if not (isinstance(value, int) and value <= 0):
                    act.wait_ge(sem_, value)

            def shape(m):
                return (TP, TR) if isinstance(m, int) and m == BLOCKS - 1 else (P, BR)

            def cols(a, np_, n):
                return a.rearrange("p (q m) -> p q m", m=P)[:, 0:n, 0:np_]

            def spread(j, c, i):
                m, b, n = j * (4 * XS) + (XS * c + i), (XS * c + i) % 4, j * XS + (XS * c + i) // 4
                if isinstance(m, int) and m >= BLOCKS:
                    return
                np_, r = shape(m)
                act.wait_ge(xm_ld[b], n * 16 + 16)
                since(xm_st[b], n * 16)
                fn(XM[0:np_, b, 0:r, 0:D], XL[0:np_, b, 0:r, :], ACT.Copy).then_inc(S["xs_copied"], 1)

            def dense(j, c, xs=False):
                s_ = j * 4 + c
                known = isinstance(s_, int)
                new = not known or 0 <= s_ < BLOCKS
                old = not known or 1 <= s_ <= BLOCKS
                ln1 = not known or s_ + 1 < BLOCKS
                ln2 = not known or 2 <= s_
                if new:
                    np_, r = shape(s_)
                    n = r // 2
                    act.wait_ge(S["d_trx"], s_ + 1)
                    since(S["d_m1"], s_)
                    fn(dh0[:, 0:n, 0:np_], cols(pT, np_, n), ACT.Copy).then_inc(S["d_h0"], 1)
                if old:
                    np1, r1 = shape(s_ - 1)
                    n1 = r1 // 2
                    act.wait_ge(S["d_m2"], s_)
                    since(S["d_r2"], s_ - 1)
                    fn(dh2[:, 0:n1, 0:np1], cols(pM2, np1, n1), ACT.Relu, bias=b1c[:, :]).then_inc(S["d_h2"], 1)
                if new:
                    act.wait_ge(S["d_m1"], s_ + 1)
                    since(S["d_m2"], s_)
                    since(S["d_r1"], s_)
                    fn(dh1[:, 0:n, 0:np_], cols(pM1, np_, n), ACT.Relu, bias=b0c[:, :]).then_inc(S["d_h1"], 1)
                if ln2:
                    sq2(s_ - 2, *shape(s_ - 2))
                if ln1:
                    sq1(s_ + 1, *shape(s_ + 1))
                if old:
                    act.wait_ge(S["d_m3"], s_)
                    since(S["d_o"], s_ - 1)
                    fn(dh3[:, 0:n1, 0:np1], cols(pM3, np1, n1), ACT.Relu, bias=b2c[:, :]).then_inc(S["d_h3"], 1)
                if ln2:
                    sd2(s_ - 2, *shape(s_ - 2))
                if ln1:
                    sd1(s_ + 1, *shape(s_ + 1))
                if xs:
                    spread(j, c, 0)
                if old:
                    act.wait_ge(S["d_r2"], s_)
                    since(d_st[2][(c - 1) % 2], (j * 2 + (c - 1) // 2) * 16)
                    fn(dR2[0:np1, (c - 1) % 2, 0:r1].rearrange("p t f -> p (t f)"), pR2[0:np1, 0:n1 * P],
                       ACT.Copy).then_inc(S["d_R2"], 1)
                if xs:
                    spread(j, c, 1)
                    spread(j, c, 2)
                if new:
                    act.wait_ge(S["d_r1"], s_ + 1)
                    since(d_st[1][c % 2], (j * 2 + c // 2) * 16)
                    fn(dR1[0:np_, c % 2, 0:r].rearrange("p t f -> p (t f)"), pR1[0:np_, 0:n * P],
                       ACT.Copy).then_inc(S["d_R1"], 1)

            sq1(0)
            sd1(0)
            for c in range(4):
                dense(0, c, xs=True)
            with act.Fori(1, XS_TURNS) as j:
                for c in range(4):
                    dense(j, c, xs=True)
            for c in range(4):
                dense(XS_TURNS, c, xs=(c == 0))
            with act.Fori(XS_TURNS + 1, DT) as j:
                for c in range(4):
                    dense(j, c)
            for c in range(8):
                dense(DT, c)
            for b in range(2):
                act.wait_ge(d_st[1][b], BLOCKS // 2 * 16)

            def sources(k, b, j):
                act.wait_ge(g_ld[b], (j + 1) * 16 * C)
                if not (isinstance(k, int) and k < 1):
                    act.wait_ge(S["g_trx"], k)
                fn(XC, G[:, b, :, 0:D], ACT.Copy).then_inc(S["g_xc"], 1)

            def evac(k, b, i):
                act.wait_ge(S[("g_trd", "g_tre", "g_trx")[i]], k + 1)
                if not (isinstance(k, int) and k < 2):
                    act.wait_ge(S["g_lg"], k - 1)
                fn(TS[(1, 2, 0)[i]][:, b % 2].rearrange("p q m -> p (q m)"), TRP[(3 * b + i) % 2], ACT.Copy).then_inc(S["g_ev"], 1)

            def deviation(k):
                act.wait_ge(S["g_v"], k + 1)
                fn(est[:, 3, :], est[:, 2, :], ACT.Sqrt, bias=eps_c[:, :], scale=1.0 / D).then_inc(S["g_sd"], 1)

            def gat(k, b, j, last=False):
                b2, half = b % 2, j * 2 + b // 2
                b_next = (b + 1) % R4
                act.wait_ge(S["g_de"], k + 1)
                fn(RX[:, :, :], DE[:, :, :], ACT.Exp).then_inc(S["g_ex"], 1)
                if not last:
                    evac(k + 1, b_next, 2)
                act.wait_ge(S["g_ex"], k + 1)
                fn(AB[:, 0:D, 1:C1].rearrange("p (h d) t -> p h d t", d=HD),
                   RX[:, 0:H, :].unsqueeze(2).to_broadcast([P, H, HD, C]), ACT.Copy).then_inc(S["g_ab"], 1)
                fn(AB[:, D:SW, 1:C1], RX[:, 0:H, :], ACT.Copy).then_inc(S["g_ab"], 1)
                fn(B[:, D:SW, 1:C1], RX[:, H:2 * H, :], ACT.Copy).then_inc(S["g_ab"], 1)
                if not (isinstance(k, int) and k >= CH - 2):
                    for i in range(2):
                        evac(k + 2, (b + 2) % R4, i)
                if not (isinstance(k, int) and k == 0):
                    deviation(k - 1)
                act.wait_ge(S["g_S"], k + 1)
                act.wait_ge(g_out[0][b2], half * 16)
                fn(NR[:, b2, :, D:SW], SS[:, b2, D:SW, 1:C1].rearrange("p h t -> p t h"), ACT.Copy).then_inc(S["g_nr"], 1)
                fn(NR[:, b2, :, SW:GW], M[:, b2, :, 1:C1].rearrange("p h t -> p t h"), ACT.Copy).then_inc(S["g_nr"], 1)
                if not (isinstance(k, int) and k >= CH - 2):
                    sources(k + 2, (b + 2) % R4, j + (1 if b >= 2 else 0))
                act.wait_ge(S["g_c"], k + 1)
                fn(Q[:, :, :], UU[:, b2], ACT.Square).then_inc(S["g_q"], 1)

            evac(0, 0, 0)
            evac(0, 0, 1)
            sources(0, 0, 0)
            evac(0, 0, 2)
            evac(1, 1, 0)
            evac(1, 1, 1)
            sources(1, 1, 0)
            for b in range(R4):
                gat(b, b, 0)
            with act.Fori(1, NB4 - 1) as j:
                for b in range(R4):
                    gat(j * R4 + b, b, j)
            for k in range(CH - R4, CH):
                gat(k, k % R4, k // R4, last=(k == CH - 1))
            deviation(CH - 1)

            def seam_exp(n, *tiles):
                act.wait_ge(S["s_ex_in"], n)
                for t in tiles:
                    fn(t, t, ACT.Exp).then_inc(S["s_ex"], 1)

            def seam_norm(n):
                act.wait_ge(S["s_c"], n)
                fn(sq[:, :], su[:, :], ACT.Square).then_inc(S["s_q"], 1)
                act.wait_ge(S["s_v"], n)
                fn(sst[:, 3:4], sst[:, 2:3], ACT.Sqrt, bias=eps_c[:, :], scale=1.0 / D).then_inc(S["s_sd"], 1)

            seam_exp(1, rE[:, :], bE[:, :])
            seam_exp(2, wS[:, :], wC[:, :])
            seam_norm(1)

            for l in range(3):
                def flags(k, b):
                    at = CH * l + k
                    if not (isinstance(k, int) and at < 2):
                        act.wait_ge(S["l_scan"], at - 1)
                    nc.scalar.sem_inc(S["turn"], 1)
                    fn(AS[:, b, :, 1:C1], same[:, bass.ds(k * C, C)].unsqueeze(1).to_broadcast([P, D, C]),
                       ACT.Copy).then_inc(S["l_as"], 1)

                def gcn(k, b, norm, more=True):
                    at = CH * l + k
                    act.wait_ge(S["l_tr"], at + 1)
                    if not (isinstance(k, int) and at < 2):
                        act.wait_ge(S["l_z"], at - 1)
                    fn(TS[b][:, 0].rearrange("p q m -> p (q m)"), TRP[b], ACT.Copy).then_inc(S["l_ev"], 1)
                    if more:
                        flags(k + 2, b)
                    if norm:
                        norm_of(k - 1)

                def norm_of(k):
                    act.wait_ge(S["l_c"], k + 1)
                    fn(Q[:, :, :], U[:, :, :], ACT.Square).then_inc(S["l_q"], 1)
                    act.wait_ge(S["l_v"], k + 1)
                    fn(est[:, 3, :], est[:, 2, :], ACT.Sqrt, bias=eps_c[:, :], scale=1.0 / D).then_inc(S["l_sd"], 1)

                flags(0, 0)
                flags(1, 1)
                for k in range(R4):
                    gcn(k, k % 2, l == 2 and k > 0)
                with act.Fori(1, NB4 - 1) as j:
                    for b in range(R4):
                        gcn(j * R4 + b, b % 2, l == 2)
                for k in range(CH - R4, CH):
                    gcn(k, k % 2, l == 2, more=k + 2 < CH)
                if l == 2:
                    norm_of(CH - 1)
            seam_norm(2)

        @block.vector
        def _(dve):
            v = nc.vector
            tt, ts, stt = v.tensor_tensor, v.tensor_scalar, v.scalar_tensor_tensor
            step = Steps(S["vector_step"])

            def do(instruction):
                step.on(dve, instruction)

            for tile, value in ((ident, 0.0), (src_i, 0), (ew, 0.0), (padneg, 0.0), (negs, -BIG), (prev_i, -1), (next_i, -1),
                                (WM, 0.0), (W0b, 0.0), (W1b, 0.0), (W2b, 0.0), (eps_c, EPS), (LS, 0.0)):
                v.memset(tile[:, :], value)
            v.memset(WA[:, :, :], 0.0)
            v.memset(XM[:, :, :, D:XW], 0.0)
            v.memset(AM[:, :, 0:1], -BIG)
            v.memset(AB[:, :, 0:1], 0.0)
            for tile in (dst_i, shiftf, map_i, out_i, row_i):
                v.memset(tile[:, T:TX], 0)
            v.memset(M[:, 1], -BIG)
            v.memset(SS[:, 1], 0.0)
            v.memset(mC[:, 0:1], -BIG)
            v.memset(rE[:, 0:1], -BIG)
            v.memset(sC[:, 0:1], 0.0).then_inc(S["zeroed"], 1)
            dve.wait_ge(S["zeroed"], 1)

            dve.wait_ge(S["loaded_dst"], DLOADS * 16)
            dve.wait_ge(S["loaded_idx"], 4 * 16)
            dve.wait_ge(S["ends_loaded"], 32)
            dve.wait_ge(S["consts_set"], 2)
            dve.wait_ge(S["filled"], 16)
            v.tensor_copy(dstf[:, :], dst_i[:, 0:T])
            v.tensor_copy(srcf[:, :], src_i[:, 0:T])
            v.tensor_copy(slotf[:, :], slot_i[:, :])
            v.tensor_copy(c_prev, prev_i[:, :])
            v.memset(same[:, 0:1], 0.0)
            do(v.tensor_copy(c_next, next_i[:, :]))
            tt(same[:, 1:T], dstf[:, 1:T], dstf[:, 0:T - 1], ALU.is_equal)
            tt(isend[:, 0:T - 1], dstf[:, 1:T], dstf[:, 0:T - 1], ALU.not_equal)
            tt(isend[:, T - 1:T], dstf[:, T - 1:T], c_next, ALU.not_equal)
            ts(first[:, :], dstf[:, :], dstf[:, 0:1], None, ALU.is_equal)
            tt(c_cont, dstf[:, 0:1], c_prev, ALU.is_equal)
            do(tt(c_whole, dstf[:, 0:1], dstf[:, T - 1:T], ALU.is_equal))
            ts(breakf[:, :], same[:, :], BIG, -BIG, ALU.mult, ALU.add)
            tt(c_run, c_whole, c_cont, ALU.mult)
            v.tensor_reduce(c_t1, first[:, :], axis=AX.X, op=ALU.add)
            tt(shiftf[:, 0:T], slotf[:, :], dstf[:, :], ALU.subtract)
            do(ts(tmpT[:, :], isend[:, :], -SKIP, SKIP, ALU.mult, ALU.add))
            ts(shiftf[:, 0:T], shiftf[:, 0:T], float(SLOT0), None, ALU.add)
            tt(map_i[:, 0:T], tmpT[:, :], dstf[:, :], ALU.add)
            tt(c_slot, slotf[:, 0:1], c_t1, ALU.add)
            do(tt(onehot[:, :], isend[:, :], first[:, :], ALU.mult))
            tt(onehot[:, :], isend[:, :], onehot[:, :], ALU.subtract)
            do(ts(c_slot, c_slot, -1.0, None, ALU.add))
            do(ts(tmpT[:, :], onehot[:, :], -SKIP, SKIP, ALU.mult, ALU.add))
            tt(out_i[:, 0:T], tmpT[:, :], dstf[:, :], ALU.add)
            v.tensor_copy(i_slot, c_slot)
            ts(i_row, c_slot, float(SLOT0), None, ALU.add)
            do(ts(onehot[:, :], slotf[:, :], c_slot, None, ALU.is_equal))
            do(tt(tmpT[:, :], onehot[:, :], isend[:, :], ALU.mult))
            do(v.tensor_reduce(c_end, tmpT[:, :], axis=AX.X, op=ALU.add))
            do(ts(c_tmp, c_end, -SKIP, SKIP, ALU.mult, ALU.add))
            tt(i_out, c_tmp, dstf[:, 0:1], ALU.add).then_inc(S["flags_ready"], 1)

            wide = [P, SW]
            v.tensor_copy(bc[:, 0, :], c_run.to_broadcast(wide))
            v.tensor_copy(bc[:, 1, :], c_cont.to_broadcast(wide))
            ts(bc[:, 2, :], c_run.to_broadcast(wide), BIG, -BIG, ALU.mult, ALU.add)
            ts(bc[:, 3, :], c_cont.to_broadcast(wide), BIG, -BIG, ALU.mult, ALU.add).then_inc(S["rows_in"], 1)
            dve.wait_ge(S["rows_T"], 1)
            for i, r in enumerate((run_r, cont_r, nrun_r, ncont_r)):
                last = v.tensor_copy(r[:, :], SM[0:SW, i * P:(i + 1) * P])
            do(last)

            def carry_sums(n):
                dve.wait_ge(S["chain_T"], n + 1)
                do(v.tensor_tensor_scan(sE[:, :], run_r[:, :], SM[0:SW, 0:P], 0.0, ALU.mult, ALU.add))
                tt(sC[:, 1:P], sE[:, 0:P - 1], cont_r[:, 1:P], ALU.mult).then_inc(S["chain_back_in"], 1)
                dve.wait_ge(S["chain_back"], n + 1)

            do(v.tensor_tensor_scan(deg[:, :], same[:, :], ew[:, :], 0.0, ALU.mult, ALU.add))
            v.tensor_copy(LS[:, :], deg[:, T - 1:T].to_broadcast(wide)).then_inc(S["chain_in"], 1)
            carry_sums(0)
            do(v.tensor_copy(c_tmp, SM[:, 2 * P:2 * P + 1]))
            do(stt(out=deg[:, :], in0=first[:, :], scalar=c_tmp, in1=deg[:, :], op0=ALU.mult, op1=ALU.add))
            do(ts(deg[:, :], deg[:, :], 1.0, None, ALU.add))
            ts(tmpT[:, :], deg[:, :], 1e-30, None, ALU.max).then_inc(S["deg_in"], 1)
            do(ts(deg[:, :], deg[:, :], 0.0, None, ALU.is_gt))
            dve.wait_ge(S["deg_sqrt"], 1)
            do(v.reciprocal(dis[:, :], dis[:, :]))
            do(tt(dis[:, :], dis[:, :], deg[:, :], ALU.mult))
            do(tt(tmpT[:, :], onehot[:, :], dis[:, :], ALU.mult))
            v.tensor_reduce(c_dis, tmpT[:, :], axis=AX.X, op=ALU.add).then_inc(S["seam_set"], 1)
            dve.wait_ge(S["seam_set"], 1)

            dve.wait_ge(S["loaded_w"], WLOADS * 16)
            for i, w in enumerate((Wn2, Wn2, We2)):
                last = tt(wprod[:, i, :], w[:, :], att_bc[:, i, :], ALU.mult)
            do(last)
            do(v.tensor_reduce(wred[:, :, :], wprod[:, :, :].rearrange("p i (h d) -> p i h d", d=HD), axis=AX.X, op=ALU.add))
            for s_ in range(2):
                half_ = slice(64 * s_, 64 * s_ + 64)
                v.tensor_copy(WA[half_, :, H * s_:H * s_ + H], wred[half_, :, :])
                last = v.tensor_copy(WM[half_, 2 * D + H * s_:2 * D + H * s_ + H], wred[half_, 0, :])
            last.then_inc(S["weights_ready"], 1)

            def center(u, st, i_sum, i_mean, r, np_):
                do(v.tensor_reduce(st[0:np_, i_sum, 0:r], u, axis=AX.X, op=ALU.add))
                do(ts(st[0:np_, i_mean, 0:r], st[0:np_, i_sum, 0:r], -1.0 / D, None, ALU.mult))
                return tt(u, u, repeat(st[0:np_, i_mean, 0:r], D), ALU.add)

            def since(sem_, value):
                if not (isinstance(value, int) and value <= 0):
                    dve.wait_ge(sem_, value)

            def shape(m):
                return (TP, TR) if isinstance(m, int) and m == BLOCKS - 1 else (P, BR)

            def norms(j, c):
                s_ = j * 4 + c
                known = isinstance(s_, int)
                ln1 = not known or s_ + 1 < BLOCKS
                ln2 = not known or s_ >= 2
                m1, h1, b1_ = s_ + 1, j * 2 + (c + 1) // 2, (c + 1) % 2
                m2, h2, b2_ = s_ - 2, j * 2 + (c - 2) // 2, c % 2
                (n1, r1), (n2, r2) = shape(m1), shape(m2)
                if ln2:
                    dve.wait_ge(S["d_o"], m2 + 1)
                    since(S["d_O"], m2)
                    u = dU[0:n2, 0:r2]
                    tt(u, pO[0:n2, 0:r2 * D].rearrange("p (t f) -> p t f", f=D), dX1[0:n2, (c + 2) % 4, 0:r2],
                       ALU.add).then_inc(S["d_u2"], 1)
                if ln1:
                    dve.wait_ge(d_xl[b1_], h1 * 16 + 16)
                    since(S["d_x1"], m1)
                    c_ = dC[0:n1, 0:r1]
                    stt(out=c_, in0=dX[0:n1, b1_, 0:r1], scalar=2.0, in1=over_rows(bias_bc[0:n1, :], r1, n1), op0=ALU.mult,
                        op1=ALU.add).then_inc(S["d_xfree"], 1)
                both = ([(u, 2, 3, r2, n2, "d_u2", m2, "d_c2")] if ln2 else []) + (
                    [(c_, 0, 1, r1, n1, "d_xfree", m1, "d_c1")] if ln1 else [])
                marks = []
                for rows_, i_sum, i_mean, r, n, there, m, done in both:
                    dve.wait_ge(S[there], m + 1)
                    marks.append(step.mark(v.tensor_reduce(dst8[0:n, i_sum, 0:r], rows_, axis=AX.X, op=ALU.add)))
                for i, (rows_, i_sum, i_mean, r, n, there, m, done) in enumerate(both):
                    dve.wait_ge(S["vector_step"], marks[i])
                    marks[i] = step.mark(ts(dst8[0:n, i_mean, 0:r], dst8[0:n, i_sum, 0:r], -1.0 / D, None, ALU.mult))
                for i, (rows_, i_sum, i_mean, r, n, there, m, done) in enumerate(both):
                    dve.wait_ge(S["vector_step"], marks[i])
                    tt(rows_, rows_, repeat(dst8[0:n, i_mean, 0:r], D), ALU.add).then_inc(S[done], 1)
                if ln2:
                    dve.wait_ge(S["d_sq2"], m2 + 1)
                    v.tensor_reduce(dst8[0:n2, 7, 0:r2], dQ2[0:n2, 0:r2], axis=AX.X, op=ALU.add).then_inc(S["d_v2"], 1)
                if ln1:
                    dve.wait_ge(S["d_sq1"], m1 + 1)
                    v.tensor_reduce(dst8[0:n1, 5, 0:r1], dQ1[0:n1, 0:r1], axis=AX.X, op=ALU.add).then_inc(S["d_v1"], 1)
                if ln2:
                    dve.wait_ge(S["d_sd2"], m2 + 1)
                    do(v.reciprocal(dst8[0:n2, 6, 0:r2], dst8[0:n2, 6, 0:r2]))
                    since(d_st[3][b2_], h2 * 16)
                    tt(dO[0:n2, b2_, 0:r2], u, repeat(dst8[0:n2, 6, 0:r2], D), ALU.mult).then_inc(S["d_O"], 1)
                if ln1:
                    dve.wait_ge(S["d_sd1"], m1 + 1)
                    do(v.reciprocal(dst8[0:n1, 4, 0:r1], dst8[0:n1, 4, 0:r1]))
                    since(d_st[0][b1_], h1 * 16)
                    since(S["d_trx"], m1 - 3)
                    tt(dX1[0:n1, (c + 1) % 4, 0:r1], c_, repeat(dst8[0:n1, 4, 0:r1], D), ALU.mult).then_inc(S["d_x1"], 1)

            norms(0, -1)
            for c in range(4):
                norms(0, c)
            with dve.Fori(1, DT) as j:
                step.enter(j - 1, 24)
                for c in range(4):
                    norms(j, c)
                step.leave(DT - 1)
            for c in range(8):
                norms(DT, c)
            for j_ in range(4):
                for b in range(2):
                    dve.wait_ge(d_st[j_][b], BLOCKS // 2 * 16)
            do(v.memset(AS[:, :, :, 0:1], 0.0))

            def norm_rows(k, c_sem, q_sem, v_sem, sd_sem):
                center(U[:, :, :], est, 0, 1, C, P).then_inc(S[c_sem], 1)
                dve.wait_ge(S[q_sem], k + 1)
                v.tensor_reduce(est[:, 2, :], Q[:, :, :], axis=AX.X, op=ALU.add).then_inc(S[v_sem], 1)
                dve.wait_ge(S[sd_sem], k + 1)
                do(v.reciprocal(est[:, 3, :], est[:, 3, :]))

            def variance(k):
                dve.wait_ge(S["g_q"], k + 1)
                v.tensor_reduce(est[:, 2, :], Q[:, :, :], axis=AX.X, op=ALU.add).then_inc(S["g_v"], 1)

            def normed(k, b2, half):
                dve.wait_ge(S["g_sd"], k + 1)
                do(v.reciprocal(est[:, 3, :], est[:, 3, :]))
                since(g_out[1][b2], half * 16)
                tt(X1[:, b2], UU[:, b2], repeat(est[:, 3, :], D), ALU.mult).then_inc(S["g_x1"], 1)
                dve.wait_ge(S["g_x1"], k + 1)
                since(g_out[2][b2], half * 16)
                tt(Y0[:, b2], X1[:, b2], repeat(dis[:, bass.ds(k * C, C)], D), ALU.mult).then_inc(S["g_y0"], 1)

            def gat(k, b, j):
                b2, half, cs = b % 2, j * 2 + b // 2, bass.ds(k * C, C)
                before = not (isinstance(k, int) and k == 0)
                dve.wait_ge(g_ld[b], (j + 1) * 16 * C)
                tt(row_i[:, cs], srcf[:, cs], G[:, b, :, D], ALU.add).then_inc(S["g_shift"], 1)
                v.tensor_copy(AM[:, :, 1:C1], breakf[:, cs].unsqueeze(1).to_broadcast([P, H, C]))
                v.tensor_copy(LB[:, :, 0], M[:, 1 - b2, :, C])
                if not (isinstance(k, int) and k < 2):
                    dve.wait_ge(S["g_x1"], k - 1)
                dve.wait_ge(g_in[b2], half * 48 + 48)
                stt(out=UU[:, b2], in0=XD4[:, b], scalar=2.0, in1=over_rows(bias_bc[:, :], C), op0=ALU.mult,
                    op1=ALU.add).then_inc(S["g_xdfree"], 1)
                dve.wait_ge(S["g_lg"], k + 1)
                for q0, q1 in ((0, 3), (3, 6), (6, 7)):
                    last = tt(Z[:, 2 * q0:2 * q1, :].rearrange("p (q s) h -> p q s h", s=2),
                              hl(q0, q1)[:, :, 2 * D:PC].rearrange("p q (s h) -> p q s h", h=H),
                              repeat(padneg[:, bass.ds(k * C + 2 * q0, 2 * (q1 - q0))].rearrange("p (q s) -> p q s", s=2), H), ALU.add)
                last.then_inc(S["g_z"], 1)
                dve.wait_ge(S["g_z"], k + 1)
                do(stt(out=LB[:, :, 1:C1].rearrange("p h t -> p t h"), in0=Z[:, :, :], scalar=0.01, in1=Z[:, :, :],
                       op0=ALU.mult, op1=ALU.max))
                do(v.tensor_tensor_scan(M[:, b2].rearrange("p h t -> p (h t)"), AM[:, :, :].rearrange("p h t -> p (h t)"),
                                        LB[:, :, :].rearrange("p h t -> p (h t)"), 0.0, ALU.add, ALU.max))
                tt(DE[:, H:2 * H, :], LB[:, :, 1:C1], M[:, b2, :, 1:C1], ALU.subtract)
                do(tt(DE[:, 0:H, :], M[:, b2, :, 0:C], M[:, b2, :, 1:C1], ALU.subtract))
                tt(DE[:, 0:H, :], DE[:, 0:H, :], AM[:, :, 1:C1], ALU.add).then_inc(S["g_de"], 1)
                v.tensor_copy(B[:, :, 0], SS[:, 1 - b2, :, C])
                if before:
                    variance(k - 1)
                dve.wait_ge(S["g_ex"], k + 1)
                for q0, q1 in ((0, 3), (3, 6), (6, 7)):
                    t0, t1 = 2 * q0, 2 * q1
                    for s_ in range(2):
                        last = tt(B[:, 0:D, 1 + t0 + s_:1 + t1:2].rearrange("p (h d) q -> p q h d", d=HD),
                                  hl(q0, q1)[:, :, D * s_:D * s_ + D].rearrange("p q (h d) -> p q h d", d=HD),
                                  RX[:, H:2 * H, t0 + s_:t1:2].rearrange("p h q -> p q h").unsqueeze(3).to_broadcast([P, q1 - q0, H, HD]),
                                  ALU.mult)
                last.then_inc(S["g_hsfree"], 1)
                dve.wait_ge(S["g_hsfree"], k + 1)
                dve.wait_ge(S["g_ab"], k * 3 + 3)
                v.tensor_tensor_scan(SS[:, b2].rearrange("p f t -> p (f t)"), AB[:, :, :].rearrange("p f t -> p (f t)"),
                                     B[:, :, :].rearrange("p f t -> p (f t)"), 0.0, ALU.mult, ALU.add).then_inc(S["g_S"], 1)
                dve.wait_ge(S["g_S"], k + 1)
                do(v.reciprocal(RD[:, :, :], SS[:, b2, D:SW, 1:C1]))
                since(g_out[0][b2], half * 16)
                tt(NR[:, b2, :, 0:D].rearrange("p t (h d) -> p h d t", d=HD),
                   SS[:, b2, 0:D, 1:C1].rearrange("p (h d) t -> p h d t", d=HD),
                   RD[:, :, :].unsqueeze(2).to_broadcast([P, H, HD, C]), ALU.mult).then_inc(S["g_nrm"], 1)
                dve.wait_ge(S["g_xdfree"], k + 1)
                dve.wait_ge(S["g_nrm"], k + 1)
                do(tt(UU[:, b2], UU[:, b2], NR[:, b2, :, 0:D], ALU.add))
                center(UU[:, b2], est, 0, 1, C, P).then_inc(S["g_c"], 1)
                if before:
                    normed(k - 1, 1 - b2, j * 2 + (b - 1) // 2)

            def gat_four(j):
                for b in range(R4):
                    gat(j * R4 + b, b, j)

            turns(dve, NB4, gat_four, step, 8 * R4)
            variance(CH - 1)
            normed(CH - 1, 1, CH // 2 - 1)

            def heads(ap4, n=HD):
                return ap4.unsqueeze(2).to_broadcast([P, H, n])

            def by_head(ap64):
                return ap64.rearrange("p (h d) -> p h d", d=HD)

            def seam_norm(n):
                do(v.tensor_reduce(sst[:, 0:1], su[:, :], axis=AX.X, op=ALU.add))
                do(ts(sst[:, 1:2], sst[:, 0:1], -1.0 / D, None, ALU.mult))
                ts(su[:, :], su[:, :], sst[:, 1:2], None, ALU.add).then_inc(S["s_c"], 1)
                dve.wait_ge(S["s_q"], n)
                v.tensor_reduce(sst[:, 2:3], sq[:, :], axis=AX.X, op=ALU.add).then_inc(S["s_v"], 1)
                dve.wait_ge(S["s_sd"], n)
                do(v.reciprocal(sst[:, 3:4], sst[:, 3:4]))

            v.tensor_copy(LS[:, :], SS[:, 1, :, C])
            v.tensor_copy(by_head(LM[:, 0:D]), heads(M[:, 1, :, C]))
            v.tensor_copy(LM[:, D:SW], M[:, 1, :, C]).then_inc(S["chain_in"], 1)
            dve.wait_ge(S["chain_T"], 2)
            do(v.tensor_tensor_scan(mE[:, :], nrun_r[:, :], SM[0:SW, P:2 * P], -BIG, ALU.add, ALU.max))
            tt(bE[:, :], SM[0:SW, P:2 * P], mE[:, :], ALU.subtract)
            tt(mC[:, 1:P], mE[:, 0:P - 1], ncont_r[:, 1:P], ALU.add)
            do(tt(rE[:, 1:P], mE[:, 0:P - 1], mE[:, 1:P], ALU.subtract))
            tt(rE[:, 1:P], rE[:, 1:P], nrun_r[:, 1:P], ALU.add).then_inc(S["s_ex_in"], 1)
            dve.wait_ge(S["s_ex"], 2)
            do(tt(bE[:, :], SM[0:SW, 0:P], bE[:, :], ALU.mult))
            do(v.tensor_tensor_scan(sE[:, :], rE[:, :], bE[:, :], 0.0, ALU.mult, ALU.add))
            tt(sC[:, 1:P], sE[:, 0:P - 1], cont_r[:, 1:P], ALU.mult).then_inc(S["chain_back_in"], 1)
            dve.wait_ge(S["s_row"], 32)
            tt(by_head(S68[:, 0:D]), by_head(grow[:, 0:D]), heads(grow[:, D:SW]), ALU.mult)
            v.tensor_copy(S68[:, D:SW], grow[:, D:SW])
            v.tensor_copy(by_head(M68[:, 0:D]), heads(grow[:, SW:GW]))
            do(v.tensor_copy(M68[:, D:SW], grow[:, SW:GW]))
            dve.wait_ge(S["chain_back"], 2)
            carS, carM = SM[:, 2 * P:2 * P + SW], SM[:, 2 * P + SW:2 * P + 2 * SW]
            do(tt(MM[:, :], M68[:, :], carM, ALU.max))
            tt(wS[:, :], M68[:, :], MM[:, :], ALU.subtract)
            tt(wC[:, :], carM, MM[:, :], ALU.subtract).then_inc(S["s_ex_in"], 1)
            dve.wait_ge(S["s_ex"], 4)
            tt(S68[:, :], S68[:, :], wS[:, :], ALU.mult)
            do(tt(wC[:, :], carS, wC[:, :], ALU.mult))
            do(tt(S68[:, :], S68[:, :], wC[:, :], ALU.add))
            do(v.reciprocal(sden[:, :], S68[:, D:SW]))
            do(tt(by_head(su[:, :]), by_head(S68[:, 0:D]), heads(sden[:, :]), ALU.mult))
            do(stt(out=su[:, :], in0=xrow[:, :], scalar=2.0, in1=su[:, :], op0=ALU.mult, op1=ALU.add))
            do(tt(su[:, :], su[:, :], bias_bc[:, :], ALU.add))
            seam_norm(1)
            do(ts(x1row[:, :], su[:, :], sst[:, 3:4], None, ALU.mult))
            ts(yrow[:, :], x1row[:, :], c_dis, None, ALU.mult).then_inc(S["s_out"], 1)

            for l in range(3):
                def sums(k, b, j):
                    b2, half, cs, at = b % 2, j * 2 + b // 2, bass.ds(k * C, C), CH * l + k
                    dve.wait_ge(l_ld[b], (j + (1 + l * NB4)) * 16 * C)
                    v.tensor_copy(B[:, 0:D, 0], SS[:, 1 - b2, 0:D, C])
                    tt(B[:, 0:D, 1:C1].rearrange("p f t -> p t f"), GX[:, b], repeat(ew[:, cs], D), ALU.mult).then_inc(S["l_gfree"], 1)
                    dve.wait_ge(S["l_gfree"], at + 1)
                    dve.wait_ge(S["l_as"], at + 1)
                    v.tensor_tensor_scan(SS[:, b2, 0:D].rearrange("p f t -> p (f t)"), AS[:, b2].rearrange("p f t -> p (f t)"),
                                         B[:, 0:D].rearrange("p f t -> p (f t)"), 0.0, ALU.mult, ALU.add).then_inc(S["l_scan"], 1)
                    dve.wait_ge(S["l_scan"], at + 1)
                    dve.wait_ge(l_in[b2], l * HALF + (half + 1) * (32 if l == 2 else 16))
                    dve.wait_ge(l_out[0][b2], l * HALF + half * 16)
                    if not (isinstance(k, int) and at < 2):
                        dve.wait_ge(S["l_tr"], at - 1)
                    tt(PR[:, b2], SS[:, b2, 0:D, 1:C1].rearrange("p f t -> p t f"), XD[:, b2], ALU.add).then_inc(S["l_pre"], 1)

                def rows_of(k, b, j):
                    b2, half, cs, at = b % 2, j * 2 + b // 2, bass.ds(k * C, C), CH * l + k
                    if not (isinstance(k, int) and k == 0):
                        dve.wait_ge(S["l_y"] if l < 2 else S["l_o"], at if l < 2 else k)
                    dve.wait_ge(S["l_z"], at + 1)
                    tt(U[:, :, :], HS, repeat(dis[:, cs], D), ALU.mult).then_inc(S["l_zfree"], 1)
                    dve.wait_ge(S["l_zfree"], at + 1)
                    do(tt(U[:, :, :], U[:, :, :], over_rows(b_bc[l][:, :], C), ALU.add))
                    if l < 2:
                        dve.wait_ge(l_out[1][b2], l * HALF + half * 16)
                        stt(out=Y0[:, b2], in0=U[:, :, :], scalar=0.0, in1=repeat(dis[:, cs], D), op0=ALU.max,
                            op1=ALU.mult).then_inc(S["l_y"], 1)
                    else:
                        stt(out=U[:, :, :], in0=U[:, :, :], scalar=0.0, in1=EA[:, b2], op0=ALU.max,
                            op1=ALU.add).then_inc(S["l_u"], 1)
                        dve.wait_ge(S["l_u"], k + 1)
                        norm_rows(k, "l_c", "l_q", "l_v", "l_sd")
                        dve.wait_ge(o_st[b], j * 16 * C)
                        tt(OB[:, b], U[:, :, :], repeat(est[:, 3, :], D), ALU.mult).then_inc(S["l_o"], 1)

                each = 1 if l < 2 else 4
                sums(0, 0, 0)

                def gcn_four(j):
                    for b in range(R4):
                        sums(j * R4 + (b + 1), (b + 1) % R4, j + (1 if b == R4 - 1 else 0))
                        rows_of(j * R4 + b, b, j)

                turns(dve, NB4 - 1, gcn_four, step, each * R4)
                for k in range(CH - R4, CH):
                    if k + 1 < CH:
                        sums(k + 1, (k + 1) % R4, (k + 1) // R4)
                    rows_of(k, k % R4, k // R4)

                v.tensor_copy(LS[:, 0:D], SS[:, 1, 0:D, C]).then_inc(S["chain_in"], 1)
                carry_sums(2 + l)
                dve.wait_ge(S["s_row"], 48 + 16 * l)
                tt(su[:, :], prow[:, :], SM[:, 2 * P:2 * P + D], ALU.add).then_inc(S["s_mid"], 1)
                dve.wait_ge(S["s_midT"], l + 1)
                v.tensor_copy(prT[:, :], SM[0:D, 0:P]).then_inc(S["s_prT"], 1)
                dve.wait_ge(S["s_mm"], l + 1)
                do(ts(su[:, :], SM[:, 384:384 + D], c_dis, None, ALU.mult))
                do(tt(su[:, :], su[:, :], b_bc[l][:, :], ALU.add))
                dve.wait_ge(S["s_stored"], 32 + 16 * l)
                if l < 2:
                    ts(yrow[:, :], su[:, :], 0.0, c_dis, ALU.max, ALU.mult).then_inc(S["s_out"], 1)
                else:
                    do(stt(out=su[:, :], in0=su[:, :], scalar=0.0, in1=x1row[:, :], op0=ALU.max, op1=ALU.add))
                    seam_norm(2)
                    ts(yrow[:, :], su[:, :], sst[:, 3:4], None, ALU.mult).then_inc(S["s_out"], 1)


_INS = ["x", "src", "dst", "edge_attr_64", "edge_weight", "L0_gnn_W_node", "L0_gnn_W_edge", "L0_gnn_attn_query",
        "L0_gnn_attn_key", "L0_gnn_attn_edge", "L0_gnn_bias", "L1_gnn_W0", "L1_gnn_b0", "L1_gnn_W1", "L1_gnn_b1",
        "L1_gnn_W2", "L1_gnn_b2"]


def kernel(**inputs):
    import numpy as np
    import concourse.bacc as bacc
    from concourse import mybir
    from concourse.bass_utils import run_bass_kernel_spmd

    nc = bacc.Bacc("TRN2", target_bir_lowering=False, num_devices=1)
    arrays, ap = {}, {}
    for name in _INS:
        a = np.ascontiguousarray(inputs[name])
        arrays[f"in_{name}"] = a
        ap[name] = nc.dram_tensor(f"in_{name}", a.shape, mybir.dt.from_np(a.dtype), kind="ExternalInput").ap()
    out = nc.dram_tensor("out_rows", [N, D], F32, kind="ExternalOutput").ap()
    build(nc, ap["x"], ap["src"], ap["dst"], ap["edge_attr_64"], ap["edge_weight"], ap["L0_gnn_W_node"], ap["L0_gnn_W_edge"],
          ap["L0_gnn_attn_query"], ap["L0_gnn_attn_key"], ap["L0_gnn_attn_edge"], ap["L0_gnn_bias"],
          ap["L1_gnn_W0"], ap["L1_gnn_b0"], ap["L1_gnn_W1"], ap["L1_gnn_b1"], ap["L1_gnn_W2"], ap["L1_gnn_b2"], out)
    r = run_bass_kernel_spmd(nc, [arrays], core_ids=[0])
    return r.results[0]["out_rows"]
```
